# Optimizing a Trainium2 kernel written in Bass

```python
import numpy as np
import jax
import jax.numpy as jnp

def _softmax(x, axis=-1):
    return jax.nn.softmax(x, axis=axis)
def _gelu(x):
    return jax.nn.gelu(x, approximate=True)
def _silu(x):
    return jax.nn.silu(x)
def _sigmoid(x):
    return jax.nn.sigmoid(x)
def _layernorm(x, axis=-1, eps=1e-5):
    m = jnp.mean(x, axis=axis, keepdims=True)
    v = jnp.var(x, axis=axis, keepdims=True)
    return (x - m) / jnp.sqrt(v + eps)
def _scatter_add(tgt, idx, src, axis=0):
    return tgt.at[idx].add(src)
def _segment_sum(src, seg, n):
    return jax.ops.segment_sum(src, seg, n)

kernel_name = 'mk_adj_resnorm_d4_adj_128_be7496'

def setup_inputs(seed: int = 0):
    np.random.seed(seed)
    _w = jnp.asarray
    def _rec_inputs():
        import jax
        import jax.numpy as jnp
        _gk = jax.random.key(seed)
        x = -0.0002928 + 1 * jax.random.normal(jax.random.fold_in(_gk, 1), (32, 512, 128), jnp.float32)
        _w = (1.0 + jnp.arange(512, dtype=jnp.float32)) ** -0.5
        _w = _w / _w.mean()
        _pij = jnp.clip(0.03125 * _w[:, None] * _w[None, :], 0.0, 1.0)
        _a = jax.random.uniform(jax.random.fold_in(_gk, 2), (512, 512)) < _pij
        _a = jnp.logical_or(_a, jnp.swapaxes(_a, -1, -2))
        _a = jnp.logical_or(_a, jnp.eye(512, dtype=bool))
        _af = _a.astype(jnp.float32)
        adj = _af
        return x, adj
    x, adj = _rec_inputs()
    def _L0_gnn_setup():
        import jax, jax.numpy as jnp
        import numpy as np
        B, N, D = (32, 1024, 128)
        LEAKY_ALPHA = 0.2
        LN_EPS = 1e-14
        key = jax.random.key(seed)
        k1, k2 = jax.random.split(key)
        x = jax.random.normal(k1, (B, N, D), dtype=jnp.float32)
        limit = 1.414 * np.sqrt(6.0 / (2 * D + 1))
        a = jax.random.uniform(k2, (2 * D, 1), dtype=jnp.float32, minval=-limit, maxval=limit)
        gamma = jnp.ones((N, N), dtype=jnp.float32)
        beta = jnp.zeros((N, N), dtype=jnp.float32)
        return {'x': x, 'a': a, 'gamma': gamma, 'beta': beta}
    _L0_gnn_all = _L0_gnn_setup()
    _L0_gnn_in = {k: v for k, v in _L0_gnn_all.items() if k in ('a', )}
    del _L0_gnn_all

    def _L1_gnn_setup():
        import jax, jax.numpy as jnp
        import numpy as np
        B, M, IN, HID, OUT = (8, 2048, 128, 128, 128)
        LN_EPS = 1e-05

        def _layernorm(x, g, b):
            mu = jnp.mean(x, axis=-1, keepdims=True)
            var = jnp.mean((x - mu) ** 2, axis=-1, keepdims=True)
            return (x - mu) * jax.lax.rsqrt(var + LN_EPS) * g + b
        key = jax.random.key(seed)
        ks = jax.random.split(key, 10)
        x = jax.random.normal(ks[0], (B, M, IN), dtype=jnp.float32)
        vals = jax.random.uniform(ks[1], (M, M), dtype=jnp.float32)
        keep = jax.random.uniform(ks[2], (M, M)) < 0.03
        A_final = jnp.where(keep, vals, 0.0) + jnp.eye(M, dtype=jnp.float32)
        s = 0.02
        return {'x': x, 'A_final': A_final, 'Wp': jax.random.normal(ks[3], (IN, HID), jnp.float32) * s, 'bp': jnp.zeros((HID,), jnp.float32), 'a_src': jax.random.normal(ks[4], (HID,), jnp.float32) * s, 'a_dst': jax.random.normal(ks[5], (HID,), jnp.float32) * s, 'gat_g': jnp.ones((HID,), jnp.float32), 'gat_b': jnp.zeros((HID,), jnp.float32), 'eps': jnp.zeros((1,), jnp.float32), 'W1': jax.random.normal(ks[6], (HID, HID), jnp.float32) * s, 'b1': jnp.zeros((HID,), jnp.float32), 'mlp_g': jnp.ones((HID,), jnp.float32), 'mlp_b': jnp.zeros((HID,), jnp.float32), 'W2': jax.random.normal(ks[7], (HID, OUT), jnp.float32) * s, 'b2': jnp.zeros((OUT,), jnp.float32)}
    _L1_gnn_all = _L1_gnn_setup()
    _L1_gnn_in = {k: v for k, v in _L1_gnn_all.items() if k in ('Wp', 'bp', 'a_src', 'a_dst', 'gat_g', 'gat_b', 'eps', 'W1', 'b1', 'mlp_g', 'mlp_b', 'W2', 'b2', )}
    del _L1_gnn_all

    def _L2_gnn_setup():
        import jax, jax.numpy as jnp
        import numpy as np
        NEG = -9000000000000000.0
        key = jax.random.key(seed)
        k1, k2, k3, k4 = jax.random.split(key, 4)
        B, N, F_in, F_out, MAX_E = (16384, 16, 128, 128, 256)
        inp = jax.random.normal(k1, (B, N, F_in), dtype=jnp.float32)
        adj = jax.random.uniform(k2, (N, N), dtype=jnp.float32)
        limit = 1.414 * np.sqrt(6.0 / (F_in + F_out))
        W = jax.random.uniform(k3, (2, F_in, F_out), dtype=jnp.float32, minval=-limit, maxval=limit)
        e = jnp.ones((1, MAX_E), dtype=jnp.float32)
        stdv = 1.0 / np.sqrt(F_out)
        bias = jax.random.uniform(k4, (F_out,), dtype=jnp.float32, minval=-stdv, maxval=stdv)
        return {'input': inp, 'adj': adj, 'W': W, 'e': e, 'bias': bias}
    _L2_gnn_all = _L2_gnn_setup()
    _L2_gnn_in = {k: v for k, v in _L2_gnn_all.items() if k in ('W', 'e', 'bias', )}
    del _L2_gnn_all

    def _L3_gnn_setup():
        import jax, jax.numpy as jnp
        import numpy as np
        _NEG_INF = -1000000000.0
        ALPHA = 0.2
        key = jax.random.key(seed)
        k0, k1, k2, k3, k4 = jax.random.split(key, 5)
        B, N, F_IN, F_OUT = (8, 2048, 128, 128)
        x = jax.random.normal(k0, (B, N, F_IN), dtype=jnp.float32)
        adj = (jax.random.uniform(k1, (N, N)) < 0.02).astype(jnp.float32)
        W = jax.random.normal(k2, (F_IN, F_OUT), dtype=jnp.float32) * (1.0 / np.sqrt(F_IN))
        bound = float(np.sqrt(6.0 / (F_OUT + 1)))
        a_src = jax.random.uniform(k3, (F_OUT, 1), minval=-bound, maxval=bound, dtype=jnp.float32)
        a_dst = jax.random.uniform(k4, (F_OUT, 1), minval=-bound, maxval=bound, dtype=jnp.float32)
        return {'x': x, 'adj': adj, 'W': W, 'a_src': a_src, 'a_dst': a_dst}
    _L3_gnn_all = _L3_gnn_setup()
    _L3_gnn_in = {k: v for k, v in _L3_gnn_all.items() if k in ('W', 'a_src', 'a_dst', )}
    del _L3_gnn_all

    return {
        "x": x,
        "adj": adj,
        "L0_gnn_a": _L0_gnn_in["a"],
        "L1_gnn_Wp": _L1_gnn_in["Wp"],
        "L1_gnn_bp": _L1_gnn_in["bp"],
        "L1_gnn_a_src": _L1_gnn_in["a_src"],
        "L1_gnn_a_dst": _L1_gnn_in["a_dst"],
        "L1_gnn_gat_g": _L1_gnn_in["gat_g"],
        "L1_gnn_gat_b": _L1_gnn_in["gat_b"],
        "L1_gnn_eps": _L1_gnn_in["eps"],
        "L1_gnn_W1": _L1_gnn_in["W1"],
        "L1_gnn_b1": _L1_gnn_in["b1"],
        "L1_gnn_mlp_g": _L1_gnn_in["mlp_g"],
        "L1_gnn_mlp_b": _L1_gnn_in["mlp_b"],
        "L1_gnn_W2": _L1_gnn_in["W2"],
        "L1_gnn_b2": _L1_gnn_in["b2"],
        "L2_gnn_W": _L2_gnn_in["W"],
        "L2_gnn_e": _L2_gnn_in["e"],
        "L2_gnn_bias": _L2_gnn_in["bias"],
        "L3_gnn_W": _L3_gnn_in["W"],
        "L3_gnn_a_src": _L3_gnn_in["a_src"],
        "L3_gnn_a_dst": _L3_gnn_in["a_dst"],
    }

def reference(x, adj, L0_gnn_a, L1_gnn_Wp, L1_gnn_bp, L1_gnn_a_src, L1_gnn_a_dst, L1_gnn_gat_g, L1_gnn_gat_b, L1_gnn_eps, L1_gnn_W1, L1_gnn_b1, L1_gnn_mlp_g, L1_gnn_mlp_b, L1_gnn_W2, L1_gnn_b2, L2_gnn_W, L2_gnn_e, L2_gnn_bias, L3_gnn_W, L3_gnn_a_src, L3_gnn_a_dst):
    import jax
    import jax.numpy as jnp
    def _L0_gnn_ref(x, a, gamma, beta):
        import jax, jax.numpy as jnp
        import numpy as np
        B, N, D = (32, 1024, 128)
        LEAKY_ALPHA = 0.2
        LN_EPS = 1e-14
        d = x.shape[-1]
        a_i = a[:d, 0]
        a_j = a[d:, 0]
        e = (x @ a_i)[:, :, None] + (x @ a_j)[:, None, :]
        mean = jnp.mean(e, axis=(1, 2), keepdims=True)
        var = jnp.mean(jnp.square(e - mean), axis=(1, 2), keepdims=True)
        e = (e - mean) * jax.lax.rsqrt(var + LN_EPS) * gamma + beta
        e = jnp.where(e >= 0, e, LEAKY_ALPHA * e)
        alpha = jax.nn.softmax(e, axis=1)
        h = jax.nn.sigmoid(jnp.einsum('bij,bjd->bid', alpha, x))
        return h

    def _L1_gnn_ref(x, A_final, Wp, bp, a_src, a_dst, gat_g, gat_b, eps, W1, b1, mlp_g, mlp_b, W2, b2):
        import jax, jax.numpy as jnp
        import numpy as np
        B, M, IN, HID, OUT = (8, 2048, 128, 128, 128)
        LN_EPS = 1e-05

        def _layernorm(x, g, b):
            mu = jnp.mean(x, axis=-1, keepdims=True)
            var = jnp.mean((x - mu) ** 2, axis=-1, keepdims=True)
            return (x - mu) * jax.lax.rsqrt(var + LN_EPS) * g + b
        h = jnp.einsum('bmi,ih->bmh', x, Wp) + bp
        s_src = jnp.einsum('bmh,h->bm', h, a_src)
        s_dst = jnp.einsum('bmh,h->bm', h, a_dst)
        scores = s_src[:, :, None] + s_dst[:, None, :]
        scores = jnp.where(scores >= 0, scores, 0.2 * scores)
        fill = jnp.finfo(scores.dtype).min
        scores = jnp.where((A_final <= 0)[None], fill, scores)
        attn = jax.nn.softmax(scores, axis=-1)
        weighted_adj = attn * A_final[None]
        h_gat = jnp.einsum('bmn,bnh->bmh', weighted_adj, h)
        h_gat = jax.nn.relu(_layernorm(h_gat, gat_g, gat_b))
        h_agg = jnp.einsum('mn,bnh->bmh', A_final, h_gat)
        h_gin = (1.0 + eps) * h_gat + h_agg
        z = jnp.einsum('bmh,hk->bmk', h_gin, W1) + b1
        z = jax.nn.relu(_layernorm(z, mlp_g, mlp_b))
        x_gin = jnp.einsum('bmk,ko->bmo', z, W2) + b2
        return jax.nn.relu(x_gin + h_gat)

    def _L2_gnn_ref(input, adj, W, e, bias):
        import jax, jax.numpy as jnp
        import numpy as np
        NEG = -9000000000000000.0
        h0 = jnp.einsum('bnf,fg->bng', input, W[0])
        h1 = jnp.einsum('bnf,fg->bng', input, W[1])
        m = adj > 0
        idx = jnp.cumsum(m.reshape(-1).astype(jnp.int32)) - 1
        vals = e[0][idx].reshape(adj.shape)
        A = jnp.where(m, vals, jnp.float32(NEG))
        A = jax.nn.softmax(A, axis=1)
        M = jnp.eye(adj.shape[0], dtype=A.dtype)
        out = jnp.einsum('ij,bjg->big', A * M, h0) + jnp.einsum('ij,bjg->big', A * (1.0 - M), h1)
        return out + bias[None, None, :]

    def _L3_gnn_ref(x, adj, W, a_src, a_dst):
        import jax, jax.numpy as jnp
        import numpy as np
        _NEG_INF = -1000000000.0
        ALPHA = 0.2
        h = jnp.einsum('bnf,fo->bno', x, W)
        N = h.shape[1]
        e_src = (h @ a_src)[..., 0]
        e_dst = (h @ a_dst)[..., 0]
        e = jax.nn.leaky_relu(e_src[:, :, None] + e_dst[:, None, :], negative_slope=ALPHA)
        adj_loops = jnp.clip(adj + jnp.eye(N, dtype=adj.dtype), 0.0, None)
        e = jnp.where(adj_loops[None, :, :] == 0, _NEG_INF, e)
        attn = jax.nn.softmax(e, axis=-1)
        attn = jnp.nan_to_num(attn, nan=0.0, posinf=0.0, neginf=0.0)
        h_prime = jnp.einsum('bij,bjo->bio', attn, h)
        return jax.nn.elu(h_prime)

    x = _layernorm(x + _L0_gnn_ref(x, L0_gnn_a, adj, adj), axis=-1)
    x = _layernorm(x + _L1_gnn_ref(x, adj, L1_gnn_Wp, L1_gnn_bp, L1_gnn_a_src, L1_gnn_a_dst, L1_gnn_gat_g, L1_gnn_gat_b, L1_gnn_eps, L1_gnn_W1, L1_gnn_b1, L1_gnn_mlp_g, L1_gnn_mlp_b, L1_gnn_W2, L1_gnn_b2), axis=-1)
    x = _layernorm(x + _L2_gnn_ref(x, adj, L2_gnn_W, L2_gnn_e, L2_gnn_bias), axis=-1)
    x = _layernorm(x + _L3_gnn_ref(x, adj, L3_gnn_W, L3_gnn_a_src, L3_gnn_a_dst), axis=-1)
    return x


_drawn_inputs = setup_inputs


def setup_inputs(seed=0):
    import zlib

    import numpy as np

    out = dict(_drawn_inputs(seed))
    spreads = {'L1_gnn_bp': (0.0, 0.1),
     'L1_gnn_gat_g': (1.0, 0.2),
     'L1_gnn_gat_b': (0.0, 0.1),
     'L1_gnn_b1': (0.0, 2.0),
     'L1_gnn_mlp_g': (1.0, 0.2),
     'L1_gnn_mlp_b': (0.0, 0.446),
     'L1_gnn_b2': (0.0, 0.1),
     'L2_gnn_e': (1.0, 0.6)}
    factors = {'L0_gnn_a': 200.0, 'L1_gnn_a_src': 71.831, 'L1_gnn_a_dst': 4.178}
    for name, (base, spread) in spreads.items():
        noise = np.random.default_rng([zlib.crc32(name.encode()), seed]).standard_normal(out[name].shape)
        drawn = base * np.exp(spread * noise) if base else spread * noise
        out[name] = jnp.asarray(drawn.astype(out[name].dtype))
    for name, factor in factors.items():
        out[name] = (out[name] * factor).astype(out[name].dtype)
    return out
```

```python
from contextlib import ExitStack

import concourse.bass as bass
from concourse import mybir

P = 128
ALU = mybir.AluOpType
ACT = mybir.ActivationFunctionType
AX_X = mybir.AxisListType.X
F32 = mybir.dt.float32
BF16 = mybir.dt.bfloat16
I32 = mybir.dt.int32

A, B, C, D, E = range(5)
STAGES = 5
BIG = 2.0 ** 100
SLOPE = 0.2
LN_EPS = 1e-5
PAIR_EPS = 1e-14
NEG = -9000000000000000.0


class Turn:

    def __init__(self, it, graphs):
        self.it, self.graphs = it, graphs

    def on(self, stage):
        return not isinstance(self.it, int) or 0 <= self.it - stage < self.graphs

    def count(self, n):
        return min(max(n, 0), self.graphs) if isinstance(n, int) else n

    def now(self, stage):
        return self.count(self.it - (stage - 1))

    def last(self, stage):
        return self.count(self.it - stage)

    def tile(self, stage, j, tiles=4):
        return self.count(self.it - stage) * tiles + (j + 1)


def resnorm_gnn(nc, x, adj, l0_a, wp, bp, a_src, a_dst, gat_g, gat_b, eps, w1, b1, mlp_g, mlp_b, w2, b2,
                l2_w, l2_e, l2_bias, l3_w, l3_src, l3_dst, out):
    GRAPHS, N, DIM = x.shape
    NT = N // P
    assert DIM == P and N == NT * P
    EDGES = l2_e.shape[1]
    EC = EDGES // P

    with ExitStack() as ctx:
        def sb(name, shape, dt=F32):
            return ctx.enter_context(nc.sbuf_tensor(name, shape, dt))

        def bank(name, n=1):
            return ctx.enter_context(nc.psum_tensor(name, [P, n, 512], F32))

        class Signals(dict):

            def __missing__(self, name):
                self[name] = nc.alloc_semaphore(name=name)
                return self[name]

        ident = sb("ident", [P, P])
        identb = sb("identb", [P, P], BF16)
        ones = sb("ones", [P, P])
        onesb = sb("onesb", [P, P], BF16)
        mhalf = sb("mhalf", [P, 2])
        adj_i = sb("adj_i", [P, NT, N])
        adj_j = sb("adj_j", [P, NT, N])
        gin_j = sb("gin_j", [P, NT, N])
        att2_j = sb("att2_j", [P, NT, N])
        diag2 = sb("diag2", [P, N])
        no1_i = sb("no1_i", [P, NT, N], BF16)
        no1_j = sb("no1_j", [P, NT, N], BF16)
        no3_i = sb("no3_i", [P, NT, N], BF16)
        no3_j = sb("no3_j", [P, NT, N], BF16)
        a01 = sb("a01", [P, 2])
        wp_sb = sb("wp_sb", [P, P])
        w1_sb = sb("w1_sb", [P, P])
        w2_sb = sb("w2_sb", [P, P])
        l2w0 = sb("l2w0", [P, P])
        l2w1 = sb("l2w1", [P, P])
        w3_sb = sb("w3_sb", [P, P])
        bp_row = sb("bp_row", [P, 1, P])
        gg_row = sb("gg_row", [P, 1, P])
        gb_row = sb("gb_row", [P, 1, P])
        b1_row = sb("b1_row", [P, 1, P])
        mg_row = sb("mg_row", [P, 1, P])
        mb_row = sb("mb_row", [P, 1, P])
        b2_row = sb("b2_row", [P, 1, P])
        l2b_row = sb("l2b_row", [P, 1, P])
        avec = sb("avec", [P, 5])
        eps_c = sb("eps_c", [P, 1])
        ws1 = sb("ws1", [P, P])
        wt1 = sb("wt1", [P, P])
        ws3 = sb("ws3", [P, P])
        wt3 = sb("wt3", [P, P])
        st1 = sb("st1", [P, 2])
        st3 = sb("st3", [P, 2])
        bst = sb("bst", [P, 1, 2])
        xA = sb("xA", [P, NT, P])
        xB = sb("xB", [P, NT, P])
        xBC = sb("xBC", [P, NT, P])
        hgat = sb("hgat", [P, NT, P])
        xD = sb("xD", [P, NT, P])
        xE = sb("xE", [P, NT, P])
        xout = sb("xout", [P, NT, P])
        xTA = sb("xTA", [P, N])
        xTB = sb("xTB", [P, N])
        xTD = sb("xTD", [P, N])
        xTE = sb("xTE", [P, N])
        xTdD = sb("xTdD", [P, N])
        ginT = sb("ginT", [P, N])
        zT = sb("zT", [P, N])
        stA = sb("stA", [P, NT, 2])
        cenA = sb("cenA", [P, NT, 2])
        sqA = sb("sqA", [P, NT, 2])
        meanA = sb("meanA", [P, 1, 2])
        varA = sb("varA", [P, 2])
        veA = sb("veA", [P, 1])
        rA = sb("rA", [P, 1])
        irA = sb("irA", [P, 1])
        rowsA = sb("rowsA", [P, 2 * N], BF16)
        spA = sb("spA", [P, 2, NT, P], BF16)
        r1A = sb("r1A", [P, NT, 2])
        r2A = sb("r2A", [P, NT, 2])
        vA = sb("vA", [P, NT, N])
        vmaxA = sb("vmaxA", [P, NT])
        lmA = sb("lmA", [P, NT])
        nmA = sb("nmA", [P, NT])
        pA = sb("pA", [P, NT, N])
        zsA = sb("zsA", [P, NT])
        rzA = sb("rzA", [P, NT])
        xsA = sb("xsA", [P, NT, P])
        xhA = sb("xhA", [P, NT, P])
        thA = sb("thA", [P, NT, P])
        att = {}
        for g in (B, E):
            n = "BE"[g == E]
            att[g] = dict(
                h=sb("h" + n, [P, NT, P + 2]), st=sb("st" + n, [P, NT, 2]), nt=sb("nt" + n, [P, NT]),
                srow=sb("srow" + n, [P, N]), mx=sb("mx" + n, [P, NT]),
                u=sb("u" + n, [P, NT]), m=sb("m" + n, [P, NT]), q=sb("q" + n, [P, NT]),
                c=sb("c" + n, [P, NT, 1]), r1=sb("r1" + n, [P, NT, 1]), r2=sb("r2" + n, [P, NT, 1]),
                sp=sb("sp" + n, [P, NT, P], BF16), crow=sb("crow" + n, [P, N], BF16),
                w=sb("w" + n, [P, NT, N]), rz=sb("rz" + n, [P, NT]),
            )
            att[g]["p"] = att[g]["w"]
        paB = sb("paB", [P, NT, N])
        psumB = sb("psumB", [P, 3, N])
        nB = sb("nB", [P, NT, P])
        ngB = sb("ngB", [P, NT, P])
        rrB = sb("rrB", [P, NT])
        tvB = sb("tvB", [P, NT])
        scB = sb("scB", [P, NT])
        znC = sb("znC", [P, NT, P])
        zgC = sb("zgC", [P, NT, P])
        hbC = sb("hbC", [P, NT, P])
        qC = sb("qC", [P, NT, P])
        h1D = sb("h1D", [P, NT, P])
        xbD = sb("xbD", [P, NT, P])
        euE = sb("euE", [P, NT, P])
        ruE = sb("ruE", [P, NT, P])
        y1E = sb("y1E", [P, NT, P])
        xmE = sb("xmE", [P, NT, P])
        ln = {k: dict(y=sb("y_" + k, [P, NT, P]) if k != "B" else None, st=sb("lnst_" + k, [P, NT, 6]), mv=sb("lnmv_" + k, [P, NT, 2]),
                      ve=sb("lnve_" + k, [P, NT]), r=sb("lnr_" + k, [P, NT]), nb=sb("lnnb_" + k, [P, NT]))
              for k in ("A", "B", "Z", "C", "D", "E")}

        zC = ln["Z"]["y"]
        psT = bank("psT")
        psS = bank("psS", 2)
        psG = bank("psG", 2)
        psF = bank("psF")
        psR = bank("psR")
        psM = bank("psM")
        psTb = psT[:, 0, :].bitcast(BF16)
        mA0, mA1, mA2, mB, mZ, mE = (psM[:, 0, 8 * k:8 * k + 8] for k in range(6))

        def tiles(ap):
            return ap.rearrange("p (t d) -> p t d", t=NT)

        def pair(ap):
            return ap.rearrange("p (t d) -> p t d", d=2)

        mask = vA
        cnt = idx = pA
        upper = dia = att[B]["w"]
        upper1 = vals = att[E]["w"]
        eye = paB
        tmp = att2_j
        sel_k = psumB[:, 0:EC]
        sel_i = sb("sel_i", [P, NT, EDGES])
        q_k = sb("q_k", [P, EC, N])
        tot = sb("tot", [P, NT])
        totb = sb("totb", [P, NT, P])
        off = sb("off", [P, NT])
        nxt = sb("nxt", [P, NT])
        kf_i = sb("kf_i", [P, EDGES], I32)
        kf = sb("kf", [P, EDGES])
        kc_i = sb("kc_i", [P, EC], I32)
        kc = sb("kc", [P, EC])
        ecol = sb("ecol", [P, EC])
        elast = sb("elast", [P, 1])
        rowm = sb("rowm", [P, NT])
        rowz = sb("rowz", [P, NT])
        rowr = sb("rowr", [P, NT])
        eps1 = sb("eps1", [P, 1])
        wT = sb("wT", [P, 2, P])
        arep = gin_j[:].rearrange("p t j -> p (t j)")[:, 0:5 * P].rearrange("p (k d) -> p k d", k=5)

        x_v = x.rearrange("b (t p) d -> b p t d", p=P)
        out_v = out.rearrange("b (t p) d -> b p t d", p=P)

        N_LOADS = 23 + EC
        mm, v, a = nc.tensor.matmul, nc.vector, nc.scalar

        def column(v):
            return v.rearrange("(p a) -> p a", a=1)

        def on_all(v):
            return v.rearrange("(a d) -> a d", a=1).partition_broadcast(P)

        with ExitStack() as setup_ctx:
            s = Signals()
            block = setup_ctx.enter_context(nc.Block())

            @block.sync
            def _(sp):
                sp.dma_start(adj_i[:], adj.rearrange("(t p) j -> p t j", p=P)).then_inc(s["adj_in"], 16)
                loads = [
                    (a01[:, 0:1], l0_a[0:P, :]), (a01[:, 1:2], l0_a[P:2 * P, :]),
                    (wp_sb[:], wp), (w1_sb[:], w1), (w2_sb[:], w2), (l2w0[:], l2_w[0]), (l2w1[:], l2_w[1]),
                    (w3_sb[:], l3_w), (avec[:, 0:1], column(a_src)), (avec[:, 1:2], column(a_dst)),
                    (avec[:, 2:3], l3_src), (avec[:, 3:4], l3_dst), (avec[:, 4:5], column(bp)),
                    (bp_row[:, 0, :], on_all(bp)), (gg_row[:, 0, :], on_all(gat_g)), (gb_row[:, 0, :], on_all(gat_b)),
                    (b1_row[:, 0, :], on_all(b1)), (mg_row[:, 0, :], on_all(mlp_g)), (mb_row[:, 0, :], on_all(mlp_b)),
                    (b2_row[:, 0, :], on_all(b2)), (l2b_row[:, 0, :], on_all(l2_bias)), (eps_c[:], on_all(eps)),
                    (elast[:], l2_e[0:1, EDGES - 1:EDGES].partition_broadcast(P)),
                ] + [(ecol[:, c:c + 1], column(l2_e[0, c * P:(c + 1) * P])) for c in range(EC)]
                assert len(loads) == N_LOADS
                for dst, src in loads:
                    sp.dma_start(dst, src).then_inc(s["weights_in"], 16)

            @block.gpsimd
            def _(pool):
                pool.memset(ident[:], 0.0).then_inc(s["ident0"], 1)
                pool.memset(identb[:], 0.0).then_inc(s["ident0"], 1)
                pool.memset(ones[:], 1.0).then_inc(s["ones_set"], 1)
                pool.memset(onesb[:], 1.0).then_inc(s["ones_set"], 1)
                pool.memset(mhalf[:, 0:1], -0.5).then_inc(s["half_set"], 1)
                pool.memset(mhalf[:, 1:2], 0.5).then_inc(s["half_set"], 1)
                pool.memset(upper[:], 1.0).then_inc(s["upper0"], 1)
                pool.memset(upper1[:], 1.0).then_inc(s["upper0"], 1)
                pool.memset(eye[:], 0.0).then_inc(s["upper0"], 1)
                pool.iota(kf_i[:], pattern=[[1, EDGES]], base=0, channel_multiplier=0).then_inc(s["iota_set"], 1)
                pool.iota(kc_i[:], pattern=[[P, EC]], base=0, channel_multiplier=1).then_inc(s["iota_set"], 1)
                pool.memset(spA[:], 0.0).then_inc(s["sp0"], 1)
                pool.memset(att[B]["sp"][:], 0.0).then_inc(s["sp0"], 1)
                pool.memset(att[E]["sp"][:], 0.0).then_inc(s["sp0"], 1)
                pool.wait_ge(s["ident0"], 2)
                for m in (ident, identb):
                    pool.affine_select(out=m[:], in_=m[:], compare_op=ALU.not_equal, fill=1.0, base=0,
                                       pattern=[[-1, P]], channel_multiplier=1).then_inc(s["ident_set"], 1)
                pool.wait_ge(s["upper0"], 3)
                above = dict(base=0, pattern=[[-P, NT], [1, N]], channel_multiplier=-1)
                pool.affine_select(out=upper[:], in_=upper[:], compare_op=ALU.is_gt, fill=0.0,
                                   **above).then_inc(s["upper_set"], 1)
                pool.affine_select(out=upper1[:], in_=upper1[:], compare_op=ALU.is_ge, fill=0.0,
                                   **above).then_inc(s["upper_set"], 1)
                pool.affine_select(out=eye[:], in_=eye[:], compare_op=ALU.not_equal, fill=1.0,
                                   **above).then_inc(s["eye_set"], 1)
                pool.wait_ge(s["sp0"], 3)
                pool.memset(spA[:, 0, :, 3:6], 1.0).then_inc(s["sp_ones"], 1)
                pool.memset(spA[:, 1, :, 0:3], 1.0).then_inc(s["sp_ones"], 1)
                pool.memset(att[E]["h"][:, :, P:P + 2], 1.0).then_inc(s["sp_ones"], 1)
                pool.wait_ge(s["weights_in"], 16 * N_LOADS)

            @block.tensor
            def _(pe):
                pe.wait_ge(s["ident_set"], 2)
                pe.wait_ge(s["ones_set"], 2)
                pe.wait_ge(s["sp_ones"], 3)
                pe.wait_ge(s["weights_in"], 16 * N_LOADS)
                nc.tensor.transpose(psM[:, 0, 0:P], wp_sb[:], ident[:])
                nc.tensor.transpose(psM[:, 0, P:2 * P], w3_sb[:], ident[:]).then_inc(s["wT_in_psum"], 1)
                pe.wait_ge(s["wT_ready"], 1)
                pe.wait_ge(s["arep_ready"], 1)
                for k in range(4):
                    mm(psF[:, 0, k * P:(k + 1) * P], wT[:, k // 2, :], arep[:, k, :], start=True, stop=True)
                mm(psM[:, 0, 256:258], arep[:, 4, :], avec[:, 0:2], start=True, stop=True).then_inc(s["wa_in_psum"], 1)
                pe.wait_ge(s["adj_in"], 16)
                for j in range(NT):
                    dst = psS[:, j % 2]
                    if j >= 2:
                        pe.wait_ge(s["adjT_copied"], j - 1)
                    for i in range(NT):
                        last = nc.tensor.transpose(dst[:, i * P:(i + 1) * P], adj_i[:, i, j * P:(j + 1) * P], ident[:])
                    last.then_inc(s["adjT_in_psum"], 1)
                pe.wait_ge(s["tot_ready"], 1)
                pe.wait_ge(s["upper_set"], 2)
                for n, u in enumerate((upper, upper1)):
                    for i in range(NT):
                        last = mm(psG[:, n], totb[:, i], u[:, i], start=(i == 0), stop=(i == NT - 1))
                last.then_inc(s["off_rows"], 1)
                for c in range(NT):
                    for i in range(NT):
                        last = mm(psR[:, 0, c:c + 1], upper[:, i, c * P:(c + 1) * P], tot[:, i:i + 1],
                                  start=(i == 0), stop=(i == NT - 1))
                last.then_inc(s["off_cols"], 1)
                pe.wait_ge(s["sel_ready"], 1)
                pe.wait_ge(s["adjT_copied"], NT)
                for c in range(EC):
                    for i in range(NT):
                        last = mm(psS[:, c], sel_i[:, i, c * P:(c + 1) * P], idx[:, i], start=(i == 0), stop=(i == NT - 1))
                last.then_inc(s["erow_in_psum"], 1)
                pe.wait_ge(s["q_ready"], 1)
                for i in range(NT):
                    if i >= 2:
                        pe.wait_ge(s["vals_taken"], i - 1)
                    for c in range(EC):
                        last = mm(psG[:, i % 2], sel_k[:, c, i * P:(i + 1) * P], q_k[:, c], start=(c == 0),
                                  stop=(c == EC - 1))
                    last.then_inc(s["vals_in_psum"], 1)
                pe.wait_ge(s["dia_ready"], 1)
                for i in range(NT):
                    last = mm(psR[:, 0], ones[:], dia[:, i], start=(i == 0), stop=(i == NT - 1))
                last.then_inc(s["diag_in_psum"], 1)
                for j in range(NT):
                    if j >= 2:
                        pe.wait_ge(s["att2T_copied"], j - 1)
                    for i in range(NT):
                        last = nc.tensor.transpose(psS[:, j % 2, i * P:(i + 1) * P], vals[:, i, j * P:(j + 1) * P], ident[:])
                    last.then_inc(s["att2T_in_psum"], 1)

            @block.vector
            def _(dve):

                def then(ins, name):
                    ins.then_inc(s[name], 1)
                    then.n[name] = then.n.get(name, 0) + 1
                    dve.wait_ge(s[name], then.n[name])
                then.n = {}

                dve.wait_ge(s["weights_in"], 16 * N_LOADS)
                for k in range(5):
                    last = v.tensor_copy(arep[:, k, :], avec[:, k:k + 1].to_broadcast([P, P]))
                last.then_inc(s["arep_ready"], 1)
                dve.wait_ge(s["wT_in_psum"], 1)
                v.tensor_copy(wT[:].rearrange("p a b -> p (a b)"), psM[:, 0, 0:2 * P]).then_inc(s["wT_ready"], 1)
                dve.wait_ge(s["adj_in"], 16)
                then(v.tensor_scalar(mask[:], adj_i[:], 0.0, None, ALU.is_gt), "mask_set")
                v.tensor_reduce(tot[:], mask[:], axis=AX_X, op=ALU.add).then_inc(s["tot0"], 1)
                dve.wait_ge(s["ones_set"], 2)
                dve.wait_ge(s["upper0"], 3)
                v.memset(tmp[:, 0], 1.0).then_inc(s["tmp_ones"], 1)
                dve.wait_ge(s["tot0"], 1)
                dve.wait_ge(s["tmp_ones"], 1)
                v.tensor_copy(totb[:], tot[:].unsqueeze(2).to_broadcast([P, NT, P])).then_inc(s["tot_ready"], 1)
                for i in range(NT):
                    last = v.tensor_tensor_scan(cnt[:, i], tmp[:, 0], mask[:, i], 0.0, ALU.mult, ALU.add)
                last.then_inc(s["cnt_ready"], 1)
                dve.wait_ge(s["wa_in_psum"], 1)
                for k, (rep, two) in enumerate(((ws1, st1), (wt1, st1), (ws3, st3), (wt3, st3))):
                    v.tensor_copy(rep[:], psF[:, 0, k * P:(k + 1) * P])
                    v.tensor_copy(two[:, k % 2:k % 2 + 1], psF[:, 0, k * P:k * P + 1])
                v.tensor_copy(bst[:, 0, :], psM[:, 0, 256:258]).then_inc(s["setup_done"], 1)
                for j in range(NT):
                    dve.wait_ge(s["adjT_in_psum"], j + 1)
                    v.tensor_copy(adj_j[:, j], psS[:, j % 2]).then_inc(s["adjT_copied"], 1)
                v.tensor_scalar(no1_i[:], adj_i[:], 0.0, -BIG, ALU.is_le, ALU.mult)
                dve.wait_ge(s["adjT_copied"], NT)
                v.tensor_scalar(no1_j[:], adj_j[:], 0.0, -BIG, ALU.is_le, ALU.mult)
                then(v.tensor_scalar(eps1[:], eps_c[:], 1.0, None, ALU.add), "eps_ready")
                dve.wait_ge(s["eye_set"], 1)
                v.scalar_tensor_tensor(gin_j[:], eye[:], eps1[:], adj_j[:], ALU.mult, ALU.add)
                dve.wait_ge(s["cnt_ready"], 1)
                for a, no in ((adj_i, no3_i), (adj_j, no3_j)):
                    then(v.tensor_tensor(tmp[:], a[:], eye[:], ALU.add), "loops")
                    then(v.tensor_scalar(tmp[:], tmp[:], 0.0, None, ALU.max), "loops")
                    then(v.tensor_scalar(no[:], tmp[:], 0.0, -BIG, ALU.is_equal, ALU.mult), "loops")
                dve.wait_ge(s["off_cols"], 1)
                then(v.tensor_copy(off[:], psR[:, 0, 0:NT]), "off_ready")
                then(v.tensor_tensor(nxt[:], off[:], tot[:], ALU.add), "off_ready")
                for i in range(NT):
                    last = v.scalar_tensor_tensor(idx[:, i], cnt[:, i], off[:, i:i + 1], mask[:, i], ALU.add, ALU.mult)
                then(last, "idx_ready")
                then(v.tensor_scalar(idx[:], idx[:], -1.0, None, ALU.add), "idx_ready")
                dve.wait_ge(s["iota_set"], 2)
                v.tensor_copy(kf[:], kf_i[:])
                then(v.tensor_copy(kc[:], kc_i[:]), "k_ready")
                for i in range(NT):
                    then(v.tensor_scalar(tmp[:, i, 0:EDGES], kf[:], off[:, i:i + 1], None, ALU.is_ge), "sel0")
                    last = v.scalar_tensor_tensor(sel_i[:, i], kf[:], nxt[:, i:i + 1], tmp[:, i, 0:EDGES], ALU.is_lt, ALU.mult)
                last.then_inc(s["sel_ready"], 1)
                dve.wait_ge(s["sel_ready"], 1)
                dve.wait_ge(s["off_rows"], 1)
                for c in range(EC):
                    then(v.tensor_scalar(tmp[:, c], psG[:, 0], kc[:, c:c + 1], None, ALU.is_le), "sel0")
                    then(v.scalar_tensor_tensor(sel_k[:, c], psG[:, 1], kc[:, c:c + 1], tmp[:, c], ALU.is_gt, ALU.mult), "sel0")
                dve.wait_ge(s["erow_in_psum"], 1)
                for c in range(EC):
                    last = v.tensor_scalar(q_k[:, c], psS[:, c], kc[:, c:c + 1], ecol[:, c:c + 1], ALU.is_equal, ALU.mult)
                last.then_inc(s["q_ready"], 1)
                then(v.tensor_scalar(tmp[:], idx[:], float(EDGES), elast[:], ALU.is_ge, ALU.mult), "past")
                dve.wait_ge(s["sel_ready"], 1)
                then(v.tensor_scalar(mask[:], mask[:], -1.0, -NEG, ALU.add, ALU.mult), "past")
                then(v.tensor_tensor(tmp[:], tmp[:], mask[:], ALU.add), "past")
                for i in range(NT):
                    dve.wait_ge(s["vals_in_psum"], i + 1)
                    v.tensor_tensor(vals[:, i], psG[:, i % 2], tmp[:, i], ALU.add).then_inc(s["vals_taken"], 1)
                dve.wait_ge(s["vals_taken"], NT)
                then(v.tensor_reduce(rowm[:], vals[:], axis=AX_X, op=ALU.max, negate=True), "rowm_ready")
                dve.wait_ge(s["exp2_ready"], 1)
                then(v.reciprocal(rowr[:], rowz[:]), "rowr_ready")
                for i in range(NT):
                    then(v.tensor_scalar(vals[:, i], vals[:, i], rowr[:, i:i + 1], None, ALU.mult), "att2")
                then(v.tensor_tensor(dia[:], vals[:], eye[:], ALU.mult), "att2")
                v.tensor_tensor(vals[:], vals[:], dia[:], ALU.subtract).then_inc(s["dia_ready"], 1)
                dve.wait_ge(s["diag_in_psum"], 1)
                v.tensor_copy(diag2[:], psR[:, 0])
                for j in range(NT):
                    dve.wait_ge(s["att2T_in_psum"], j + 1)
                    last = v.tensor_copy(att2_j[:, j], psS[:, j % 2])
                    last.then_inc(s["att2T_copied"], 1)
                dve.wait_ge(s["att2T_copied"], NT)
                v.tensor_copy(rowm[:, 0:1], rowr[:, 0:1]).then_inc(s["setup_done"], 1)

            @block.scalar
            def _(act):

                act.wait_ge(s["rowm_ready"], 1)
                for i in range(NT):
                    last = a.activation(vals[:, i], vals[:, i], ACT.Exp, bias=rowm[:, i:i + 1], accum_out=rowz[:, i:i + 1])
                last.then_inc(s["exp2_ready"], 1)
                act.wait_ge(s["exp2_ready"], 1)

        nc.clear_and_free_semaphores(list(s.values()))
        nc.all_engine_barrier()
        s = Signals()
        block = ctx.enter_context(nc.Block())

        def turns(eng, body):
            for it in range(STAGES):
                body(Turn(it, GRAPHS))
            with eng.Fori(STAGES, GRAPHS) as it:
                body(Turn(it, GRAPHS))
            for it in range(GRAPHS, GRAPHS + STAGES - 1):
                body(Turn(it, GRAPHS))

        SMALL = 9


        @block.sync
        def _(sp):
            def turn(t):
                if t.on(A):
                    sp.wait_ge(s["xA_transposed"], t.last(A))
                    sp.wait_ge(s["xA_scaled"], t.last(A))
                    sp.wait_ge(s["xhA_ready"], t.last(A))
                    sp.dma_start(xA[:], x_v[t.it]).then_inc(s["xA_in"], 16)
                if t.on(E):
                    sp.wait_ge(s["xout_ready"], t.now(E))
                    sp.dma_start(out_v[t.it - E], xout[:]).then_inc(s["xout_stored"], 16)

            turns(sp, turn)
            sp.wait_ge(s["xout_stored"], 16 * GRAPHS)

        @block.gpsimd
        def _(pool):
            def rstd(t, k, stage, var=None):
                L = ln[k]
                pool.wait_ge(s["stats_" + k], 1)
                pool.wait_ge(s["stats_" + k], t.now(stage))
                pool.tensor_scalar(L["ve"][:], var if var is not None else L["mv"][:, :, 1], LN_EPS, None,
                                   ALU.add).then_inc(s["ve_" + k], 1)
                pool.wait_ge(s["ve_" + k], t.now(stage))
                pool.wait_ge(s["nb_" + k], t.last(stage))
                pool.wait_ge(s["applied_" + k], t.last(stage))
                pool.tensor_tensor(L["r"][:], L["ve"][:], mhalf[:, 0:1].to_broadcast([P, NT]),
                                   ALU.pow).then_inc(s["rstd_" + k], 1)

            def turn(t):
                if t.on(C):
                    pool.wait_ge(s["applied_B"], t.last(B))
                    pool.wait_ge(s["qC_ready"], t.last(C))
                    pool.tensor_tensor(hbC[:], hgat[:], b2_row[:].to_broadcast([P, NT, P]),
                                       ALU.add).then_inc(s["hbC_ready"], 1)
                if t.on(A):
                    pool.wait_ge(s["xTA_ready"], t.now(A))
                    pool.wait_ge(s["y_A"], t.last(A))
                    pool.tensor_tensor(xhA[:], xA[:], mhalf[:, 1:2].unsqueeze(2).to_broadcast([P, NT, P]), ALU.add).then_inc(s["xhA_ready"], 1)
                if t.on(D):
                    pool.wait_ge(s["applied_C"], t.last(C))
                    pool.wait_ge(s["y_D"], t.last(D))
                    pool.tensor_tensor(xbD[:], xD[:], l2b_row[:].to_broadcast([P, NT, P]),
                                       ALU.add).then_inc(s["xbD_ready"], 1)
                    pool.wait_ge(s["xTD_ready"], t.now(D))
                    pool.wait_ge(s["aggD_ready"], t.last(D))
                if t.on(E):
                    pool.wait_ge(s["y_E"], t.last(E))
                if t.on(D):
                    pool.tensor_tensor(xTdD[:], xTD[:], diag2[:], ALU.mult).then_inc(s["xTdD_ready"], 1)
                if t.on(E):
                    pool.wait_ge(s["applied_D"], 1)
                    pool.wait_ge(s["applied_D"], t.last(D))
                    pool.tensor_scalar(xmE[:], xE[:], -1.0, None, ALU.add).then_inc(s["xmE_ready"], 1)
                if t.on(A):
                    pool.wait_ge(s["veA_ready"], t.now(A))
                    pool.wait_ge(s["expA"], NT * t.last(A))
                    pool.wait_ge(s["nmA_ready"], t.last(A))
                    pool.tensor_tensor(irA[:], veA[:], mhalf[:, 1:2], ALU.pow).then_inc(s["irA_ready"], 1)
                    pool.tensor_tensor(rA[:], veA[:], mhalf[:, 0:1], ALU.pow).then_inc(s["rA_ready"], 1)
                if t.on(C):
                    rstd(t, "Z", C)
                    pool.wait_ge(s["applied_Z"], t.now(C))
                    pool.tensor_tensor(zgC[:], znC[:], mg_row[:].to_broadcast([P, NT, P]),
                                       ALU.mult).then_inc(s["zgC_ready"], 1)
                    pool.wait_ge(s["zgC_ready"], t.now(C))
                    pool.wait_ge(s["zT_in_psum"], t.last(C))
                    pool.tensor_tensor(znC[:], zgC[:], mb_row[:].to_broadcast([P, NT, P]),
                                       ALU.add).then_inc(s["zbC_ready"], 1)
                if t.on(D):
                    rstd(t, "D", D)
                if t.on(B):
                    b = att[B]
                    for j in range(NT):
                        pool.wait_ge(s["expB"], t.tile(B, j))
                        pool.wait_ge(s["aggB_ready"], t.last(B))
                        pool.tensor_tensor(paB[:, j], b["p"][:, j], adj_j[:, j], ALU.mult).then_inc(s["paB"], 1)
                        if j:
                            before = b["p"][:, 0] if j == 1 else psumB[:, j - 2]
                            if j > 1:
                                pool.wait_ge(s["psB"], t.tile(B, j - 2, NT - 1))
                            pool.wait_ge(s["zsumB_ready"], t.last(B))
                            pool.tensor_tensor(psumB[:, j - 1], before, b["p"][:, j],
                                               ALU.add).then_inc(s["psB"], 1)
                if t.on(C):
                    rstd(t, "C", C)
                if t.on(A):
                    rstd(t, "A", A)
                if t.on(B):
                    rstd(t, "B", B, var=tvB[:])
                    pool.wait_ge(s["applied0_B"], t.now(B))
                    pool.tensor_tensor(ngB[:], nB[:], gg_row[:].to_broadcast([P, NT, P]),
                                       ALU.mult).then_inc(s["ngB_ready"], 1)
                    pool.wait_ge(s["ngB_ready"], t.now(B))
                    pool.tensor_tensor(nB[:], ngB[:], gb_row[:].to_broadcast([P, NT, P]),
                                       ALU.add).then_inc(s["nbB_ready"], 1)
                if t.on(E):
                    rstd(t, "E", E)

            turns(pool, turn)

        @block.tensor
        def _(pe):
            def transpose(src):
                for i in range(NT):
                    last = nc.tensor.transpose(psT[:, 0, i * P:(i + 1) * P], src[:, i], ident[:])
                return last

            def features(src, w):
                for i in range(NT):
                    last = mm(psF[:, 0, i * P:(i + 1) * P], src[:, i * P:(i + 1) * P], w, start=True, stop=True)
                return last

            def columns(dst, src, w):
                for i in range(NT):
                    last = mm(dst[:, 2 * i:2 * i + 2], src[:, i * P:(i + 1) * P], w, start=True, stop=True)
                return last

            IN_T = [("xTA_ready", A, 1), ("xTB_ready", B, 1), ("xTD_ready", D, 1), ("xTE_ready", E, 1),
                    ("sB_ready", B, 1), ("rowsA_ready", A, 1), ("sE_ready", E, 1), ("crowB", B, 1),
                    ("crowE", E, 1), ("zT_ready", C, 1)]
            IN_F = [("ginT_ready", C, 1), ("hB_ready", B, 1), ("y_Z", C, 1), ("h1D_ready", D, 1),
                    ("hE_ready", E, 1), ("qC_ready", C, 1)]
            IN_M = [("stA_ready", A, 1), ("meanA", A, 1), ("stB_taken", B, 1), ("varA", A, 1),
                    ("stE_taken", E, 1), ("rzB_ready", B, 1)]
            IN_R = [("maxB_ready", B, 1), ("maxE_ready", E, 1)]
            IN_S = [("vA", A, NT), ("wB", B, NT), ("wE", E, NT)]
            IN_G0 = [("y_D", D, 1), ("thA_ready", A, 1), ("euE_ready", E, 1)]
            IN_G1 = [("applied0_B", B, 1), ("euE_ready", E, 1)]

            def bank_free(t, readers, k):
                for back in range(1, len(readers) + 1):
                    name, stage, per = readers[k - back]
                    before = back > k
                    if Turn(t.it - before, GRAPHS).on(stage):
                        pe.wait_ge(s[name], per * (t.last(stage) if before else t.now(stage)))
                        return

            def split_rows(t, g, n):
                pe.wait_ge(s["sp" + n], t.now(g))
                bank_free(t, IN_T, {A: 5, B: 7, E: 8}[g])
                cols = [att[g]["sp"][:, i] for i in range(NT)] if g != A else \
                    [spA[:, k, i] for k in range(2) for i in range(NT)]
                for i, col in enumerate(cols):
                    last = nc.tensor.transpose(psTb[:, i * P:(i + 1) * P], col, identb[:])
                last.then_inc(s["rows_in_psum_" + n], 1)

            def project(t, g, n, xT, ws, wt, st, w):
                pe.wait_ge(s[f"xT{n}_ready"], t.now(g))
                bank_free(t, IN_T, 4 if g == B else 6)
                mm(psT[:, 0], ws[:], xT[:], start=True, stop=True).then_inc(s[f"s{n}_in_psum"], 1)
                bank_free(t, IN_M, 2 if g == B else 4)
                columns(mB if g == B else mE, xT, st[:]).then_inc(s[f"st{n}_in_psum"], 1)
                bank_free(t, IN_R, 0 if g == B else 1)
                mm(psR[:, 0], wt[:], xT[:], start=True, stop=True).then_inc(s[f"t{n}_in_psum"], 1)
                bank_free(t, IN_F, 1 if g == B else 4)
                features(xT, w[:]).then_inc(s[f"h{n}_in_psum"], 1)

            def score_tiles(t, g, n, no_edge, tile_done):
                pe.wait_ge(s["crow" + n], t.now(g))
                for j in range(NT):
                    if j >= 2:
                        pe.wait_ge(s[f"w{n}"], t.tile(g, j - 2))
                    mm(psS[:, j % 2], identb[:], no_edge[:, j], start=True, stop=False)
                    mm(psS[:, j % 2], onesb[:], att[g]["crow"][:], start=False, stop=True).then_inc(
                        s[f"cmask{n}"], 1)
                    if j >= 2:
                        tile_done(j - 2)
                for j in range(NT - 2, NT):
                    tile_done(j)

            def turn(t):
                if t.on(C):
                    pe.wait_ge(s["applied_B"], t.last(B))
                    bank_free(t, IN_F, 0)
                    for j in range(NT):
                        last = mm(psF[:, 0], hgat[:, j], gin_j[:, j], start=(j == 0), stop=(j == NT - 1))
                    last.then_inc(s["ginT_in_psum"], 1)
                if t.on(A):
                    pe.wait_ge(s["xA_in"], 16 * t.now(A))
                    bank_free(t, IN_T, 0)
                    transpose(xA).then_inc(s["xA_transposed"], 1)
                    pe.wait_ge(s["xTA_ready"], t.now(A))
                    pe.wait_ge(s["stA_ready"], t.last(A))
                    bank_free(t, IN_M, 0)
                    columns(mA0, xTA, a01[:]).then_inc(s["stA_in_psum"], 1)
                if t.on(B):
                    pe.wait_ge(s["applied_A"], t.last(A))
                    bank_free(t, IN_T, 1)
                    transpose(xB).then_inc(s["xB_transposed"], 1)
                if t.on(D):
                    pe.wait_ge(s["applied_C"], t.last(C))
                    bank_free(t, IN_T, 2)
                    transpose(xD).then_inc(s["xD_transposed"], 1)
                if t.on(A):
                    pe.wait_ge(s["stA_ready"], t.now(A))
                    mm(mA1, ones[:], stA[:].rearrange("p t c -> p (t c)"), start=True, stop=True).then_inc(
                        s["sumA_in_psum"], 1)
                if t.on(E):
                    pe.wait_ge(s["applied_D"], t.last(D))
                    bank_free(t, IN_T, 3)
                    transpose(xE).then_inc(s["xE_transposed"], 1)
                if t.on(B):
                    project(t, B, "B", xTB, ws1, wt1, st1, wp_sb)
                if t.on(A):
                    pe.wait_ge(s["sqA_ready"], t.now(A))
                    bank_free(t, IN_M, 3)
                    mm(mA2, ones[:], sqA[:].rearrange("p t c -> p (t c)"), start=True, stop=True).then_inc(
                        s["sqA_in_psum"], 1)
                if t.on(C):
                    pe.wait_ge(s["ginT_ready"], t.now(C))
                    bank_free(t, IN_F, 2)
                    features(ginT, w1_sb[:]).then_inc(s["z_in_psum"], 1)
                if t.on(D):
                    pe.wait_ge(s["xTD_ready"], t.now(D))
                    bank_free(t, IN_F, 3)
                    features(xTD, l2w1[:]).then_inc(s["h1D_in_psum"], 1)
                if t.on(A):
                    split_rows(t, A, "A")
                if t.on(E):
                    project(t, E, "E", xTE, ws3, wt3, st3, w3_sb)
                if t.on(B):
                    split_rows(t, B, "B")
                if t.on(A):
                    pe.wait_ge(s["rowsA_ready"], t.now(A))
                    for j in range(NT):
                        if j == 0:
                            bank_free(t, IN_S, 0)
                        if j >= 2:
                            pe.wait_ge(s["vA"], t.tile(A, j - 2))
                        mm(psS[:, j % 2], rowsA[:, N + j * P:N + (j + 1) * P], rowsA[:, 0:N], start=True,
                           stop=True).then_inc(s[f"eA{j}"], 1)
                if t.on(E):
                    split_rows(t, E, "E")
                if t.on(D):
                    pe.wait_ge(s["h1D_ready"], t.now(D))
                    pe.wait_ge(s["xTdD_ready"], t.now(D))
                    bank_free(t, IN_G0, 0)
                    for i in range(NT):
                        dst = psG[:, 0, i * P:(i + 1) * P]
                        for j in range(NT):
                            mm(dst, att2_j[:, j, i * P:(i + 1) * P], h1D[:, j], start=(j == 0), stop=False)
                        last = mm(dst, xTdD[:, i * P:(i + 1) * P], l2w0[:], start=False, stop=True)
                    last.then_inc(s["aggD_ready"], 1)
                if t.on(B):
                    bank_free(t, IN_S, 1)
                    pe.wait_ge(s["hB_ready"], t.now(B))

                    def aggregate(j):
                        if j == 0:
                            bank_free(t, IN_G1, 0)
                        pe.wait_ge(s["paB"], t.tile(B, j))
                        for i in range(NT):
                            last = mm(psG[:, 1, i * P:(i + 1) * P], paB[:, j, i * P:(i + 1) * P],
                                      att[B]["h"][:, j, 0:P], start=(j == 0 and i == 0), stop=(j == NT - 1),
                                      skip_group_check=True)
                        if j == NT - 1:
                            last.then_inc(s["aggB_ready"], 1)

                    score_tiles(t, B, "B", no1_j, aggregate)
                    pe.wait_ge(s["psB"], (NT - 1) * t.now(B))
                    bank_free(t, IN_M, 5)
                    for i in range(NT):
                        last = mm(mZ[:, i:i + 1], psumB[:, 2, i * P:(i + 1) * P], ones[:, 0:1], start=True, stop=True)
                    last.then_inc(s["zsumB_ready"], 1)
                if t.on(C):
                    pe.wait_ge(s["zbC_ready"], t.now(C))
                    bank_free(t, IN_T, 9)
                    transpose(znC).then_inc(s["zT_in_psum"], 1)
                if t.on(A):
                    pe.wait_ge(s["xA_scaled"], t.now(A))
                    bank_free(t, IN_G0, 1)
                    for i in range(NT):
                        for j in range(NT):
                            last = mm(psG[:, 0, i * P:(i + 1) * P], pA[:, j, i * P:(i + 1) * P], xsA[:, j],
                                      start=(j == 0), stop=(j == NT - 1))
                    last.then_inc(s["aggA_ready"], 1)
                if t.on(C):
                    pe.wait_ge(s["zT_ready"], t.now(C))
                    bank_free(t, IN_F, 5)
                    features(zT, w2_sb[:]).then_inc(s["x2C_in_psum"], 1)
                if t.on(E):
                    pe.wait_ge(s["hE_ready"], t.now(E))
                    bank_free(t, IN_S, 2)

                    def aggregate(j):
                        if j == 0:
                            bank_free(t, IN_G0, 2)
                            bank_free(t, IN_G1, 1)
                        pe.wait_ge(s["expE"], t.tile(E, j))
                        for i in range(NT):
                            k = (i % 2) * (P + 2)
                            last = mm(psG[:, i // 2, k:k + P + 2], att[E]["p"][:, j, i * P:(i + 1) * P],
                                      att[E]["h"][:, j], start=(j == 0 and i % 2 == 0), stop=(j == NT - 1),
                                      skip_group_check=True)
                        if j == NT - 1:
                            last.then_inc(s["aggE_ready"], 1)

                    score_tiles(t, E, "E", no3_j, aggregate)

            turns(pe, turn)

        @block.vector
        def _(dve):
            def stats(t, k, stage, src):
                L = ln[k]
                dve.wait_ge(s["y_" + k], t.now(stage))
                for i in range(NT):
                    last = v.bn_stats(L["st"][:, i], src[:, i])
                last.then_inc(s["bn_" + k], 1)
                dve.wait_ge(s["bn_" + k], 1)
                dve.wait_ge(s["bn_" + k], t.now(stage))
                dve.wait_ge(s["ve_" + k], t.last(stage))
                for i in range(NT):
                    last = v.bn_aggr(L["mv"][:, i], L["st"][:, i])
                last.then_inc(s["aggr_" + k if k == "B" else "stats_" + k], 1)

            def neg_mean(t, k, stage, rstd):
                L = ln[k]
                dve.wait_ge(s["applied_" + k], t.last(stage))
                v.scalar_tensor_tensor(L["nb"][:], L["mv"][:, :, 0], -1.0, rstd, ALU.mult,
                                       ALU.mult).then_inc(s["nb_" + k], 1)

            def neighbour_max(t, g, n, no_edge):
                b = att[g]
                small = s["small_" + n]
                dve.wait_ge(s[f"st{n}_in_psum"], t.now(g))
                dve.wait_ge(s["exp" + n], NT * t.last(g))
                if g == B:
                    dve.wait_ge(s["paB"], NT * t.last(B))
                    dve.wait_ge(s["psB"], (NT - 1) * t.last(B))
                else:
                    dve.wait_ge(s["aggE_ready"], t.last(E))
                src = pair(mB if g == B else mE)
                if g == B:
                    v.tensor_tensor(b["st"][:], src, bst[:].to_broadcast([P, NT, 2]), ALU.add).then_inc(
                        s["stB_taken"], 1)
                else:
                    v.tensor_copy(b["st"][:], src).then_inc(s["stE_taken"], 1)
                dve.wait_ge(s[f"st{n}_taken"], t.now(g))
                v.tensor_scalar(b["nt"][:], b["st"][:, :, 1], -1.0, None, ALU.mult).then_inc(small, 1)
                v.tensor_scalar(b["q"][:], b["st"][:, :, 0], 0.25, None, ALU.mult).then_inc(small, 1)
                dve.wait_ge(s[f"t{n}_in_psum"], 1)
                dve.wait_ge(s[f"t{n}_in_psum"], t.now(g))
                for i in range(NT):
                    last = v.tensor_tensor_reduce(out=b["w"][:, i], in0=psR[:, 0], in1=no_edge[:, i], scale=1.0,
                                                  scalar=-3e38, op0=ALU.add, op1=ALU.max,
                                                  accum_out=b["mx"][:, i:i + 1])
                last.then_inc(s[f"max{n}_ready"], 1)
                dve.wait_ge(s[f"max{n}_ready"], t.now(g))
                if g == B:
                    v.scalar_tensor_tensor(b["u"][:], b["mx"][:], bst[:, 0, 1:2], b["st"][:, :, 0], ALU.add,
                                           ALU.add).then_inc(small, 1)
                else:
                    v.tensor_tensor(b["u"][:], b["mx"][:], b["st"][:, :, 0], ALU.add).then_inc(small, 1)
                dve.wait_ge(small, t.tile(g, 2, SMALL))
                v.scalar_tensor_tensor(b["m"][:], b["u"][:], SLOPE, b["u"][:], ALU.mult, ALU.max).then_inc(small, 1)
                dve.wait_ge(small, t.tile(g, 3, SMALL))
                v.scalar_tensor_tensor(b["c"][:, :, 0], b["m"][:], -1.25, b["q"][:], ALU.mult, ALU.add).then_inc(
                    small, 1)
                dve.wait_ge(s["rows_in_psum_" + n], t.last(g))
                parts = [b["sp"][:, :, k:k + 1] for k in range(3)]
                dve.wait_ge(small, t.tile(g, 4, SMALL))
                v.tensor_copy(parts[0], b["c"][:]).then_inc(small, 1)
                dve.wait_ge(small, t.tile(g, 5, SMALL))
                v.tensor_tensor(b["r1"][:], b["c"][:], parts[0], ALU.subtract).then_inc(small, 1)
                dve.wait_ge(small, t.tile(g, 6, SMALL))
                v.tensor_copy(parts[1], b["r1"][:]).then_inc(small, 1)
                dve.wait_ge(small, t.tile(g, 7, SMALL))
                v.tensor_tensor(b["r2"][:], b["r1"][:], parts[1], ALU.subtract).then_inc(small, 1)
                dve.wait_ge(small, t.tile(g, 8, SMALL))
                v.tensor_copy(parts[2], b["r2"][:]).then_inc(s["sp" + n], 1)

            def exponents(t, g, n):
                b = att[g]
                dve.wait_ge(s[f"s{n}_ready"], t.now(g))
                for j in range(NT):
                    dve.wait_ge(s[f"cmask{n}"], t.tile(g, j))
                    v.scalar_tensor_tensor(b["w"][:, j], b["srow"][:], b["nt"][:, j:j + 1], psS[:, j % 2],
                                           ALU.max, ALU.add).then_inc(s[f"w{n}"], 1)

            def turn(t):
                if t.on(A):
                    dve.wait_ge(s["stA_in_psum"], t.now(A))
                    dve.wait_ge(s["cenA_ready"], t.last(A))
                    v.tensor_copy(stA[:], pair(mA0)).then_inc(s["stA_ready"], 1)
                    dve.wait_ge(s["sumA_in_psum"], t.now(A))
                    v.tensor_reduce(meanA[:, 0, :], pair(mA1).rearrange("p t c -> p c t"), axis=AX_X,
                                    op=ALU.add).then_inc(s["meanA"], 1)
                    dve.wait_ge(s["meanA"], t.now(A))
                    dve.wait_ge(s["spA"], t.last(A))
                    v.scalar_tensor_tensor(cenA[:], meanA[:].to_broadcast([P, NT, 2]), -1.0 / N, stA[:], ALU.mult,
                                           ALU.add).then_inc(s["cenA_ready"], 1)
                    dve.wait_ge(s["cenA_ready"], t.now(A))
                    v.tensor_tensor(sqA[:], cenA[:], cenA[:], ALU.mult).then_inc(s["sqA_ready"], 1)
                if t.on(B):
                    neighbour_max(t, B, "B", no1_i)
                    dve.wait_ge(s["hB_in_psum"], t.now(B))
                    dve.wait_ge(s["aggB_ready"], t.last(B))
                    v.tensor_tensor(att[B]["h"][:, :, 0:P], tiles(psF[:, 0]), bp_row[:].to_broadcast([P, NT, P]),
                                    ALU.add).then_inc(s["hB_ready"], 1)
                if t.on(A):
                    dve.wait_ge(s["sqA_in_psum"], t.now(A))
                    v.tensor_reduce(varA[:, 0:1], mA2, axis=AX_X, op=ALU.add).then_inc(s["varA"], 1)
                    dve.wait_ge(s["varA"], t.now(A))
                    dve.wait_ge(s["rA_ready"], t.last(A))
                    v.tensor_scalar(veA[:], varA[:, 0:1], 1.0 / N, PAIR_EPS, ALU.mult, ALU.add).then_inc(
                        s["veA_ready"], 1)
                if t.on(C):
                    dve.wait_ge(s["z_in_psum"], t.now(C))
                    dve.wait_ge(s["applied_Z"], t.last(C))
                    v.tensor_tensor(zC[:], tiles(psF[:, 0]), b1_row[:].to_broadcast([P, NT, P]), ALU.add).then_inc(
                        s["y_Z"], 1)
                    stats(t, "Z", C, zC)
                if t.on(A):
                    dve.wait_ge(s["irA_ready"], t.now(A))
                    v.tensor_scalar(cenA[:, :, 1], cenA[:, :, 1], irA[:], None, ALU.add).then_inc(s["tirA"], 1)
                    dve.wait_ge(s["tirA"], t.now(A))
                    dve.wait_ge(s["rows_in_psum_A"], t.last(A))
                    flat = spA[:].rearrange("p h t c -> p t h c")
                    split_to = lambda k: [spA[:, 0, :, k:k + 1], spA[:, 1, :, 3 + k:4 + k]]
                    for k, (val, rest) in enumerate(((cenA, r1A), (r1A, r2A), (r2A, None))):
                        for h in range(2):
                            last = v.tensor_copy(split_to(k)[h], val[:, :, h:h + 1])
                        last.then_inc(s[("hiA", "midA", "spA")[k]], 1)
                        if rest is not None:
                            dve.wait_ge(s[("hiA", "midA")[k]], t.now(A))
                            for h in range(2):
                                last = v.tensor_tensor(rest[:, :, h:h + 1], val[:, :, h:h + 1], split_to(k)[h],
                                                       ALU.subtract)
                            last.then_inc(s[("rest1A", "rest2A")[k]], 1)
                            dve.wait_ge(s[("rest1A", "rest2A")[k]], t.now(A))
                if t.on(E):
                    neighbour_max(t, E, "E", no3_i)
                if t.on(C):
                    dve.wait_ge(s["rstd_Z"], t.now(C))
                    neg_mean(t, "Z", C, ln["Z"]["r"][:])
                if t.on(A):
                    for j in range(NT):
                        dve.wait_ge(s[f"eA{j}"], 1)
                        dve.wait_ge(s[f"eA{j}"], t.now(A))
                        v.tensor_tensor_reduce(out=vA[:, j], in0=psS[:, j % 2], in1=adj_j[:, j], scale=1.0,
                                               scalar=-3e38, op0=ALU.mult, op1=ALU.max,
                                               accum_out=vmaxA[:, j:j + 1]).then_inc(s["vA"], 1)
                    dve.wait_ge(s["vA"], NT * t.now(A))
                    v.scalar_tensor_tensor(lmA[:], vmaxA[:], SLOPE, vmaxA[:], ALU.mult, ALU.max).then_inc(s["lmA"], 1)
                    dve.wait_ge(s["lmA"], t.now(A))
                    dve.wait_ge(s["rA_ready"], t.now(A))
                    dve.wait_ge(s["expA"], NT * t.last(A))
                    v.tensor_scalar(nmA[:], lmA[:], rA[:], -1.0, ALU.mult, ALU.mult).then_inc(s["nmA_ready"], 1)
                    dve.wait_ge(s["aggA_ready"], t.last(A))
                    for j in range(NT):
                        v.scalar_tensor_tensor(pA[:, j], vA[:, j], SLOPE, vA[:, j], ALU.mult, ALU.max).then_inc(
                            s["lA"], 1)
                if t.on(D):
                    dve.wait_ge(s["aggD_ready"], t.now(D))
                    dve.wait_ge(s["xbD_ready"], t.now(D))
                    dve.wait_ge(s["applied_D"], t.last(D))
                    v.tensor_tensor(ln["D"]["y"][:], tiles(psG[:, 0]), xbD[:], ALU.add).then_inc(s["y_D"], 1)
                    stats(t, "D", D, ln["D"]["y"])
                if t.on(B):
                    exponents(t, B, "B")
                if t.on(A):
                    dve.wait_ge(s["expA"], NT * t.now(A))
                    v.reciprocal(rzA[:], zsA[:]).then_inc(s["rzA"], 1)
                    dve.wait_ge(s["rzA"], t.now(A))
                    dve.wait_ge(s["aggA_ready"], t.last(A))
                    for j in range(NT):
                        last = v.tensor_scalar(xsA[:, j], xA[:, j], rzA[:, j:j + 1], None, ALU.mult)
                    last.then_inc(s["xA_scaled"], 1)
                if t.on(D):
                    dve.wait_ge(s["rstd_D"], t.now(D))
                    neg_mean(t, "D", D, ln["D"]["r"][:])
                if t.on(C):
                    dve.wait_ge(s["x2C_in_psum"], t.now(C))
                    dve.wait_ge(s["hbC_ready"], t.now(C))
                    v.tensor_tensor(qC[:], tiles(psF[:, 0]), hbC[:], ALU.add).then_inc(s["qC_ready"], 1)
                    dve.wait_ge(s["qC_ready"], t.now(C))
                    dve.wait_ge(s["applied_C"], t.last(C))
                    v.scalar_tensor_tensor(ln["C"]["y"][:], qC[:], 0.0, xBC[:], ALU.max, ALU.add).then_inc(s["y_C"], 1)
                    stats(t, "C", C, ln["C"]["y"])
                if t.on(B):
                    dve.wait_ge(s["applied_A"], t.last(A))
                    dve.wait_ge(s["y_C"], t.now(C))
                    v.tensor_copy(xBC[:], xB[:]).then_inc(s["xBC_ready"], 1)
                    dve.wait_ge(s["aggB_ready"], t.now(B))
                    for i in range(NT):
                        last = v.bn_stats(ln["B"]["st"][:, i], psG[:, 1, i * P:(i + 1) * P])
                    last.then_inc(s["bn_B"], 1)
                    dve.wait_ge(s["zsumB_ready"], t.now(B))
                    v.reciprocal(att[B]["rz"][:], mZ[:, 0:NT]).then_inc(s["rzB_ready"], 1)
                    dve.wait_ge(s["rzB_ready"], 1)
                    dve.wait_ge(s["bn_B"], t.now(B))
                    dve.wait_ge(s["rzB_ready"], t.now(B))
                    for i in range(NT):
                        last = v.bn_aggr(ln["B"]["mv"][:, i], ln["B"]["st"][:, i])
                    last.then_inc(s["aggr_B"], 1)
                    v.tensor_tensor(rrB[:], att[B]["rz"][:], att[B]["rz"][:], ALU.mult).then_inc(s["rrB"], 1)
                    dve.wait_ge(s["aggr_B"], t.now(B))
                    dve.wait_ge(s["rrB"], t.now(B))
                    dve.wait_ge(s["ve_B"], t.last(B))
                    v.tensor_tensor(tvB[:], ln["B"]["mv"][:, :, 1], rrB[:], ALU.mult).then_inc(s["stats_B"], 1)
                if t.on(A):
                    dve.wait_ge(s["thA_ready"], t.now(A))
                    dve.wait_ge(s["xhA_ready"], t.now(A))
                    dve.wait_ge(s["applied_A"], t.last(A))
                    v.scalar_tensor_tensor(ln["A"]["y"][:], thA[:], 0.5, xhA[:], ALU.mult, ALU.add).then_inc(s["y_A"], 1)
                    stats(t, "A", A, ln["A"]["y"])
                if t.on(C):
                    dve.wait_ge(s["rstd_C"], t.now(C))
                    neg_mean(t, "C", C, ln["C"]["r"][:])
                if t.on(B):
                    dve.wait_ge(s["rstd_B"], t.now(B))
                    dve.wait_ge(s["applied0_B"], t.last(B))
                    v.tensor_tensor(scB[:], ln["B"]["r"][:], att[B]["rz"][:], ALU.mult).then_inc(s["scB_ready"], 1)
                    dve.wait_ge(s["scB_ready"], t.now(B))
                    neg_mean(t, "B", B, scB[:])
                if t.on(E):
                    exponents(t, E, "E")
                if t.on(A):
                    dve.wait_ge(s["rstd_A"], t.now(A))
                    neg_mean(t, "A", A, ln["A"]["r"][:])
                if t.on(E):
                    dve.wait_ge(s["aggE_ready"], t.now(E))
                    dve.wait_ge(s["ruE_ready"], t.last(E))
                    for i in range(NT):
                        k = (i % 2) * (P + 2) + P
                        last = v.reciprocal(att[E]["rz"][:, i:i + 1], psG[:, i // 2, k:k + 1])
                    last.then_inc(s["rzE_ready"], 1)
                    dve.wait_ge(s["ruE_ready"], t.now(E))
                    dve.wait_ge(s["euE_ready"], t.now(E))
                    v.scalar_tensor_tensor(y1E[:], euE[:], 1.0, ruE[:], ALU.min, ALU.add).then_inc(s["y1E"], 1)
                    dve.wait_ge(s["y1E"], t.now(E))
                    dve.wait_ge(s["xmE_ready"], t.now(E))
                    dve.wait_ge(s["applied_E"], t.last(E))
                    v.tensor_tensor(ln["E"]["y"][:], y1E[:], xmE[:], ALU.add).then_inc(s["y_E"], 1)
                    stats(t, "E", E, ln["E"]["y"])
                    dve.wait_ge(s["rstd_E"], t.now(E))
                    neg_mean(t, "E", E, ln["E"]["r"][:])

            turns(dve, turn)

        @block.scalar
        def _(act):
            def normalise(t, k, stage, src, dst, scale=None, name=None):
                L = ln[k]
                act.wait_ge(s["nb_" + k], t.now(stage))
                act.wait_ge(s["rstd_" + k], t.now(stage))
                for i in range(NT):
                    last = a.activation(dst[:, i], src(i), ACT.Identity, scale=(L["r"] if scale is None else scale)[:, i:i + 1],
                                        bias=L["nb"][:, i:i + 1])
                last.then_inc(s[name or "applied_" + k], 1)

            def exps(t, g, n):
                b = att[g]
                for j in range(NT):
                    act.wait_ge(s[f"w{n}"], t.tile(g, j))
                    a.activation(b["p"][:, j], b["w"][:, j], ACT.Exp, scale=1.0 - SLOPE,
                                 bias=b["st"][:, j, 1:2]).then_inc(s[f"exp{n}"], 1)

            def turn(t):
                if t.on(A):
                    act.wait_ge(s["xA_transposed"], t.now(A))
                    act.wait_ge(s["stA_in_psum"], t.last(A))
                    a.copy(xTA[:], psT[:, 0]).then_inc(s["xTA_ready"], 1)
                if t.on(C):
                    act.wait_ge(s["ginT_in_psum"], t.now(C))
                    act.wait_ge(s["z_in_psum"], t.last(C))
                    a.copy(ginT[:], psF[:, 0]).then_inc(s["ginT_ready"], 1)
                if t.on(B):
                    act.wait_ge(s["xB_transposed"], t.now(B))
                    act.wait_ge(s["hB_in_psum"], t.last(B))
                    a.copy(xTB[:], psT[:, 0]).then_inc(s["xTB_ready"], 1)
                if t.on(D):
                    act.wait_ge(s["xD_transposed"], t.now(D))
                    act.wait_ge(s["h1D_in_psum"], t.last(D))
                    act.wait_ge(s["xTdD_ready"], t.last(D))
                    a.copy(xTD[:], psT[:, 0]).then_inc(s["xTD_ready"], 1)
                if t.on(E):
                    act.wait_ge(s["xE_transposed"], t.now(E))
                    act.wait_ge(s["hE_in_psum"], t.last(E))
                    a.copy(xTE[:], psT[:, 0]).then_inc(s["xTE_ready"], 1)
                if t.on(B):
                    act.wait_ge(s["sB_in_psum"], t.now(B))
                    act.wait_ge(s["wB"], NT * t.last(B))
                    a.activation(att[B]["srow"][:], psT[:, 0], ACT.Identity, bias=bst[:, 0, 0:1]).then_inc(
                        s["sB_ready"], 1)
                if t.on(D):
                    act.wait_ge(s["h1D_in_psum"], t.now(D))
                    act.wait_ge(s["aggD_ready"], t.last(D))
                    a.copy(h1D[:].rearrange("p t d -> p (t d)"), psF[:, 0]).then_inc(s["h1D_ready"], 1)
                if t.on(A):
                    act.wait_ge(s["rows_in_psum_A"], t.now(A))
                    act.wait_ge(s["eA3"], t.last(A))
                    a.copy(rowsA[:], psTb).then_inc(s["rowsA_ready"], 1)
                if t.on(E):
                    act.wait_ge(s["sE_in_psum"], t.now(E))
                    act.wait_ge(s["wE"], NT * t.last(E))
                    a.copy(att[E]["srow"][:], psT[:, 0]).then_inc(s["sE_ready"], 1)
                    act.wait_ge(s["hE_in_psum"], t.now(E))
                    act.wait_ge(s["aggE_ready"], t.last(E))
                    a.copy(att[E]["h"][:, :, 0:P], tiles(psF[:, 0])).then_inc(s["hE_ready"], 1)
                if t.on(B):
                    act.wait_ge(s["rows_in_psum_B"], t.now(B))
                    act.wait_ge(s["cmaskB"], NT * t.last(B))
                    a.copy(att[B]["crow"][:], psTb[:, 0:N]).then_inc(s["crowB"], 1)
                if t.on(C):
                    act.wait_ge(s["zgC_ready"], t.last(C))
                    act.wait_ge(s["zT_in_psum"], t.last(C))
                    normalise(t, "Z", C, lambda i: zC[:, i], znC)
                if t.on(E):
                    act.wait_ge(s["rows_in_psum_E"], t.now(E))
                    act.wait_ge(s["cmaskE"], NT * t.last(E))
                    a.copy(att[E]["crow"][:], psTb[:, 0:N]).then_inc(s["crowE"], 1)
                if t.on(A):
                    act.wait_ge(s["nmA_ready"], t.now(A))
                    act.wait_ge(s["aggA_ready"], t.last(A))
                    act.wait_ge(s["rzA"], t.last(A))
                    for j in range(NT):
                        act.wait_ge(s["lA"], t.tile(A, j))
                        a.activation(pA[:, j], pA[:, j], ACT.Exp, scale=rA[:], bias=nmA[:, j:j + 1],
                                     accum_out=zsA[:, j:j + 1]).then_inc(s["expA"], 1)
                if t.on(B):
                    exps(t, B, "B")
                if t.on(D):
                    act.wait_ge(s["xmE_ready"], t.now(E))
                    act.wait_ge(s["xE_transposed"], t.now(E))
                    normalise(t, "D", D, lambda i: ln["D"]["y"][:, i], xE)
                if t.on(C):
                    act.wait_ge(s["zT_in_psum"], t.now(C))
                    act.wait_ge(s["x2C_in_psum"], t.last(C))
                    a.activation(zT[:], psT[:, 0], ACT.Relu).then_inc(s["zT_ready"], 1)
                if t.on(A):
                    act.wait_ge(s["aggA_ready"], t.now(A))
                    act.wait_ge(s["y_A"], t.last(A))
                    a.activation(thA[:], tiles(psG[:, 0]), ACT.Tanh, scale=0.5).then_inc(s["thA_ready"], 1)
                if t.on(C):
                    act.wait_ge(s["xbD_ready"], t.now(D))
                    act.wait_ge(s["xD_transposed"], t.now(D))
                    normalise(t, "C", C, lambda i: ln["C"]["y"][:, i], xD)
                if t.on(B):
                    act.wait_ge(s["nbB_ready"], t.last(B))
                    act.wait_ge(s["applied_B"], t.last(B))
                    act.wait_ge(s["scB_ready"], t.now(B))
                    normalise(t, "B", B, lambda i: psG[:, 1, i * P:(i + 1) * P], nB, scale=scB, name="applied0_B")
                if t.on(E):
                    exps(t, E, "E")
                if t.on(A):
                    act.wait_ge(s["xB_transposed"], t.now(B))
                    act.wait_ge(s["xBC_ready"], t.now(B))
                    normalise(t, "A", A, lambda i: ln["A"]["y"][:, i], xB)
                if t.on(B):
                    act.wait_ge(s["nbB_ready"], t.now(B))
                    act.wait_ge(s["hbC_ready"], t.now(C))
                    act.wait_ge(s["ginT_in_psum"], t.now(C))
                    a.activation(hgat[:], nB[:], ACT.Relu).then_inc(s["applied_B"], 1)
                if t.on(E):
                    act.wait_ge(s["rzE_ready"], t.now(E))
                    act.wait_ge(s["y1E"], t.last(E))
                    for f, dst, name in ((ACT.Relu, ruE, "ruE_ready"), (ACT.Exp, euE, "euE_ready")):
                        for i in range(NT):
                            k = (i % 2) * (P + 2)
                            last = a.activation(dst[:, i], psG[:, i // 2, k:k + P], f, scale=att[E]["rz"][:, i:i + 1])
                        last.then_inc(s[name], 1)
                    act.wait_ge(s["xout_stored"], 16 * t.last(E))
                    normalise(t, "E", E, lambda i: ln["E"]["y"][:, i], xout, name="xout_ready")
                    act.sem_inc(s["applied_E"], 1)

            turns(act, turn)


_INS = ["x", "adj", "L0_gnn_a", "L1_gnn_Wp", "L1_gnn_bp", "L1_gnn_a_src", "L1_gnn_a_dst", "L1_gnn_gat_g",
        "L1_gnn_gat_b", "L1_gnn_eps", "L1_gnn_W1", "L1_gnn_b1", "L1_gnn_mlp_g", "L1_gnn_mlp_b", "L1_gnn_W2",
        "L1_gnn_b2", "L2_gnn_W", "L2_gnn_e", "L2_gnn_bias", "L3_gnn_W", "L3_gnn_a_src", "L3_gnn_a_dst"]


def kernel(**inputs):
    import numpy as _np
    import concourse.bacc as _bacc
    from concourse import mybir as _mybir
    from concourse.bass_utils import run_bass_kernel_spmd as _run

    nc = _bacc.Bacc("TRN2", target_bir_lowering=False, num_devices=1)
    arrays, args = {}, []
    for name in _INS:
        a = _np.ascontiguousarray(inputs[name])
        arrays[f"in_{name}_dram"] = a
        args.append(nc.dram_tensor(f"in_{name}_dram", a.shape, _mybir.dt.from_np(a.dtype), kind="ExternalInput").ap())
    out = nc.dram_tensor("out_0_dram", inputs["x"].shape, _mybir.dt.float32, kind="ExternalOutput").ap()
    resnorm_gnn(nc, *args, out)
    r = _run(nc, [arrays], core_ids=[0])
    return r.results[0]["out_0_dram"]
```

```python
from contextlib import ExitStack

import concourse.bass as bass
from concourse import mybir

P = 128
ALU = mybir.AluOpType
ACT = mybir.ActivationFunctionType
AX_X = mybir.AxisListType.X
F32 = mybir.dt.float32
BF16 = mybir.dt.bfloat16
I32 = mybir.dt.int32

B, E = "BE"
LAST_DELAY = 5
BIG = 2.0 ** 100
SLOPE = 0.2
LN_EPS = 1e-5
PAIR_EPS = 1e-14
NEG = -9000000000000000.0


class Graph:

    def __init__(self, turn, delay):
        self.turn, self.delay = turn, delay
        self.g = turn.it - delay
        self.real = not isinstance(turn.it, int) or 0 <= self.g < turn.graphs
        self.now = turn.it - (delay - 1)
        self.last = self.g

    def tile(self, j, tiles=4):
        return self.now if tiles == 1 else self.g * tiles + (j + 1)


class Turn:
    def __init__(self, it, graphs):
        self.it, self.graphs = it, graphs

    def graph(self, delay):
        return Graph(self, delay)

    def run(self, step, delay):
        g = self.graph(delay)
        if g.real:
            step(g)


def resnorm_gnn(nc, x, adj, l0_a, wp, bp, a_src, a_dst, gat_g, gat_b, eps, w1, b1, mlp_g, mlp_b, w2, b2,
                l2_w, l2_e, l2_bias, l3_w, l3_src, l3_dst, out):
    GRAPHS, N, DIM = x.shape
    NT = N // P
    assert DIM == P and N == NT * P
    EDGES = l2_e.shape[1]
    EC = EDGES // P

    with ExitStack() as ctx:
        def sb(name, shape, dt=F32):
            return ctx.enter_context(nc.sbuf_tensor(name, shape, dt))

        def bank(name, n=1):
            return ctx.enter_context(nc.psum_tensor(name, [P, n, 512], F32))

        class Signals(dict):

            def __missing__(self, name):
                self[name] = nc.alloc_semaphore(name=name)
                return self[name]

        ident = sb("ident", [P, P])
        identb = sb("identb", [P, P], BF16)
        ones = sb("ones", [P, P])
        onesb = sb("onesb", [P, P], BF16)
        consts = sb("consts", [P, 4])
        adj_i = sb("adj_i", [P, NT, N])
        adj_j = sb("adj_j", [P, NT, N])
        gin_j = sb("gin_j", [P, NT, N])
        att2_j = sb("att2_j", [P, NT, N])
        diag2 = sb("diag2", [P, N])
        no1_i = sb("no1_i", [P, NT, N], BF16)
        no1_j = sb("no1_j", [P, NT, N], BF16)
        no3_i = sb("no3_i", [P, NT, N], BF16)
        no3_j = sb("no3_j", [P, NT, N], BF16)
        a01 = sb("a01", [P, 2])
        wp_sb = sb("wp_sb", [P, P])
        w1_sb = sb("w1_sb", [P, P])
        w2_sb = sb("w2_sb", [P, P])
        l2w0 = sb("l2w0", [P, P])
        l2w1 = sb("l2w1", [P, P])
        w3_sb = sb("w3_sb", [P, P])
        bp_row = sb("bp_row", [P, 1, P])
        gg_row = sb("gg_row", [P, 1, P])
        gb_row = sb("gb_row", [P, 1, P])
        b1_row = sb("b1_row", [P, 1, P])
        mg_row = sb("mg_row", [P, 1, P])
        mb_row = sb("mb_row", [P, 1, P])
        b2_row = sb("b2_row", [P, 1, P])
        l2b_row = sb("l2b_row", [P, 1, P])
        avec = sb("avec", [P, 5])
        eps_c = sb("eps_c", [P, 1])
        ws1 = sb("ws1", [P, P])
        wt1 = sb("wt1", [P, P])
        ws3 = sb("ws3", [P, P])
        wt3 = sb("wt3", [P, P])
        st1 = sb("st1", [P, 2])
        st3 = sb("st3", [P, 2])
        bst = sb("bst", [P, 1, 2])
        xA = sb("xA", [P, NT, P])
        xB = sb("xB", [P, NT, P])
        xBC = sb("xBC", [P, NT, P])
        hgat = sb("hgat", [P, NT, P])
        xD = sb("xD", [P, NT, P])
        xE = sb("xE", [P, NT, P])
        xout = sb("xout", [P, NT, P])
        xTA = sb("xTA", [P, N])
        xTB = sb("xTB", [P, N])
        xTD = sb("xTD", [P, N])
        xTE = sb("xTE", [P, N])
        xTdD = sb("xTdD", [P, N])
        ginT = sb("ginT", [P, N])
        zT = sb("zT", [P, N])
        stA = sb("stA", [P, NT, 2])
        cenA = sb("cenA", [P, NT, 2])
        sqA = sb("sqA", [P, NT, 2])
        meanA = sb("meanA", [P, 1, 2])
        varA = sb("varA", [P, 2])
        veA = sb("veA", [P, 1])
        rA = sb("rA", [P, 1])
        irA = sb("irA", [P, 1])
        rowsA = sb("rowsA", [P, 2 * N], BF16)
        spA = sb("spA", [P, 2, NT, P], BF16)
        r1A = sb("r1A", [P, NT, 2])
        r2A = sb("r2A", [P, NT, 2])
        vA = sb("vA", [P, NT, N])
        vmaxA = sb("vmaxA", [P, NT])
        lmA = sb("lmA", [P, NT])
        nmA = sb("nmA", [P, NT])
        pA = sb("pA", [P, NT, N])
        zsA = sb("zsA", [P, NT])
        rzA = sb("rzA", [P, NT])
        xsA = sb("xsA", [P, NT, P])
        xhA = sb("xhA", [P, NT, P])
        thA = sb("thA", [P, NT, P])
        att = {}
        for g in (B, E):
            n = g
            att[g] = dict(
                h=sb("h" + n, [P, NT, P + 2]), st=sb("st" + n, [P, NT, 2]), nt=sb("nt" + n, [P, NT]),
                srow=sb("srow" + n, [P, N]), mx=sb("mx" + n, [P, NT]),
                u=sb("u" + n, [P, NT]), m=sb("m" + n, [P, NT]), q=sb("q" + n, [P, NT]),
                c=sb("c" + n, [P, NT, 1]), r1=sb("r1" + n, [P, NT, 1]), r2=sb("r2" + n, [P, NT, 1]),
                sp=sb("sp" + n, [P, NT, P], BF16), crow=sb("crow" + n, [P, N], BF16),
                w=sb("w" + n, [P, NT, N]), rz=sb("rz" + n, [P, NT]),
            )
            att[g]["p"] = att[g]["w"]
        paB = sb("paB", [P, NT, N])
        psumB = sb("psumB", [P, 3, N])
        nB = sb("nB", [P, NT, P])
        ngB = sb("ngB", [P, NT, P])
        rrB = sb("rrB", [P, NT])
        tvB = sb("tvB", [P, NT])
        scB = sb("scB", [P, NT])
        znC = sb("znC", [P, NT, P])
        zgC = sb("zgC", [P, NT, P])
        hbC = sb("hbC", [P, NT, P])
        qC = sb("qC", [P, NT, P])
        h1D = sb("h1D", [P, NT, P])
        xbD = sb("xbD", [P, NT, P])
        euE = sb("euE", [P, NT, P])
        ruE = sb("ruE", [P, NT, P])
        y1E = sb("y1E", [P, NT, P])
        xmE = sb("xmE", [P, NT, P])
        ln = {k: dict(y=sb("y_" + k, [P, NT, P]) if k != "B" else None, st=sb("lnst_" + k, [P, NT, 6]), mv=sb("lnmv_" + k, [P, NT, 2]),
                      ve=sb("lnve_" + k, [P, NT]), r=sb("lnr_" + k, [P, NT]), nb=sb("lnnb_" + k, [P, NT]))
              for k in ("A", "B", "Z", "C", "D", "E")}

        zC = ln["Z"]["y"]
        psT = bank("psT")
        psS = bank("psS", 2)
        psG = bank("psG", 2)
        psF = bank("psF")
        psR = bank("psR")
        psM = bank("psM")
        psTb = psT[:, 0, :].bitcast(BF16)
        mA0, mA1, mA2, mB, mZ, mE = (psM[:, 0, 8 * k:8 * k + 8] for k in range(6))

        def tiles(ap):
            return ap.rearrange("p (t d) -> p t d", t=NT)

        def pair(ap):
            return ap.rearrange("p (t d) -> p t d", d=2)

        mask = vA
        cnt = idx = pA
        upper = dia = att[B]["w"]
        upper1 = vals = att[E]["w"]
        eye = paB
        tmp = att2_j
        sel_k = psumB[:, 0:EC]
        sel_i = sb("sel_i", [P, NT, EDGES])
        q_k = sb("q_k", [P, EC, N])
        tot = sb("tot", [P, NT])
        totb = sb("totb", [P, NT, P])
        off = sb("off", [P, NT])
        nxt = sb("nxt", [P, NT])
        kf_i = sb("kf_i", [P, EDGES], I32)
        kf = sb("kf", [P, EDGES])
        kc_i = sb("kc_i", [P, EC], I32)
        kc = sb("kc", [P, EC])
        ecol = sb("ecol", [P, EC])
        elast = sb("elast", [P, 1])
        rowm = sb("rowm", [P, NT])
        rowz = sb("rowz", [P, NT])
        rowr = sb("rowr", [P, NT])
        eps1 = sb("eps1", [P, 1])
        wT = sb("wT", [P, 2, P])
        arep = gin_j[:].rearrange("p t j -> p (t j)")[:, 0:5 * P].rearrange("p (k d) -> p k d", k=5)

        x_v = x.rearrange("b (t p) d -> b p t d", p=P)
        out_v = out.rearrange("b (t p) d -> b p t d", p=P)

        N_LOADS = 23 + EC
        mm, v, a = nc.tensor.matmul, nc.vector, nc.scalar

        def column(v):
            return v.rearrange("(p a) -> p a", a=1)

        def on_all(v):
            return v.rearrange("(a d) -> a d", a=1).partition_broadcast(P)

        with ExitStack() as setup_ctx:
            s = Signals()
            block = setup_ctx.enter_context(nc.Block())

            @block.sync
            def _(sp):
                sp.dma_start(adj_i[:], adj.rearrange("(t p) j -> p t j", p=P)).then_inc(s["adj_in"], 16)
                loads = [
                    (a01[:, 0:1], l0_a[0:P, :]), (a01[:, 1:2], l0_a[P:2 * P, :]),
                    (wp_sb[:], wp), (w1_sb[:], w1), (w2_sb[:], w2), (l2w0[:], l2_w[0]), (l2w1[:], l2_w[1]),
                    (w3_sb[:], l3_w), (avec[:, 0:1], column(a_src)), (avec[:, 1:2], column(a_dst)),
                    (avec[:, 2:3], l3_src), (avec[:, 3:4], l3_dst), (avec[:, 4:5], column(bp)),
                    (bp_row[:, 0, :], on_all(bp)), (gg_row[:, 0, :], on_all(gat_g)), (gb_row[:, 0, :], on_all(gat_b)),
                    (b1_row[:, 0, :], on_all(b1)), (mg_row[:, 0, :], on_all(mlp_g)), (mb_row[:, 0, :], on_all(mlp_b)),
                    (b2_row[:, 0, :], on_all(b2)), (l2b_row[:, 0, :], on_all(l2_bias)), (eps_c[:], on_all(eps)),
                    (elast[:], l2_e[0:1, EDGES - 1:EDGES].partition_broadcast(P)),
                ] + [(ecol[:, c:c + 1], column(l2_e[0, c * P:(c + 1) * P])) for c in range(EC)]
                assert len(loads) == N_LOADS
                for dst, src in loads:
                    sp.dma_start(dst, src).then_inc(s["weights_in"], 16)

            @block.gpsimd
            def _(pool):
                pool.memset(ident[:], 0.0).then_inc(s["ident0"], 1)
                pool.memset(identb[:], 0.0).then_inc(s["ident0"], 1)
                pool.memset(ones[:], 1.0).then_inc(s["ones_set"], 1)
                pool.memset(onesb[:], 1.0).then_inc(s["ones_set"], 1)
                for k, value in enumerate((-0.5, 0.5, LN_EPS, -1.0)):
                    pool.memset(consts[:, k:k + 1], value).then_inc(s["consts_set"], 1)
                pool.memset(upper[:], 1.0).then_inc(s["upper0"], 1)
                pool.memset(upper1[:], 1.0).then_inc(s["upper0"], 1)
                pool.memset(eye[:], 0.0).then_inc(s["upper0"], 1)
                pool.iota(kf_i[:], pattern=[[1, EDGES]], base=0, channel_multiplier=0).then_inc(s["iota_set"], 1)
                pool.iota(kc_i[:], pattern=[[P, EC]], base=0, channel_multiplier=1).then_inc(s["iota_set"], 1)
                pool.memset(spA[:], 0.0).then_inc(s["sp0"], 1)
                pool.memset(att[B]["sp"][:], 0.0).then_inc(s["sp0"], 1)
                pool.memset(att[E]["sp"][:], 0.0).then_inc(s["sp0"], 1)
                pool.wait_ge(s["ident0"], 2)
                for m in (ident, identb):
                    pool.affine_select(out=m[:], in_=m[:], compare_op=ALU.not_equal, fill=1.0, base=0,
                                       pattern=[[-1, P]], channel_multiplier=1).then_inc(s["ident_set"], 1)
                pool.wait_ge(s["upper0"], 3)
                above = dict(base=0, pattern=[[-P, NT], [1, N]], channel_multiplier=-1)
                pool.affine_select(out=upper[:], in_=upper[:], compare_op=ALU.is_gt, fill=0.0,
                                   **above).then_inc(s["upper_set"], 1)
                pool.affine_select(out=upper1[:], in_=upper1[:], compare_op=ALU.is_ge, fill=0.0,
                                   **above).then_inc(s["upper_set"], 1)
                pool.affine_select(out=eye[:], in_=eye[:], compare_op=ALU.not_equal, fill=1.0,
                                   **above).then_inc(s["eye_set"], 1)
                pool.wait_ge(s["sp0"], 3)
                pool.memset(spA[:, 0, :, 3:6], 1.0).then_inc(s["sp_ones"], 1)
                pool.memset(spA[:, 1, :, 0:3], 1.0).then_inc(s["sp_ones"], 1)
                pool.memset(att[E]["h"][:, :, P:P + 2], 1.0).then_inc(s["sp_ones"], 1)
                pool.wait_ge(s["weights_in"], 16 * N_LOADS)

            @block.tensor
            def _(pe):
                pe.wait_ge(s["ident_set"], 2)
                pe.wait_ge(s["ones_set"], 2)
                pe.wait_ge(s["sp_ones"], 3)
                pe.wait_ge(s["weights_in"], 16 * N_LOADS)
                nc.tensor.transpose(psM[:, 0, 0:P], wp_sb[:], ident[:])
                nc.tensor.transpose(psM[:, 0, P:2 * P], w3_sb[:], ident[:]).then_inc(s["wT_in_psum"], 1)
                pe.wait_ge(s["wT_ready"], 1)
                pe.wait_ge(s["arep_ready"], 1)
                for k in range(4):
                    mm(psF[:, 0, k * P:(k + 1) * P], wT[:, k // 2, :], arep[:, k, :], start=True, stop=True)
                mm(psM[:, 0, 256:258], arep[:, 4, :], avec[:, 0:2], start=True, stop=True).then_inc(s["wa_in_psum"], 1)
                pe.wait_ge(s["adj_in"], 16)
                for j in range(NT):
                    dst = psS[:, j % 2]
                    if j >= 2:
                        pe.wait_ge(s["adjT_copied"], j - 1)
                    for i in range(NT):
                        last = nc.tensor.transpose(dst[:, i * P:(i + 1) * P], adj_i[:, i, j * P:(j + 1) * P], ident[:])
                    last.then_inc(s["adjT_in_psum"], 1)
                pe.wait_ge(s["tot_ready"], 1)
                pe.wait_ge(s["upper_set"], 2)
                for n, u in enumerate((upper, upper1)):
                    for i in range(NT):
                        last = mm(psG[:, n], totb[:, i], u[:, i], start=(i == 0), stop=(i == NT - 1))
                last.then_inc(s["off_rows"], 1)
                for c in range(NT):
                    for i in range(NT):
                        last = mm(psR[:, 0, c:c + 1], upper[:, i, c * P:(c + 1) * P], tot[:, i:i + 1],
                                  start=(i == 0), stop=(i == NT - 1))
                last.then_inc(s["off_cols"], 1)
                pe.wait_ge(s["sel_ready"], 1)
                pe.wait_ge(s["adjT_copied"], NT)
                for c in range(EC):
                    for i in range(NT):
                        last = mm(psS[:, c], sel_i[:, i, c * P:(c + 1) * P], idx[:, i], start=(i == 0), stop=(i == NT - 1))
                last.then_inc(s["erow_in_psum"], 1)
                pe.wait_ge(s["q_ready"], 1)
                for i in range(NT):
                    if i >= 2:
                        pe.wait_ge(s["vals_taken"], i - 1)
                    for c in range(EC):
                        last = mm(psG[:, i % 2], sel_k[:, c, i * P:(i + 1) * P], q_k[:, c], start=(c == 0),
                                  stop=(c == EC - 1))
                    last.then_inc(s["vals_in_psum"], 1)
                pe.wait_ge(s["dia_ready"], 1)
                for i in range(NT):
                    last = mm(psR[:, 0], ones[:], dia[:, i], start=(i == 0), stop=(i == NT - 1))
                last.then_inc(s["diag_in_psum"], 1)
                for j in range(NT):
                    if j >= 2:
                        pe.wait_ge(s["att2T_copied"], j - 1)
                    for i in range(NT):
                        last = nc.tensor.transpose(psS[:, j % 2, i * P:(i + 1) * P], vals[:, i, j * P:(j + 1) * P], ident[:])
                    last.then_inc(s["att2T_in_psum"], 1)

            @block.vector
            def _(dve):

                def then(ins, name):
                    ins.then_inc(s[name], 1)
                    then.n[name] = then.n.get(name, 0) + 1
                    dve.wait_ge(s[name], then.n[name])
                then.n = {}

                dve.wait_ge(s["weights_in"], 16 * N_LOADS)
                for k in range(5):
                    last = v.tensor_copy(arep[:, k, :], avec[:, k:k + 1].to_broadcast([P, P]))
                last.then_inc(s["arep_ready"], 1)
                dve.wait_ge(s["wT_in_psum"], 1)
                v.tensor_copy(wT[:].rearrange("p a b -> p (a b)"), psM[:, 0, 0:2 * P]).then_inc(s["wT_ready"], 1)
                dve.wait_ge(s["adj_in"], 16)
                then(v.tensor_scalar(mask[:], adj_i[:], 0.0, None, ALU.is_gt), "mask_set")
                v.tensor_reduce(tot[:], mask[:], axis=AX_X, op=ALU.add).then_inc(s["tot0"], 1)
                dve.wait_ge(s["ones_set"], 2)
                dve.wait_ge(s["upper0"], 3)
                v.memset(tmp[:, 0], 1.0).then_inc(s["tmp_ones"], 1)
                dve.wait_ge(s["tot0"], 1)
                dve.wait_ge(s["tmp_ones"], 1)
                v.tensor_copy(totb[:], tot[:].unsqueeze(2).to_broadcast([P, NT, P])).then_inc(s["tot_ready"], 1)
                for i in range(NT):
                    last = v.tensor_tensor_scan(cnt[:, i], tmp[:, 0], mask[:, i], 0.0, ALU.mult, ALU.add)
                last.then_inc(s["cnt_ready"], 1)
                dve.wait_ge(s["wa_in_psum"], 1)
                for k, (rep, two) in enumerate(((ws1, st1), (wt1, st1), (ws3, st3), (wt3, st3))):
                    v.tensor_copy(rep[:], psF[:, 0, k * P:(k + 1) * P])
                    v.tensor_copy(two[:, k % 2:k % 2 + 1], psF[:, 0, k * P:k * P + 1])
                v.tensor_copy(bst[:, 0, :], psM[:, 0, 256:258]).then_inc(s["setup_done"], 1)
                for j in range(NT):
                    dve.wait_ge(s["adjT_in_psum"], j + 1)
                    v.tensor_copy(adj_j[:, j], psS[:, j % 2]).then_inc(s["adjT_copied"], 1)
                v.tensor_scalar(no1_i[:], adj_i[:], 0.0, -BIG, ALU.is_le, ALU.mult)
                dve.wait_ge(s["adjT_copied"], NT)
                v.tensor_scalar(no1_j[:], adj_j[:], 0.0, -BIG, ALU.is_le, ALU.mult)
                then(v.tensor_scalar(eps1[:], eps_c[:], 1.0, None, ALU.add), "eps_ready")
                dve.wait_ge(s["eye_set"], 1)
                v.scalar_tensor_tensor(gin_j[:], eye[:], eps1[:], adj_j[:], ALU.mult, ALU.add)
                dve.wait_ge(s["cnt_ready"], 1)
                for a, no in ((adj_i, no3_i), (adj_j, no3_j)):
                    then(v.tensor_tensor(tmp[:], a[:], eye[:], ALU.add), "loops")
                    then(v.tensor_scalar(tmp[:], tmp[:], 0.0, None, ALU.max), "loops")
                    then(v.tensor_scalar(no[:], tmp[:], 0.0, -BIG, ALU.is_equal, ALU.mult), "loops")
                dve.wait_ge(s["off_cols"], 1)
                then(v.tensor_copy(off[:], psR[:, 0, 0:NT]), "off_ready")
                then(v.tensor_tensor(nxt[:], off[:], tot[:], ALU.add), "off_ready")
                for i in range(NT):
                    last = v.scalar_tensor_tensor(idx[:, i], cnt[:, i], off[:, i:i + 1], mask[:, i], ALU.add, ALU.mult)
                then(last, "idx_ready")
                then(v.tensor_scalar(idx[:], idx[:], -1.0, None, ALU.add), "idx_ready")
                dve.wait_ge(s["iota_set"], 2)
                v.tensor_copy(kf[:], kf_i[:])
                then(v.tensor_copy(kc[:], kc_i[:]), "k_ready")
                for i in range(NT):
                    then(v.tensor_scalar(tmp[:, i, 0:EDGES], kf[:], off[:, i:i + 1], None, ALU.is_ge), "sel0")
                    last = v.scalar_tensor_tensor(sel_i[:, i], kf[:], nxt[:, i:i + 1], tmp[:, i, 0:EDGES], ALU.is_lt, ALU.mult)
                last.then_inc(s["sel_ready"], 1)
                dve.wait_ge(s["sel_ready"], 1)
                dve.wait_ge(s["off_rows"], 1)
                for c in range(EC):
                    then(v.tensor_scalar(tmp[:, c], psG[:, 0], kc[:, c:c + 1], None, ALU.is_le), "sel0")
                    then(v.scalar_tensor_tensor(sel_k[:, c], psG[:, 1], kc[:, c:c + 1], tmp[:, c], ALU.is_gt, ALU.mult), "sel0")
                dve.wait_ge(s["erow_in_psum"], 1)
                for c in range(EC):
                    last = v.tensor_scalar(q_k[:, c], psS[:, c], kc[:, c:c + 1], ecol[:, c:c + 1], ALU.is_equal, ALU.mult)
                last.then_inc(s["q_ready"], 1)
                then(v.tensor_scalar(tmp[:], idx[:], float(EDGES), elast[:], ALU.is_ge, ALU.mult), "past")
                dve.wait_ge(s["sel_ready"], 1)
                then(v.tensor_scalar(mask[:], mask[:], -1.0, -NEG, ALU.add, ALU.mult), "past")
                then(v.tensor_tensor(tmp[:], tmp[:], mask[:], ALU.add), "past")
                for i in range(NT):
                    dve.wait_ge(s["vals_in_psum"], i + 1)
                    v.tensor_tensor(vals[:, i], psG[:, i % 2], tmp[:, i], ALU.add).then_inc(s["vals_taken"], 1)
                dve.wait_ge(s["vals_taken"], NT)
                then(v.tensor_reduce(rowm[:], vals[:], axis=AX_X, op=ALU.max, negate=True), "rowm_ready")
                dve.wait_ge(s["exp2_ready"], 1)
                then(v.reciprocal(rowr[:], rowz[:]), "rowr_ready")
                for i in range(NT):
                    then(v.tensor_scalar(vals[:, i], vals[:, i], rowr[:, i:i + 1], None, ALU.mult), "att2")
                then(v.tensor_tensor(dia[:], vals[:], eye[:], ALU.mult), "att2")
                v.tensor_tensor(vals[:], vals[:], dia[:], ALU.subtract).then_inc(s["dia_ready"], 1)
                dve.wait_ge(s["diag_in_psum"], 1)
                v.tensor_copy(diag2[:], psR[:, 0])
                for j in range(NT):
                    dve.wait_ge(s["att2T_in_psum"], j + 1)
                    last = v.tensor_copy(att2_j[:, j], psS[:, j % 2])
                    last.then_inc(s["att2T_copied"], 1)
                dve.wait_ge(s["att2T_copied"], NT)
                v.tensor_copy(rowm[:, 0:1], rowr[:, 0:1]).then_inc(s["setup_done"], 1)

            @block.scalar
            def _(act):

                act.wait_ge(s["rowm_ready"], 1)
                for i in range(NT):
                    last = a.activation(vals[:, i], vals[:, i], ACT.Exp, bias=rowm[:, i:i + 1], accum_out=rowz[:, i:i + 1])
                last.then_inc(s["exp2_ready"], 1)
                act.wait_ge(s["exp2_ready"], 1)

        nc.clear_and_free_semaphores(list(s.values()))
        nc.all_engine_barrier()
        s = Signals()
        block = ctx.enter_context(nc.Block())

        def turns(eng, body):
            for it in range(LAST_DELAY + 1):
                body(Turn(it, GRAPHS))
            with eng.Fori(LAST_DELAY + 1, GRAPHS) as it:
                body(Turn(it, GRAPHS))
            for it in range(GRAPHS, GRAPHS + LAST_DELAY):
                body(Turn(it, GRAPHS))

        SMALL = 9


        @block.sync
        def _(sp):
            def load_xA(g):
                sp.wait_ge(s["xA_transposed"], g.last)
                sp.wait_ge(s["xA_scaled"], g.last)
                sp.wait_ge(s["xhA_ready"], g.last)
                sp.dma_start(xA[:], x_v[g.g]).then_inc(s["xA_in"], 16)

            def store(g):
                sp.wait_ge(s["xout_ready"], g.now)
                sp.dma_start(out_v[g.g], xout[:]).then_inc(s["xout_stored"], 16)

            def turn(t):
                t.run(load_xA, 0)
                t.run(store, 5)

            turns(sp, turn)
            sp.wait_ge(s["xout_stored"], 16 * GRAPHS)

        @block.gpsimd
        def _(pool):
            def rstd(k, var=None):
                def step(g):
                    L = ln[k]
                    pool.wait_ge(s["stats_" + k], g.now)
                    pool.tensor_tensor(L["ve"][:], var if var is not None else L["mv"][:, :, 1],
                                       consts[:, 2:3].to_broadcast([P, NT]), ALU.add).then_inc(s["ve_" + k], 1)
                    pool.wait_ge(s["ve_" + k], g.now)
                    pool.wait_ge(s["nb_" + k], g.last)
                    if k != "B":
                        pool.wait_ge(s["applied_" + k], g.last)
                    pool.tensor_tensor(L["r"][:], L["ve"][:], consts[:, 0:1].to_broadcast([P, NT]),
                                       ALU.pow).then_inc(s["rstd_" + k], 1)
                return step

            rstd_A, rstd_Z, rstd_C, rstd_D, rstd_E = (rstd(k) for k in "AZCDE")
            rstd_B = rstd("B", var=tvB[:])

            def hb_C(g):
                pool.wait_ge(s["applied_B"], g.now)
                pool.wait_ge(s["qC_ready"], g.last)
                pool.tensor_tensor(hbC[:], hgat[:], b2_row[:].to_broadcast([P, NT, P]),
                                   ALU.add).then_inc(s["hbC_ready"], 1)

            def half_xA(g):
                pool.wait_ge(s["xTA_ready"], g.now)
                pool.wait_ge(s["y_A"], g.last)
                pool.tensor_tensor(xhA[:], xA[:], consts[:, 1:2].unsqueeze(2).to_broadcast([P, NT, P]),
                                   ALU.add).then_inc(s["xhA_ready"], 1)

            def bias_D(g):
                pool.wait_ge(s["applied_C"], g.now)
                pool.wait_ge(s["y_D"], g.last)
                pool.tensor_tensor(xbD[:], xD[:], l2b_row[:].to_broadcast([P, NT, P]),
                                   ALU.add).then_inc(s["xbD_ready"], 1)

            def diag_D(g):
                pool.wait_ge(s["xTD_ready"], g.now)
                pool.wait_ge(s["aggD_ready"], g.last)
                pool.tensor_tensor(xTdD[:], xTD[:], diag2[:], ALU.mult).then_inc(s["xTdD_ready"], 1)

            def minus1_E(g):
                pool.wait_ge(s["applied_D"], g.now)
                pool.wait_ge(s["y_E"], g.last)
                pool.tensor_tensor(xmE[:], xE[:], consts[:, 3:4].unsqueeze(2).to_broadcast([P, NT, P]),
                                   ALU.add).then_inc(s["xmE_ready"], 1)

            def power_A(g):
                pool.wait_ge(s["veA_ready"], g.now)
                pool.wait_ge(s["expA"], NT * g.last)
                pool.wait_ge(s["nmA_ready"], g.last)
                pool.tensor_tensor(irA[:], veA[:], consts[:, 1:2], ALU.pow).then_inc(s["irA_ready"], 1)
                pool.tensor_tensor(rA[:], veA[:], consts[:, 0:1], ALU.pow).then_inc(s["rA_ready"], 1)

            def gain_Z(g):
                pool.wait_ge(s["applied_Z"], g.now)
                pool.tensor_tensor(zgC[:], znC[:], mg_row[:].to_broadcast([P, NT, P]),
                                   ALU.mult).then_inc(s["zgC_ready"], 1)
                pool.wait_ge(s["zgC_ready"], g.now)
                pool.wait_ge(s["zT_in_psum"], g.last)
                pool.tensor_tensor(znC[:], zgC[:], mb_row[:].to_broadcast([P, NT, P]),
                                   ALU.add).then_inc(s["zbC_ready"], 1)

            def mult_B(j):
                def step(g):
                    pool.wait_ge(s["expB"], g.tile(j))
                    pool.wait_ge(s["aggB_ready"], g.last)
                    pool.tensor_tensor(paB[:, j], att[B]["p"][:, j], adj_j[:, j], ALU.mult).then_inc(s["paB"], 1)
                return step

            def add_B(j):
                def step(g):
                    p = att[B]["p"]
                    before = p[:, 0] if j == 1 else psumB[:, j - 2]
                    pool.wait_ge(s["expB"], g.tile(j))
                    if j > 1:
                        pool.wait_ge(s["psB"], g.tile(j - 2, NT - 1))
                    pool.wait_ge(s["zsumB_ready"], g.last)
                    pool.tensor_tensor(psumB[:, j - 1], before, p[:, j], ALU.add).then_inc(s["psB"], 1)
                return step

            mult_B0, mult_B1, mult_B2, mult_B3 = (mult_B(j) for j in range(NT))
            add_B1, add_B2, add_B3 = (add_B(j) for j in range(1, NT))

            def gain_B(g):
                pool.wait_ge(s["applied0_B"], g.now)
                pool.wait_ge(s["applied_B"], g.last)
                pool.tensor_tensor(ngB[:], nB[:], gg_row[:].to_broadcast([P, NT, P]),
                                   ALU.mult).then_inc(s["ngB_ready"], 1)
                pool.wait_ge(s["ngB_ready"], g.now)
                pool.tensor_tensor(nB[:], ngB[:], gb_row[:].to_broadcast([P, NT, P]),
                                   ALU.add).then_inc(s["nbB_ready"], 1)

            def turn(t):
                t.run(rstd_Z, 3)
                t.run(gain_Z, 3)
                t.run(mult_B0, 2)
                t.run(rstd_A, 1)
                t.run(mult_B1, 2)
                t.run(add_B1, 2)
                t.run(rstd_C, 3)
                t.run(diag_D, 3)
                t.run(mult_B2, 2)
                t.run(power_A, 0)
                t.run(bias_D, 3)
                t.run(mult_B3, 2)
                t.run(add_B2, 2)
                t.run(add_B3, 2)
                t.run(rstd_D, 3)
                t.run(half_xA, 0)
                t.run(rstd_B, 2)
                t.run(rstd_E, 4)
                t.run(minus1_E, 3)
                t.run(gain_B, 2)
                t.run(hb_C, 2)

            turns(pool, turn)

        @block.tensor
        def _(pe):
            IN_T = [
                ("crowE", 4, 0, 1), ("xTA_ready", 0, 0, 1), ("zT_ready", 3, 0, 1), ("xTD_ready", 3, 0, 1),
                ("xTB_ready", 1, 0, 1), ("rowsA_ready", 0, 0, 1), ("xTE_ready", 3, 0, 1), ("crowB", 1, 0, 1),
                ("sB_ready", 1, 0, 1), ("sE_ready", 3, 0, 1),
            ]
            IN_F = [
                ("hE_ready", 4, 0, 1), ("qC_ready", 3, 0, 1), ("hB_ready", 2, 0, 1), ("h1D_ready", 3, 0, 1),
                ("ginT_ready", 2, 0, 1), ("y_Z", 2, 0, 1),
            ]
            IN_M = [
                ("stA_ready", 0, 0, 1), ("meanA", 0, 0, 1), ("varA", 0, 0, 1), ("stB_taken", 1, 0, 1),
                ("rzB_ready", 2, 0, 1), ("stE_taken", 3, 0, 1),
            ]
            IN_R = [
                ("maxB_ready", 1, 0, 1), ("maxE_ready", 3, 0, 1),
            ]
            IN_S0 = [
                ("wB", 2, 0, 4), ("wE", 4, 0, 4), ("wE", 4, 2, 4), ("wB", 2, 2, 4), ("vA", 0, 0, 4),
                ("vA", 0, 2, 4),
            ]
            IN_S1 = [
                ("wB", 2, 1, 4), ("wE", 4, 1, 4), ("wE", 4, 3, 4), ("wB", 2, 3, 4), ("vA", 0, 1, 4),
                ("vA", 0, 3, 4),
            ]
            IN_G0 = [
                ("thA_ready", 1, 0, 1), ("euE_ready", 4, 0, 1), ("y_D", 3, 0, 1),
            ]
            IN_G1 = [
                ("euE_ready", 4, 0, 1), ("applied0_B", 2, 0, 1),
            ]

            def bank_free(g, readers, mine, tile=0):
                at = next(i for i, r in enumerate(readers) if r[0] == mine and r[2] == tile)
                for back in range(1, len(readers) + 1):
                    name, delay, k, per = readers[at - back]
                    reader = g.turn.graph(delay + (back > at))
                    if reader.real:
                        pe.wait_ge(s[name], reader.tile(k, per))
                        return

            def transpose(src):
                for i in range(NT):
                    last = nc.tensor.transpose(psT[:, 0, i * P:(i + 1) * P], src[:, i], ident[:])
                return last

            def features(src, w):
                for i in range(NT):
                    last = mm(psF[:, 0, i * P:(i + 1) * P], src[:, i * P:(i + 1) * P], w, start=True, stop=True)
                return last

            def columns(dst, src, w):
                for i in range(NT):
                    last = mm(dst[:, 2 * i:2 * i + 2], src[:, i * P:(i + 1) * P], w, start=True, stop=True)
                return last

            def transpose_xA(g):
                pe.wait_ge(s["xA_in"], 16 * g.now)
                bank_free(g, IN_T, "xTA_ready")
                transpose(xA).then_inc(s["xA_transposed"], 1)

            def columns_A(g):
                pe.wait_ge(s["xTA_ready"], g.now)
                bank_free(g, IN_M, "stA_ready")
                columns(mA0, xTA, a01[:]).then_inc(s["stA_in_psum"], 1)

            def sum_A(g):
                pe.wait_ge(s["stA_ready"], g.now)
                bank_free(g, IN_M, "meanA")
                mm(mA1, ones[:], stA[:].rearrange("p t c -> p (t c)"), start=True, stop=True).then_inc(
                    s["sumA_in_psum"], 1)

            def squares_A(g):
                pe.wait_ge(s["sqA_ready"], g.now)
                bank_free(g, IN_M, "varA")
                mm(mA2, ones[:], sqA[:].rearrange("p t c -> p (t c)"), start=True, stop=True).then_inc(
                    s["sqA_in_psum"], 1)

            def rows_A(g):
                pe.wait_ge(s["spA"], g.now)
                bank_free(g, IN_T, "rowsA_ready")
                for i in range(2 * NT):
                    last = nc.tensor.transpose(psTb[:, i * P:(i + 1) * P], spA[:, i // NT, i % NT], identb[:])
                last.then_inc(s["rows_in_psum_A"], 1)

            def pair_A(j):
                def step(g):
                    pe.wait_ge(s["rowsA_ready"], g.now)
                    bank_free(g, (IN_S0, IN_S1)[j % 2], "vA", j)
                    mm(psS[:, j % 2], rowsA[:, N + j * P:N + (j + 1) * P], rowsA[:, 0:N], start=True,
                       stop=True).then_inc(s[f"eA{j}"], 1)
                return step

            pair_A0, pair_A1, pair_A2, pair_A3 = (pair_A(j) for j in range(NT))

            def agg_A(g):
                pe.wait_ge(s["xA_scaled"], g.now)
                bank_free(g, IN_G0, "thA_ready")
                for i in range(NT):
                    for j in range(NT):
                        last = mm(psG[:, 0, i * P:(i + 1) * P], pA[:, j, i * P:(i + 1) * P], xsA[:, j],
                                  start=(j == 0), stop=(j == NT - 1))
                last.then_inc(s["aggA_ready"], 1)

            def transpose_xB(g):
                pe.wait_ge(s["applied_A"], g.now)
                bank_free(g, IN_T, "xTB_ready")
                transpose(xB).then_inc(s["xB_transposed"], 1)

            def transpose_xE(g):
                pe.wait_ge(s["applied_D"], g.now)
                bank_free(g, IN_T, "xTE_ready")
                transpose(xE).then_inc(s["xE_transposed"], 1)

            def project(n, xT, ws, wt, st, w, mcols):
                def s_row(g):
                    pe.wait_ge(s[f"xT{n}_ready"], g.now)
                    bank_free(g, IN_T, f"s{n}_ready")
                    mm(psT[:, 0], ws[:], xT[:], start=True, stop=True).then_inc(s[f"s{n}_in_psum"], 1)

                def cols(g):
                    pe.wait_ge(s[f"xT{n}_ready"], g.now)
                    bank_free(g, IN_M, f"st{n}_taken")
                    columns(mcols, xT, st[:]).then_inc(s[f"st{n}_in_psum"], 1)

                def t_row(g):
                    pe.wait_ge(s[f"xT{n}_ready"], g.now)
                    bank_free(g, IN_R, f"max{n}_ready")
                    mm(psR[:, 0], wt[:], xT[:], start=True, stop=True).then_inc(s[f"t{n}_in_psum"], 1)

                def feats(g):
                    pe.wait_ge(s[f"xT{n}_ready"], g.now)
                    bank_free(g, IN_F, f"h{n}_ready")
                    features(xT, w[:]).then_inc(s[f"h{n}_in_psum"], 1)

                def c_row(g):
                    pe.wait_ge(s["sp" + n], g.now)
                    bank_free(g, IN_T, "crow" + n)
                    for i in range(NT):
                        last = nc.tensor.transpose(psTb[:, i * P:(i + 1) * P], att[B if n == "B" else E]["sp"][:, i],
                                                   identb[:])
                    last.then_inc(s["rows_in_psum_" + n], 1)
                return s_row, cols, t_row, feats, c_row

            s_B, columns_B, t_B, h_B, rows_B = project("B", xTB, ws1, wt1, st1, wp_sb, mB)
            s_E, columns_E, t_E, h_E, rows_E = project("E", xTE, ws3, wt3, st3, w3_sb, mE)

            def scores(n, b, no_edge, j):
                def step(g):
                    pe.wait_ge(s["crow" + n], g.now)
                    bank_free(g, (IN_S0, IN_S1)[j % 2], "w" + n, j)
                    mm(psS[:, j % 2], identb[:], no_edge[:, j], start=True, stop=False)
                    mm(psS[:, j % 2], onesb[:], b["crow"][:], start=False, stop=True).then_inc(s["cmask" + n], 1)
                return step

            scores_B0, scores_B1, scores_B2, scores_B3 = (scores("B", att[B], no1_j, j) for j in range(NT))
            scores_E0, scores_E1, scores_E2, scores_E3 = (scores("E", att[E], no3_j, j) for j in range(NT))

            def agg_B(j):
                def step(g):
                    if j == 0:
                        pe.wait_ge(s["hB_ready"], g.now)
                        bank_free(g, IN_G1, "applied0_B")
                    pe.wait_ge(s["paB"], g.tile(j))
                    for i in range(NT):
                        last = mm(psG[:, 1, i * P:(i + 1) * P], paB[:, j, i * P:(i + 1) * P],
                                  att[B]["h"][:, j, 0:P], start=(j == 0 and i == 0), stop=(j == NT - 1),
                                  skip_group_check=True)
                    if j == NT - 1:
                        last.then_inc(s["aggB_ready"], 1)
                return step

            agg_B0, agg_B1, agg_B2, agg_B3 = (agg_B(j) for j in range(NT))

            def zsum_B(g):
                pe.wait_ge(s["psB"], (NT - 1) * g.now)
                bank_free(g, IN_M, "rzB_ready")
                for i in range(NT):
                    last = mm(mZ[:, i:i + 1], psumB[:, 2, i * P:(i + 1) * P], ones[:, 0:1], start=True, stop=True)
                last.then_inc(s["zsumB_ready"], 1)

            def agg_E(j):
                def step(g):
                    if j == 0:
                        pe.wait_ge(s["hE_ready"], g.now)
                        bank_free(g, IN_G0, "euE_ready")
                        bank_free(g, IN_G1, "euE_ready")
                    pe.wait_ge(s["expE"], g.tile(j))
                    for i in range(NT):
                        k = (i % 2) * (P + 2)
                        last = mm(psG[:, i // 2, k:k + P + 2], att[E]["p"][:, j, i * P:(i + 1) * P],
                                  att[E]["h"][:, j], start=(j == 0 and i % 2 == 0), stop=(j == NT - 1),
                                  skip_group_check=True)
                    if j == NT - 1:
                        last.then_inc(s["aggE_ready"], 1)
                return step

            agg_E0, agg_E1, agg_E2, agg_E3 = (agg_E(j) for j in range(NT))

            def gin(g):
                pe.wait_ge(s["applied_B"], g.now)
                bank_free(g, IN_F, "ginT_ready")
                for j in range(NT):
                    last = mm(psF[:, 0], hgat[:, j], gin_j[:, j], start=(j == 0), stop=(j == NT - 1))
                last.then_inc(s["ginT_in_psum"], 1)

            def z_C(g):
                pe.wait_ge(s["ginT_ready"], g.now)
                bank_free(g, IN_F, "y_Z")
                features(ginT, w1_sb[:]).then_inc(s["z_in_psum"], 1)

            def zT_C(g):
                pe.wait_ge(s["zbC_ready"], g.now)
                bank_free(g, IN_T, "zT_ready")
                transpose(znC).then_inc(s["zT_in_psum"], 1)

            def x2_C(g):
                pe.wait_ge(s["zT_ready"], g.now)
                bank_free(g, IN_F, "qC_ready")
                features(zT, w2_sb[:]).then_inc(s["x2C_in_psum"], 1)

            def transpose_xD(g):
                pe.wait_ge(s["applied_C"], g.now)
                bank_free(g, IN_T, "xTD_ready")
                transpose(xD).then_inc(s["xD_transposed"], 1)

            def h_D(g):
                pe.wait_ge(s["xTD_ready"], g.now)
                bank_free(g, IN_F, "h1D_ready")
                features(xTD, l2w1[:]).then_inc(s["h1D_in_psum"], 1)

            def agg_D(g):
                pe.wait_ge(s["h1D_ready"], g.now)
                pe.wait_ge(s["xTdD_ready"], g.now)
                bank_free(g, IN_G0, "y_D")
                for i in range(NT):
                    dst = psG[:, 0, i * P:(i + 1) * P]
                    for j in range(NT):
                        mm(dst, att2_j[:, j, i * P:(i + 1) * P], h1D[:, j], start=(j == 0), stop=False)
                    last = mm(dst, xTdD[:, i * P:(i + 1) * P], l2w0[:], start=False, stop=True)
                last.then_inc(s["aggD_ready"], 1)

            def turn(t):
                t.run(rows_E, 4)
                t.run(scores_B0, 2)
                t.run(agg_A, 1)
                t.run(scores_B1, 2)
                t.run(scores_E0, 4)
                t.run(transpose_xA, 0)
                t.run(h_E, 4)
                t.run(scores_E1, 4)
                t.run(scores_E2, 4)
                t.run(zT_C, 3)
                t.run(x2_C, 3)
                t.run(agg_E0, 4)
                t.run(agg_E1, 4)
                t.run(scores_E3, 4)
                t.run(scores_B2, 2)
                t.run(agg_E2, 4)
                t.run(scores_B3, 2)
                t.run(agg_E3, 4)
                t.run(h_B, 2)
                t.run(transpose_xD, 3)
                t.run(h_D, 3)
                t.run(columns_A, 0)
                t.run(sum_A, 0)
                t.run(squares_A, 0)
                t.run(agg_D, 3)
                t.run(transpose_xB, 1)
                t.run(agg_B0, 2)
                t.run(t_B, 1)
                t.run(columns_B, 1)
                t.run(agg_B1, 2)
                t.run(agg_B2, 2)
                t.run(rows_A, 0)
                t.run(agg_B3, 2)
                t.run(zsum_B, 2)
                t.run(pair_A0, 0)
                t.run(pair_A1, 0)
                t.run(transpose_xE, 3)
                t.run(pair_A2, 0)
                t.run(columns_E, 3)
                t.run(t_E, 3)
                t.run(rows_B, 1)
                t.run(pair_A3, 0)
                t.run(s_B, 1)
                t.run(gin, 2)
                t.run(s_E, 3)
                t.run(z_C, 2)

            turns(pe, turn)

        @block.vector
        def _(dve):
            def stats(g, k, src):
                L = ln[k]
                dve.wait_ge(s["y_" + k], g.now)
                for i in range(NT):
                    last = v.bn_stats(L["st"][:, i], src[:, i])
                last.then_inc(s["bn_" + k], 1)
                dve.wait_ge(s["bn_" + k], 1)
                dve.wait_ge(s["bn_" + k], g.now)
                dve.wait_ge(s["ve_" + k], g.last)
                for i in range(NT):
                    last = v.bn_aggr(L["mv"][:, i], L["st"][:, i])
                last.then_inc(s["stats_" + k], 1)

            def neg_mean(g, k, rstd):
                L = ln[k]
                dve.wait_ge(s["applied0_B" if k == "B" else "applied_" + k], g.last)
                v.scalar_tensor_tensor(L["nb"][:], L["mv"][:, :, 0], -1.0, rstd, ALU.mult,
                                       ALU.mult).then_inc(s["nb_" + k], 1)

            def neg_mean_of(k):
                def step(g):
                    dve.wait_ge(s["rstd_" + k], g.now)
                    neg_mean(g, k, ln[k]["r"][:])
                return step

            nb_A, nb_Z, nb_C, nb_D, nb_E = (neg_mean_of(k) for k in "AZCDE")

            def row_max(n, b, no_edge, src):
                small = s["small_" + n]

                def cols(g):
                    dve.wait_ge(s[f"st{n}_in_psum"], g.now)
                    dve.wait_ge(s["exp" + n], NT * g.last)
                    if n == "B":
                        v.tensor_tensor(b["st"][:], src, bst[:].to_broadcast([P, NT, 2]), ALU.add).then_inc(
                            s["stB_taken"], 1)
                    else:
                        v.tensor_copy(b["st"][:], src).then_inc(s["stE_taken"], 1)

                def maxima(g):
                    dve.wait_ge(s[f"st{n}_taken"], g.now)
                    dve.wait_ge(s[f"t{n}_in_psum"], g.now)
                    if n == "B":
                        dve.wait_ge(s["paB"], NT * g.last)
                        dve.wait_ge(s["psB"], (NT - 1) * g.last)
                    else:
                        dve.wait_ge(s["aggE_ready"], g.last)
                    v.tensor_scalar(b["nt"][:], b["st"][:, :, 1], -1.0, None, ALU.mult).then_inc(small, 1)
                    v.tensor_scalar(b["q"][:], b["st"][:, :, 0], 0.25, None, ALU.mult).then_inc(small, 1)
                    for i in range(NT):
                        last = v.tensor_tensor_reduce(out=b["w"][:, i], in0=psR[:, 0], in1=no_edge[:, i], scale=1.0,
                                                      scalar=-3e38, op0=ALU.add, op1=ALU.max,
                                                      accum_out=b["mx"][:, i:i + 1])
                    last.then_inc(s[f"max{n}_ready"], 1)

                def split(g):
                    dve.wait_ge(s[f"max{n}_ready"], g.now)
                    if n == "B":
                        v.scalar_tensor_tensor(b["u"][:], b["mx"][:], bst[:, 0, 1:2], b["st"][:, :, 0], ALU.add,
                                               ALU.add).then_inc(small, 1)
                    else:
                        v.tensor_tensor(b["u"][:], b["mx"][:], b["st"][:, :, 0], ALU.add).then_inc(small, 1)
                    dve.wait_ge(small, g.tile(2, SMALL))
                    v.scalar_tensor_tensor(b["m"][:], b["u"][:], SLOPE, b["u"][:], ALU.mult, ALU.max).then_inc(small, 1)
                    dve.wait_ge(small, g.tile(3, SMALL))
                    v.scalar_tensor_tensor(b["c"][:, :, 0], b["m"][:], -1.25, b["q"][:], ALU.mult,
                                           ALU.add).then_inc(small, 1)
                    dve.wait_ge(s["rows_in_psum_" + n], g.last)
                    parts = [b["sp"][:, :, k:k + 1] for k in range(3)]
                    dve.wait_ge(small, g.tile(4, SMALL))
                    v.tensor_copy(parts[0], b["c"][:]).then_inc(small, 1)
                    dve.wait_ge(small, g.tile(5, SMALL))
                    v.tensor_tensor(b["r1"][:], b["c"][:], parts[0], ALU.subtract).then_inc(small, 1)
                    dve.wait_ge(small, g.tile(6, SMALL))
                    v.tensor_copy(parts[1], b["r1"][:]).then_inc(small, 1)
                    dve.wait_ge(small, g.tile(7, SMALL))
                    v.tensor_tensor(b["r2"][:], b["r1"][:], parts[1], ALU.subtract).then_inc(small, 1)
                    dve.wait_ge(small, g.tile(8, SMALL))
                    v.tensor_copy(parts[2], b["r2"][:]).then_inc(s["sp" + n], 1)
                return cols, maxima, split

            cols_B, max_B, split_B = row_max("B", att[B], no1_i, pair(mB))
            cols_E, max_E, split_E = row_max("E", att[E], no3_i, pair(mE))

            def w(n, b, j):
                def step(g):
                    if j == 0:
                        dve.wait_ge(s[f"s{n}_ready"], g.now)
                    dve.wait_ge(s["cmask" + n], g.tile(j))
                    v.scalar_tensor_tensor(b["w"][:, j], b["srow"][:], b["nt"][:, j:j + 1], psS[:, j % 2],
                                           ALU.max, ALU.add).then_inc(s["w" + n], 1)
                return step

            w_B0, w_B1, w_B2, w_B3 = (w("B", att[B], j) for j in range(NT))
            w_E0, w_E1, w_E2, w_E3 = (w("E", att[E], j) for j in range(NT))

            def centre_A0(g):
                dve.wait_ge(s["stA_in_psum"], g.now)
                dve.wait_ge(s["cenA_ready"], g.last)
                v.tensor_copy(stA[:], pair(mA0)).then_inc(s["stA_ready"], 1)

            def centre_A1(g):
                dve.wait_ge(s["sumA_in_psum"], g.now)
                v.tensor_reduce(meanA[:, 0, :], pair(mA1).rearrange("p t c -> p c t"), axis=AX_X,
                                op=ALU.add).then_inc(s["meanA"], 1)
                dve.wait_ge(s["meanA"], g.now)
                dve.wait_ge(s["spA"], g.last)
                v.scalar_tensor_tensor(cenA[:], meanA[:].to_broadcast([P, NT, 2]), -1.0 / N, stA[:], ALU.mult,
                                       ALU.add).then_inc(s["cenA_ready"], 1)
                dve.wait_ge(s["cenA_ready"], g.now)
                v.tensor_tensor(sqA[:], cenA[:], cenA[:], ALU.mult).then_inc(s["sqA_ready"], 1)

            def variance_A(g):
                dve.wait_ge(s["sqA_in_psum"], g.now)
                v.tensor_reduce(varA[:, 0:1], mA2, axis=AX_X, op=ALU.add).then_inc(s["varA"], 1)
                dve.wait_ge(s["varA"], g.now)
                dve.wait_ge(s["rA_ready"], g.last)
                v.tensor_scalar(veA[:], varA[:, 0:1], 1.0 / N, PAIR_EPS, ALU.mult, ALU.add).then_inc(
                    s["veA_ready"], 1)

            def split_A(g):
                dve.wait_ge(s["irA_ready"], g.now)
                v.tensor_scalar(cenA[:, :, 1], cenA[:, :, 1], irA[:], None, ALU.add).then_inc(s["tirA"], 1)
                dve.wait_ge(s["tirA"], g.now)
                dve.wait_ge(s["rows_in_psum_A"], g.last)
                split_to = lambda k: [spA[:, 0, :, k:k + 1], spA[:, 1, :, 3 + k:4 + k]]
                for k, (val, rest) in enumerate(((cenA, r1A), (r1A, r2A), (r2A, None))):
                    for h in range(2):
                        last = v.tensor_copy(split_to(k)[h], val[:, :, h:h + 1])
                    last.then_inc(s[("hiA", "midA", "spA")[k]], 1)
                    if rest is not None:
                        dve.wait_ge(s[("hiA", "midA")[k]], g.now)
                        for h in range(2):
                            last = v.tensor_tensor(rest[:, :, h:h + 1], val[:, :, h:h + 1], split_to(k)[h],
                                                   ALU.subtract)
                        last.then_inc(s[("rest1A", "rest2A")[k]], 1)
                        dve.wait_ge(s[("rest1A", "rest2A")[k]], g.now)

            def v_A(j):
                def step(g):
                    dve.wait_ge(s[f"eA{j}"], 1)
                    dve.wait_ge(s[f"eA{j}"], g.now)
                    v.tensor_tensor_reduce(out=vA[:, j], in0=psS[:, j % 2], in1=adj_j[:, j], scale=1.0,
                                           scalar=-3e38, op0=ALU.mult, op1=ALU.max,
                                           accum_out=vmaxA[:, j:j + 1]).then_inc(s["vA"], 1)
                return step

            v_A0, v_A1, v_A2, v_A3 = (v_A(j) for j in range(NT))

            def max_A(g):
                dve.wait_ge(s["vA"], NT * g.now)
                v.scalar_tensor_tensor(lmA[:], vmaxA[:], SLOPE, vmaxA[:], ALU.mult, ALU.max).then_inc(s["lmA"], 1)
                dve.wait_ge(s["lmA"], g.now)
                dve.wait_ge(s["rA_ready"], g.now)
                dve.wait_ge(s["expA"], NT * g.last)
                v.tensor_scalar(nmA[:], lmA[:], rA[:], -1.0, ALU.mult, ALU.mult).then_inc(s["nmA_ready"], 1)

            def lrelu_A(j):
                def step(g):
                    if j == 0:
                        dve.wait_ge(s["aggA_ready"], g.last)
                        dve.wait_ge(s["vA"], NT * g.now)
                    v.scalar_tensor_tensor(pA[:, j], vA[:, j], SLOPE, vA[:, j], ALU.mult, ALU.max).then_inc(
                        s["lA"], 1)
                return step

            lrelu_A0, lrelu_A1, lrelu_A2, lrelu_A3 = (lrelu_A(j) for j in range(NT))

            def scale_xA(g):
                dve.wait_ge(s["expA"], NT * g.now)
                v.reciprocal(rzA[:], zsA[:]).then_inc(s["rzA"], 1)
                dve.wait_ge(s["rzA"], g.now)
                dve.wait_ge(s["aggA_ready"], g.last)
                for j in range(NT):
                    last = v.tensor_scalar(xsA[:, j], xA[:, j], rzA[:, j:j + 1], None, ALU.mult)
                last.then_inc(s["xA_scaled"], 1)

            def y_A(g):
                dve.wait_ge(s["thA_ready"], g.now)
                dve.wait_ge(s["xhA_ready"], g.now)
                dve.wait_ge(s["applied_A"], g.last)
                v.scalar_tensor_tensor(ln["A"]["y"][:], thA[:], 0.5, xhA[:], ALU.mult, ALU.add).then_inc(s["y_A"], 1)
                stats(g, "A", ln["A"]["y"])

            def copy_hB(g):
                dve.wait_ge(s["hB_in_psum"], g.now)
                dve.wait_ge(s["aggB_ready"], g.last)
                v.tensor_tensor(att[B]["h"][:, :, 0:P], tiles(psF[:, 0]), bp_row[:].to_broadcast([P, NT, P]),
                                ALU.add).then_inc(s["hB_ready"], 1)

            def copy_xBC(g):
                dve.wait_ge(s["applied_A"], g.now)
                dve.wait_ge(s["y_C"], g.last)
                v.tensor_copy(xBC[:], xB[:]).then_inc(s["xBC_ready"], 1)

            def bn_B(g):
                dve.wait_ge(s["aggB_ready"], g.now)
                for i in range(NT):
                    last = v.bn_stats(ln["B"]["st"][:, i], psG[:, 1, i * P:(i + 1) * P])
                last.then_inc(s["bn_B"], 1)

            def stats_B(g):
                dve.wait_ge(s["zsumB_ready"], g.now)
                dve.wait_ge(s["scB_ready"], g.last)
                v.reciprocal(att[B]["rz"][:], mZ[:, 0:NT]).then_inc(s["rzB_ready"], 1)
                dve.wait_ge(s["rzB_ready"], 1)
                dve.wait_ge(s["bn_B"], g.now)
                dve.wait_ge(s["nb_B"], g.last)
                for i in range(NT):
                    last = v.bn_aggr(ln["B"]["mv"][:, i], ln["B"]["st"][:, i])
                last.then_inc(s["aggr_B"], 1)
                dve.wait_ge(s["rzB_ready"], g.now)
                v.tensor_tensor(rrB[:], att[B]["rz"][:], att[B]["rz"][:], ALU.mult).then_inc(s["rrB"], 1)
                dve.wait_ge(s["aggr_B"], g.now)
                dve.wait_ge(s["rrB"], g.now)
                dve.wait_ge(s["ve_B"], g.last)
                v.tensor_tensor(tvB[:], ln["B"]["mv"][:, :, 1], rrB[:], ALU.mult).then_inc(s["stats_B"], 1)

            def nb_B(g):
                dve.wait_ge(s["rstd_B"], g.now)
                dve.wait_ge(s["applied0_B"], g.last)
                v.tensor_tensor(scB[:], ln["B"]["r"][:], att[B]["rz"][:], ALU.mult).then_inc(s["scB_ready"], 1)
                dve.wait_ge(s["scB_ready"], g.now)
                neg_mean(g, "B", scB[:])

            def y_Z(g):
                dve.wait_ge(s["z_in_psum"], g.now)
                dve.wait_ge(s["applied_Z"], g.last)
                v.tensor_tensor(zC[:], tiles(psF[:, 0]), b1_row[:].to_broadcast([P, NT, P]), ALU.add).then_inc(
                    s["y_Z"], 1)
                stats(g, "Z", zC)

            def y_C(g):
                dve.wait_ge(s["x2C_in_psum"], g.now)
                dve.wait_ge(s["hbC_ready"], g.now)
                v.tensor_tensor(qC[:], tiles(psF[:, 0]), hbC[:], ALU.add).then_inc(s["qC_ready"], 1)
                dve.wait_ge(s["qC_ready"], g.now)
                dve.wait_ge(s["xBC_ready"], g.now)
                dve.wait_ge(s["applied_C"], g.last)
                v.scalar_tensor_tensor(ln["C"]["y"][:], qC[:], 0.0, xBC[:], ALU.max, ALU.add).then_inc(s["y_C"], 1)
                stats(g, "C", ln["C"]["y"])

            def y_D(g):
                dve.wait_ge(s["aggD_ready"], g.now)
                dve.wait_ge(s["xbD_ready"], g.now)
                dve.wait_ge(s["applied_D"], g.last)
                v.tensor_tensor(ln["D"]["y"][:], tiles(psG[:, 0]), xbD[:], ALU.add).then_inc(s["y_D"], 1)
                stats(g, "D", ln["D"]["y"])

            def recip_E(g):
                dve.wait_ge(s["aggE_ready"], g.now)
                dve.wait_ge(s["euE_ready"], g.last)
                for i in range(NT):
                    k = (i % 2) * (P + 2) + P
                    last = v.reciprocal(att[E]["rz"][:, i:i + 1], psG[:, i // 2, k:k + 1])
                last.then_inc(s["rzE_ready"], 1)

            def y_E(g):
                dve.wait_ge(s["ruE_ready"], g.now)
                dve.wait_ge(s["euE_ready"], g.now)
                v.scalar_tensor_tensor(y1E[:], euE[:], 1.0, ruE[:], ALU.min, ALU.add).then_inc(s["y1E"], 1)
                dve.wait_ge(s["y1E"], g.now)
                dve.wait_ge(s["xmE_ready"], g.now)
                dve.wait_ge(s["applied_E"], g.last)
                v.tensor_tensor(ln["E"]["y"][:], y1E[:], xmE[:], ALU.add).then_inc(s["y_E"], 1)
                stats(g, "E", ln["E"]["y"])

            def turn(t):
                t.run(y_Z, 3)
                t.run(nb_E, 5)
                t.run(w_B0, 2)
                t.run(nb_Z, 3)
                t.run(w_B1, 2)
                t.run(w_E0, 4)
                t.run(w_E1, 4)
                t.run(y_A, 1)
                t.run(w_E2, 4)
                t.run(y_C, 3)
                t.run(w_E3, 4)
                t.run(w_B2, 2)
                t.run(nb_C, 3)
                t.run(copy_xBC, 2)
                t.run(w_B3, 2)
                t.run(copy_hB, 2)
                t.run(recip_E, 4)
                t.run(centre_A0, 0)
                t.run(nb_A, 1)
                t.run(centre_A1, 0)
                t.run(variance_A, 0)
                t.run(y_E, 4)
                t.run(split_A, 0)
                t.run(y_D, 3)
                t.run(cols_B, 1)
                t.run(max_B, 1)
                t.run(nb_D, 3)
                t.run(bn_B, 2)
                t.run(stats_B, 2)
                t.run(v_A0, 0)
                t.run(split_B, 1)
                t.run(nb_B, 2)
                t.run(v_A1, 0)
                t.run(v_A2, 0)
                t.run(v_A3, 0)
                t.run(cols_E, 3)
                t.run(max_A, 0)
                t.run(lrelu_A0, 0)
                t.run(lrelu_A1, 0)
                t.run(lrelu_A2, 0)
                t.run(max_E, 3)
                t.run(lrelu_A3, 0)
                t.run(split_E, 3)
                t.run(scale_xA, 0)

            turns(dve, turn)

        @block.scalar
        def _(act):
            def normalise(g, k, src, dst, scale=None, name=None):
                L = ln[k]
                act.wait_ge(s["nb_" + k], g.now)
                act.wait_ge(s["rstd_" + k], g.now)
                for i in range(NT):
                    last = a.activation(dst[:, i], src(i), ACT.Identity, scale=(L["r"] if scale is None else scale)[:, i:i + 1],
                                        bias=L["nb"][:, i:i + 1])
                last.then_inc(s[name or "applied_" + k], 1)

            def exp(n, b, j):
                def step(g):
                    act.wait_ge(s["w" + n], g.tile(j))
                    a.activation(b["p"][:, j], b["w"][:, j], ACT.Exp, scale=1.0 - SLOPE,
                                 bias=b["st"][:, j, 1:2]).then_inc(s["exp" + n], 1)
                return step

            exp_B0, exp_B1, exp_B2, exp_B3 = (exp("B", att[B], j) for j in range(NT))
            exp_E0, exp_E1, exp_E2, exp_E3 = (exp("E", att[E], j) for j in range(NT))

            def copy_xTA(g):
                act.wait_ge(s["xA_transposed"], g.now)
                act.wait_ge(s["stA_in_psum"], g.last)
                a.copy(xTA[:], psT[:, 0]).then_inc(s["xTA_ready"], 1)

            def copy_rowsA(g):
                act.wait_ge(s["rows_in_psum_A"], g.now)
                act.wait_ge(s["eA3"], g.last)
                a.copy(rowsA[:], psTb).then_inc(s["rowsA_ready"], 1)

            def exp_A(j):
                def step(g):
                    act.wait_ge(s["lA"], g.tile(j))
                    act.wait_ge(s["nmA_ready"], g.now)
                    act.wait_ge(s["rzA"], g.last)
                    a.activation(pA[:, j], pA[:, j], ACT.Exp, scale=rA[:], bias=nmA[:, j:j + 1],
                                 accum_out=zsA[:, j:j + 1]).then_inc(s["expA"], 1)
                return step

            exp_A0, exp_A1, exp_A2, exp_A3 = (exp_A(j) for j in range(NT))

            def tanh_A(g):
                act.wait_ge(s["aggA_ready"], g.now)
                act.wait_ge(s["y_A"], g.last)
                a.activation(thA[:], tiles(psG[:, 0]), ACT.Tanh, scale=0.5).then_inc(s["thA_ready"], 1)

            def norm_A(g):
                act.wait_ge(s["xB_transposed"], g.last)
                act.wait_ge(s["xBC_ready"], g.last)
                normalise(g, "A", lambda i: ln["A"]["y"][:, i], xB)

            def copy_xTB(g):
                act.wait_ge(s["xB_transposed"], g.now)
                for used in ("hB_in_psum", "sB_in_psum", "stB_in_psum", "tB_in_psum"):
                    act.wait_ge(s[used], g.last)
                a.copy(xTB[:], psT[:, 0]).then_inc(s["xTB_ready"], 1)

            def copy_sB(g):
                act.wait_ge(s["sB_in_psum"], g.now)
                act.wait_ge(s["wB"], NT * g.last)
                a.activation(att[B]["srow"][:], psT[:, 0], ACT.Identity, bias=bst[:, 0, 0:1]).then_inc(
                    s["sB_ready"], 1)

            def copy_cB(g):
                act.wait_ge(s["rows_in_psum_B"], g.now)
                act.wait_ge(s["cmaskB"], NT * g.last)
                a.copy(att[B]["crow"][:], psTb[:, 0:N]).then_inc(s["crowB"], 1)

            def norm_B(g):
                act.wait_ge(s["nbB_ready"], g.last)
                act.wait_ge(s["applied_B"], g.last)
                act.wait_ge(s["scB_ready"], g.now)
                normalise(g, "B", lambda i: psG[:, 1, i * P:(i + 1) * P], nB, scale=scB, name="applied0_B")

            def relu_B(g):
                act.wait_ge(s["nbB_ready"], g.now)
                act.wait_ge(s["hbC_ready"], g.last)
                act.wait_ge(s["ginT_in_psum"], g.last)
                a.activation(hgat[:], nB[:], ACT.Relu).then_inc(s["applied_B"], 1)

            def copy_ginT(g):
                act.wait_ge(s["ginT_in_psum"], g.now)
                act.wait_ge(s["z_in_psum"], g.last)
                a.copy(ginT[:], psF[:, 0]).then_inc(s["ginT_ready"], 1)

            def norm_Z(g):
                act.wait_ge(s["zgC_ready"], g.last)
                act.wait_ge(s["zT_in_psum"], g.last)
                normalise(g, "Z", lambda i: zC[:, i], znC)

            def copy_zT(g):
                act.wait_ge(s["zT_in_psum"], g.now)
                act.wait_ge(s["x2C_in_psum"], g.last)
                a.activation(zT[:], psT[:, 0], ACT.Relu).then_inc(s["zT_ready"], 1)

            def norm_C(g):
                act.wait_ge(s["xbD_ready"], g.last)
                act.wait_ge(s["xD_transposed"], g.last)
                normalise(g, "C", lambda i: ln["C"]["y"][:, i], xD)

            def copy_xTD(g):
                act.wait_ge(s["xD_transposed"], g.now)
                act.wait_ge(s["h1D_in_psum"], g.last)
                act.wait_ge(s["xTdD_ready"], g.last)
                a.copy(xTD[:], psT[:, 0]).then_inc(s["xTD_ready"], 1)

            def copy_hD(g):
                act.wait_ge(s["h1D_in_psum"], g.now)
                act.wait_ge(s["aggD_ready"], g.last)
                a.copy(h1D[:].rearrange("p t d -> p (t d)"), psF[:, 0]).then_inc(s["h1D_ready"], 1)

            def norm_D(g):
                act.wait_ge(s["xmE_ready"], g.last)
                act.wait_ge(s["xE_transposed"], g.last)
                normalise(g, "D", lambda i: ln["D"]["y"][:, i], xE)

            def copy_xTE(g):
                act.wait_ge(s["xE_transposed"], g.now)
                for used in ("hE_in_psum", "sE_in_psum", "stE_in_psum", "tE_in_psum"):
                    act.wait_ge(s[used], g.last)
                a.copy(xTE[:], psT[:, 0]).then_inc(s["xTE_ready"], 1)

            def copy_sE(g):
                act.wait_ge(s["sE_in_psum"], g.now)
                act.wait_ge(s["wE"], NT * g.last)
                a.copy(att[E]["srow"][:], psT[:, 0]).then_inc(s["sE_ready"], 1)

            def copy_hE(g):
                act.wait_ge(s["hE_in_psum"], g.now)
                act.wait_ge(s["aggE_ready"], g.last)
                a.copy(att[E]["h"][:, :, 0:P], tiles(psF[:, 0])).then_inc(s["hE_ready"], 1)

            def copy_cE(g):
                act.wait_ge(s["rows_in_psum_E"], g.now)
                act.wait_ge(s["cmaskE"], NT * g.last)
                a.copy(att[E]["crow"][:], psTb[:, 0:N]).then_inc(s["crowE"], 1)

            def elu_E(g):
                act.wait_ge(s["rzE_ready"], g.now)
                act.wait_ge(s["y1E"], g.last)
                for f, dst, name in ((ACT.Relu, ruE, "ruE_ready"), (ACT.Exp, euE, "euE_ready")):
                    for i in range(NT):
                        k = (i % 2) * (P + 2)
                        last = a.activation(dst[:, i], psG[:, i // 2, k:k + P], f, scale=att[E]["rz"][:, i:i + 1])
                    last.then_inc(s[name], 1)

            def norm_E(g):
                act.wait_ge(s["xout_stored"], 16 * g.last)
                normalise(g, "E", lambda i: ln["E"]["y"][:, i], xout, name="xout_ready")
                act.sem_inc(s["applied_E"], 1)

            def turn(t):
                t.run(copy_cE, 4)
                t.run(norm_E, 5)
                t.run(norm_Z, 3)
                t.run(exp_B0, 2)
                t.run(tanh_A, 1)
                t.run(copy_hE, 4)
                t.run(copy_xTA, 0)
                t.run(exp_E0, 4)
                t.run(copy_zT, 3)
                t.run(exp_E1, 4)
                t.run(exp_B1, 2)
                t.run(exp_E2, 4)
                t.run(exp_E3, 4)
                t.run(norm_C, 3)
                t.run(exp_B2, 2)
                t.run(copy_xTD, 3)
                t.run(elu_E, 4)
                t.run(copy_hD, 3)
                t.run(exp_B3, 2)
                t.run(norm_A, 1)
                t.run(copy_xTB, 1)
                t.run(copy_rowsA, 0)
                t.run(norm_D, 3)
                t.run(copy_xTE, 3)
                t.run(norm_B, 2)
                t.run(copy_cB, 1)
                t.run(exp_A0, 0)
                t.run(relu_B, 2)
                t.run(copy_sB, 1)
                t.run(exp_A1, 0)
                t.run(exp_A2, 0)
                t.run(exp_A3, 0)
                t.run(copy_ginT, 2)
                t.run(copy_sE, 3)

            turns(act, turn)


_INS = ["x", "adj", "L0_gnn_a", "L1_gnn_Wp", "L1_gnn_bp", "L1_gnn_a_src", "L1_gnn_a_dst", "L1_gnn_gat_g",
        "L1_gnn_gat_b", "L1_gnn_eps", "L1_gnn_W1", "L1_gnn_b1", "L1_gnn_mlp_g", "L1_gnn_mlp_b", "L1_gnn_W2",
        "L1_gnn_b2", "L2_gnn_W", "L2_gnn_e", "L2_gnn_bias", "L3_gnn_W", "L3_gnn_a_src", "L3_gnn_a_dst"]


def kernel(**inputs):
    import numpy as _np
    import concourse.bacc as _bacc
    from concourse import mybir as _mybir
    from concourse.bass_utils import run_bass_kernel_spmd as _run

    nc = _bacc.Bacc("TRN2", target_bir_lowering=False, num_devices=1)
    arrays, args = {}, []
    for name in _INS:
        a = _np.ascontiguousarray(inputs[name])
        arrays[f"in_{name}_dram"] = a
        args.append(nc.dram_tensor(f"in_{name}_dram", a.shape, _mybir.dt.from_np(a.dtype), kind="ExternalInput").ap())
    out = nc.dram_tensor("out_0_dram", inputs["x"].shape, _mybir.dt.float32, kind="ExternalOutput").ap()
    resnorm_gnn(nc, *args, out)
    r = _run(nc, [arrays], core_ids=[0])
    return r.results[0]["out_0_dram"]
```

```python
from contextlib import ExitStack

import concourse.bass as bass
from concourse import mybir

P = 128
ALU = mybir.AluOpType
ACT = mybir.ActivationFunctionType
AX_X = mybir.AxisListType.X
F32 = mybir.dt.float32
BF16 = mybir.dt.bfloat16
I32 = mybir.dt.int32

B, E = "BE"
LAST_DELAY = 4
BIG = 2.0 ** 100
SLOPE = 0.2
LN_EPS = 1e-5
PAIR_EPS = 1e-14
NEG = -9000000000000000.0


class Graph:

    def __init__(self, turn, delay):
        self.turn, self.delay = turn, delay
        self.g = turn.it - delay
        self.real = not isinstance(turn.it, int) or 0 <= self.g < turn.graphs
        self.now = turn.it - (delay - 1)
        self.last = self.g

    def tile(self, j, tiles=4):
        return self.now if tiles == 1 else self.g * tiles + (j + 1)


class Turn:
    def __init__(self, it, graphs):
        self.it, self.graphs = it, graphs

    def graph(self, delay):
        return Graph(self, delay)

    def run(self, step, delay):
        g = self.graph(delay)
        if g.real:
            step(g)


def resnorm_gnn(nc, x, adj, l0_a, wp, bp, a_src, a_dst, gat_g, gat_b, eps, w1, b1, mlp_g, mlp_b, w2, b2,
                l2_w, l2_e, l2_bias, l3_w, l3_src, l3_dst, out):
    GRAPHS, N, DIM = x.shape
    NT = N // P
    assert DIM == P and N == NT * P
    EDGES = l2_e.shape[1]
    EC = EDGES // P

    with ExitStack() as ctx:
        def sb(name, shape, dt=F32):
            return ctx.enter_context(nc.sbuf_tensor(name, shape, dt))

        def bank(name, n=1):
            return ctx.enter_context(nc.psum_tensor(name, [P, n, 512], F32))

        class Signals(dict):

            def __missing__(self, name):
                self[name] = nc.alloc_semaphore(name=name)
                return self[name]

        ident = sb("ident", [P, P])
        identb = sb("identb", [P, P], BF16)
        ones = sb("ones", [P, P])
        onesb = sb("onesb", [P, P], BF16)
        consts = sb("consts", [P, 4])
        adj_i = sb("adj_i", [P, NT, N])
        adj_j = sb("adj_j", [P, NT, N])
        gin_j = sb("gin_j", [P, NT, N])
        att2_j = sb("att2_j", [P, NT, N])
        diag2 = sb("diag2", [P, N])
        no1_i = sb("no1_i", [P, NT, N], BF16)
        no1_j = sb("no1_j", [P, NT, N], BF16)
        no3_i = sb("no3_i", [P, NT, N], BF16)
        no3_j = sb("no3_j", [P, NT, N], BF16)
        a01 = sb("a01", [P, 2])
        wp_sb = sb("wp_sb", [P, P])
        w1_sb = sb("w1_sb", [P, P])
        w2_sb = sb("w2_sb", [P, P])
        l2w0 = sb("l2w0", [P, P])
        l2w1 = sb("l2w1", [P, P])
        w3_sb = sb("w3_sb", [P, P])
        bp_row = sb("bp_row", [P, 1, P])
        gg_row = sb("gg_row", [P, 1, P])
        gb_row = sb("gb_row", [P, 1, P])
        b1_row = sb("b1_row", [P, 1, P])
        mlp_gb = sb("mlp_gb", [P, 2])
        b2_row = sb("b2_row", [P, 1, P])
        l2b_row = sb("l2b_row", [P, 1, P])
        avec = sb("avec", [P, 5])
        eps_c = sb("eps_c", [P, 1])
        ws1 = sb("ws1", [P, P])
        wt1 = sb("wt1", [P, P])
        ws3 = sb("ws3", [P, P])
        wt3 = sb("wt3", [P, P])
        st1 = sb("st1", [P, 2])
        st3 = sb("st3", [P, 2])
        bst = sb("bst", [P, 1, 2])
        xA = sb("xA", [P, NT, P])
        xB = sb("xB", [P, NT, P])
        xBC = sb("xBC", [P, NT, P])
        hgat = sb("hgat", [P, NT, P])
        xD = sb("xD", [P, NT, P])
        xE = sb("xE", [P, NT, P])
        xout = sb("xout", [P, NT, P])
        xTA = sb("xTA", [P, N])
        xTB = sb("xTB", [P, N])
        xTD = sb("xTD", [P, N])
        xTE = sb("xTE", [P, N])
        xTdD = sb("xTdD", [P, N])
        ginT = sb("ginT", [P, N])
        zT = sb("zT", [P, N])
        stA = sb("stA", [P, NT, 2])
        cenA = sb("cenA", [P, NT, 2])
        sqA = sb("sqA", [P, NT, 2])
        meanA = sb("meanA", [P, 1, 2])
        varA = sb("varA", [P, 2])
        veA = sb("veA", [P, 1])
        rA = sb("rA", [P, 1])
        irA = sb("irA", [P, 1])
        rowsA = sb("rowsA", [P, 2 * N], BF16)
        spA = sb("spA", [P, 2, NT, P], BF16)
        r1A = sb("r1A", [P, NT, 2])
        r2A = sb("r2A", [P, NT, 2])
        vA = sb("vA", [P, NT, N])
        vmaxA = sb("vmaxA", [P, NT])
        lmA = sb("lmA", [P, NT])
        nmA = sb("nmA", [P, NT])
        pA = sb("pA", [P, NT, N])
        zsA = sb("zsA", [P, NT])
        rzA = sb("rzA", [P, NT])
        xsA = sb("xsA", [P, NT, P])
        xhA = sb("xhA", [P, NT, P])
        thA = sb("thA", [P, NT, P])
        att = {}
        for g in (B, E):
            n = g
            att[g] = dict(
                h=sb("h" + n, [P, NT, P + 2]), st=sb("st" + n, [P, NT, 2]), nt=sb("nt" + n, [P, NT]),
                srow=sb("srow" + n, [P, N]), mx=sb("mx" + n, [P, NT]),
                u=sb("u" + n, [P, NT]), m=sb("m" + n, [P, NT]), q=sb("q" + n, [P, NT]),
                c=sb("c" + n, [P, NT, 1]), r1=sb("r1" + n, [P, NT, 1]),
                sp=sb("sp" + n, [P, NT, P], BF16), crow=sb("crow" + n, [P, N], BF16),
                w=sb("w" + n, [P, NT, N]), rz=sb("rz" + n, [P, NT]),
            )
            att[g]["p"] = att[g]["w"]
        paB = sb("paB", [P, NT, N])
        psumB = sb("psumB", [P, 3, N])
        nB = sb("nB", [P, NT, P])
        ngB = sb("ngB", [P, NT, P])
        rrB = sb("rrB", [P, NT])
        tvB = sb("tvB", [P, NT])
        scB = sb("scB", [P, NT])
        znC = sb("znC", [P, NT, P])
        hbC = sb("hbC", [P, NT, P])
        qC = sb("qC", [P, NT, P])
        h1D = sb("h1D", [P, NT, P])
        xbD = sb("xbD", [P, NT, P])
        euE = sb("euE", [P, NT, P])
        ruE = sb("ruE", [P, NT, P])
        y1E = sb("y1E", [P, NT, P])
        xmE = sb("xmE", [P, NT, P])
        ln = {k: dict(y=sb("y_" + k, [P, NT, P]) if k != "B" else None, st=sb("lnst_" + k, [P, NT, 6]), mv=sb("lnmv_" + k, [P, NT, 2]),
                      ve=sb("lnve_" + k, [P, NT]), r=sb("lnr_" + k, [P, NT]), nb=sb("lnnb_" + k, [P, NT]))
              for k in ("A", "B", "Z", "C", "D", "E")}

        zC = ln["Z"]["y"]
        psT = bank("psT")
        psS = bank("psS", 2)
        psG = bank("psG", 2)
        psF = bank("psF")
        psR = bank("psR")
        psM = bank("psM")
        psTb = psT[:, 0, :].bitcast(BF16)
        mA0, mA1, mA2, mB, mZ, mE = (psM[:, 0, 8 * k:8 * k + 8] for k in range(6))

        def tiles(ap):
            return ap.rearrange("p (t d) -> p t d", t=NT)

        def pair(ap):
            return ap.rearrange("p (t d) -> p t d", d=2)

        mask = vA
        cnt = idx = pA
        upper = dia = att[B]["w"]
        vals = att[E]["w"]
        eye = paB
        tmp = att2_j
        sel_k = psumB[:, 0:EC]
        sel_i = sb("sel_i", [P, NT, EDGES])
        q_k = sb("q_k", [P, EC, N])
        tot = sb("tot", [P, NT])
        off = sb("off", [P, NT])
        nxt = sb("nxt", [P, NT])
        kf_i = sb("kf_i", [P, EDGES], I32)
        kf = sb("kf", [P, EDGES])
        kc_i = sb("kc_i", [P, EC], I32)
        kc = sb("kc", [P, EC])
        ecol = sb("ecol", [P, EC])
        elast = sb("elast", [P, 1])
        rowm = sb("rowm", [P, NT])
        rowz = sb("rowz", [P, NT])
        rowr = sb("rowr", [P, NT])
        eps1 = sb("eps1", [P, 1])
        wT = sb("wT", [P, 2, P])
        arep = gin_j[:].rearrange("p t j -> p (t j)")[:, 0:5 * P].rearrange("p (k d) -> p k d", k=5)

        x_v = x.rearrange("b (t p) d -> b p t d", p=P)
        out_v = out.rearrange("b (t p) d -> b p t d", p=P)

        N_LOADS = 23 + EC
        mm, v, a = nc.tensor.matmul, nc.vector, nc.scalar

        def column(v):
            return v.rearrange("(p a) -> p a", a=1)

        def on_all(v):
            return v.rearrange("(a d) -> a d", a=1).partition_broadcast(P)

        with ExitStack() as setup_ctx:
            s = Signals()
            block = setup_ctx.enter_context(nc.Block())

            @block.sync
            def _(sp):
                sp.dma_start(adj_i[:], adj.rearrange("(t p) j -> p t j", p=P)).then_inc(s["adj_in"], 16)
                loads = [
                    (a01[:, 0:1], l0_a[0:P, :]), (a01[:, 1:2], l0_a[P:2 * P, :]),
                    (wp_sb[:], wp), (w1_sb[:], w1), (w2_sb[:], w2), (l2w0[:], l2_w[0]), (l2w1[:], l2_w[1]),
                    (w3_sb[:], l3_w), (avec[:, 0:1], column(a_src)), (avec[:, 1:2], column(a_dst)),
                    (avec[:, 2:3], l3_src), (avec[:, 3:4], l3_dst), (avec[:, 4:5], column(bp)),
                    (bp_row[:, 0, :], on_all(bp)), (gg_row[:, 0, :], on_all(gat_g)), (gb_row[:, 0, :], on_all(gat_b)),
                    (b1_row[:, 0, :], on_all(b1)), (mlp_gb[:, 0:1], column(mlp_g)), (mlp_gb[:, 1:2], column(mlp_b)),
                    (b2_row[:, 0, :], on_all(b2)), (l2b_row[:, 0, :], on_all(l2_bias)), (eps_c[:], on_all(eps)),
                    (elast[:], l2_e[0:1, EDGES - 1:EDGES].partition_broadcast(P)),
                ] + [(ecol[:, c:c + 1], column(l2_e[0, c * P:(c + 1) * P])) for c in range(EC)]
                assert len(loads) == N_LOADS
                for dst, src in loads:
                    sp.dma_start(dst, src).then_inc(s["weights_in"], 16)

            @block.gpsimd
            def _(pool):
                pool.memset(ident[:], 0.0).then_inc(s["ident0"], 1)
                pool.memset(identb[:], 0.0).then_inc(s["ident0"], 1)
                pool.memset(ones[:], 1.0).then_inc(s["ones_set"], 1)
                pool.memset(onesb[:], 1.0).then_inc(s["ones_set"], 1)
                for k, value in enumerate((-0.5, 0.5, LN_EPS, -1.0)):
                    pool.memset(consts[:, k:k + 1], value).then_inc(s["consts_set"], 1)
                pool.memset(upper[:], 1.0).then_inc(s["upper0"], 1)
                pool.memset(eye[:], 0.0).then_inc(s["upper0"], 1)
                pool.iota(kf_i[:], pattern=[[1, EDGES]], base=0, channel_multiplier=0).then_inc(s["iota_set"], 1)
                pool.iota(kc_i[:], pattern=[[P, EC]], base=0, channel_multiplier=1).then_inc(s["iota_set"], 1)
                pool.wait_ge(s["ident0"], 2)
                for m in (ident, identb):
                    pool.affine_select(out=m[:], in_=m[:], compare_op=ALU.not_equal, fill=1.0, base=0,
                                       pattern=[[-1, P]], channel_multiplier=1).then_inc(s["ident_set"], 1)
                pool.wait_ge(s["upper0"], 2)
                above = dict(base=0, pattern=[[-P, NT], [1, N]], channel_multiplier=-1)
                pool.affine_select(out=upper[:], in_=upper[:], compare_op=ALU.is_gt, fill=0.0,
                                   **above).then_inc(s["upper_set"], 1)
                pool.affine_select(out=eye[:], in_=eye[:], compare_op=ALU.not_equal, fill=1.0,
                                   **above).then_inc(s["eye_set"], 1)
                pool.memset(spA[:], 0.0).then_inc(s["sp0"], 1)
                pool.memset(att[B]["sp"][:], 0.0).then_inc(s["sp0"], 1)
                pool.memset(att[E]["sp"][:], 0.0).then_inc(s["sp0"], 1)
                pool.wait_ge(s["sp0"], 3)
                pool.memset(spA[:, 0, :, 3:6], 1.0).then_inc(s["sp_ones"], 1)
                pool.memset(spA[:, 1, :, 0:3], 1.0).then_inc(s["sp_ones"], 1)
                pool.memset(att[E]["h"][:, :, P:P + 2], 1.0).then_inc(s["sp_ones"], 1)
                pool.wait_ge(s["adj_in"], 16)
                pool.wait_ge(s["eye_set"], 1)
                n = 0
                for n_copied, a, no in ((0, adj_i, no3_i), (NT, adj_j, no3_j)):
                    if n_copied:
                        pool.wait_ge(s["adjT_copied"], n_copied)
                    for i in range(NT):
                        loops = (xTA, xTB, xTD, xTE)[i]
                        pool.tensor_tensor(loops[:], a[:, i], eye[:, i], ALU.add).then_inc(s["loops"], 1)
                        n += 1
                        pool.wait_ge(s["loops"], n)
                        last = pool.tensor_scalar(no[:, i], loops[:], 0.0, -BIG, ALU.is_le, ALU.mult)
                last.then_inc(s["no3_ready"], 1)
                pool.wait_ge(s["no3_ready"], 1)
                pool.wait_ge(s["weights_in"], 16 * N_LOADS)

            @block.tensor
            def _(pe):
                pe.wait_ge(s["ident_set"], 2)
                pe.wait_ge(s["ones_set"], 2)
                pe.wait_ge(s["tot_ready"], 1)
                pe.wait_ge(s["upper_set"], 1)
                for c in range(NT):
                    for i in range(NT):
                        last = mm(psR[:, 0, c:c + 1], upper[:, i, c * P:(c + 1) * P], tot[:, i:i + 1],
                                  start=(i == 0), stop=(i == NT - 1))
                last.then_inc(s["off_cols"], 1)
                pe.wait_ge(s["adj_in"], 16)
                for j in range(NT):
                    dst = psS[:, j % 2]
                    if j >= 2:
                        pe.wait_ge(s["adjT_copied"], j - 1)
                    for i in range(NT):
                        last = nc.tensor.transpose(dst[:, i * P:(i + 1) * P], adj_i[:, i, j * P:(j + 1) * P], ident[:])
                    last.then_inc(s["adjT_in_psum"], 1)
                pe.wait_ge(s["weights_in"], 16 * N_LOADS)
                nc.tensor.transpose(psM[:, 0, 0:P], wp_sb[:], ident[:])
                nc.tensor.transpose(psM[:, 0, P:2 * P], w3_sb[:], ident[:]).then_inc(s["wT_in_psum"], 1)
                pe.wait_ge(s["sel_ready"], 1)
                for c in range(EC):
                    for i in range(NT):
                        last = nc.tensor.transpose(psG[:, c, i * P:(i + 1) * P], sel_i[:, i, c * P:(c + 1) * P], ident[:])
                    last.then_inc(s["sel_k_in_psum"], 1)
                pe.wait_ge(s["adjT_copied"], NT)
                for c in range(EC):
                    for i in range(NT):
                        last = mm(psS[:, c], sel_i[:, i, c * P:(c + 1) * P], idx[:, i], start=(i == 0), stop=(i == NT - 1))
                last.then_inc(s["erow_in_psum"], 1)
                pe.wait_ge(s["wT_ready"], 1)
                pe.wait_ge(s["arep_ready"], 1)
                for k in range(4):
                    mm(psF[:, 0, k * P:(k + 1) * P], wT[:, k // 2, :], arep[:, k, :], start=True, stop=True)
                mm(psM[:, 0, 256:258], arep[:, 4, :], avec[:, 0:2], start=True, stop=True).then_inc(s["wa_in_psum"], 1)
                pe.wait_ge(s["q_ready"], 1)
                pe.wait_ge(s["sel_k_ready"], EC)
                for i in range(NT):
                    if i >= 2:
                        pe.wait_ge(s["vals_taken"], i - 1)
                    for c in range(EC):
                        last = mm(psG[:, i % 2], sel_k[:, c, i * P:(i + 1) * P], q_k[:, c], start=(c == 0),
                                  stop=(c == EC - 1))
                    last.then_inc(s["vals_in_psum"], 1)
                for i in range(NT):
                    pe.wait_ge(s["dia_ready"], i + 1)
                    last = mm(psR[:, 0], ones[:], dia[:, i], start=(i == 0), stop=(i == NT - 1))
                last.then_inc(s["diag_in_psum"], 1)
                for j in range(NT):
                    if j >= 2:
                        pe.wait_ge(s["att2T_copied"], j - 1)
                    for i in range(NT):
                        last = nc.tensor.transpose(psS[:, j % 2, i * P:(i + 1) * P], vals[:, i, j * P:(j + 1) * P], ident[:])
                    last.then_inc(s["att2T_in_psum"], 1)

            @block.vector
            def _(dve):

                def then(ins, name):
                    ins.then_inc(s[name], 1)
                    then.n[name] = then.n.get(name, 0) + 1
                    dve.wait_ge(s[name], then.n[name])
                then.n = {}

                dve.wait_ge(s["adj_in"], 16)
                then(v.tensor_scalar(mask[:], adj_i[:], 0.0, None, ALU.is_gt), "mask_set")
                then(v.tensor_reduce(tot[:], mask[:], axis=AX_X, op=ALU.add), "tot_ready")
                then(v.memset(tmp[:, 0], 1.0), "tmp_ones")
                for i in range(NT):
                    last = v.tensor_tensor_scan(cnt[:, i], tmp[:, 0], mask[:, i], 0.0, ALU.mult, ALU.add)
                last.then_inc(s["cnt_ready"], 1)
                dve.wait_ge(s["iota_set"], 2)
                v.tensor_copy(kf[:], kf_i[:])
                then(v.tensor_copy(kc[:], kc_i[:]), "k_ready")
                dve.wait_ge(s["off_cols"], 1)
                then(v.tensor_copy(off[:], psR[:, 0, 0:NT]), "off_ready")
                then(v.tensor_tensor(nxt[:], off[:], tot[:], ALU.add), "off_ready")
                dve.wait_ge(s["cnt_ready"], 1)
                for i in range(NT):
                    then(v.tensor_scalar(tmp[:, i, 0:EDGES], kf[:], off[:, i:i + 1], None, ALU.is_ge), "sel0")
                    last = v.scalar_tensor_tensor(sel_i[:, i], kf[:], nxt[:, i:i + 1], tmp[:, i, 0:EDGES], ALU.is_lt, ALU.mult)
                for i in range(NT):
                    last = v.scalar_tensor_tensor(idx[:, i], cnt[:, i], off[:, i:i + 1], mask[:, i], ALU.add, ALU.mult)
                then(last, "idx_ready")
                then(v.tensor_scalar(idx[:], idx[:], -1.0, None, ALU.add), "sel_ready")
                dve.wait_ge(s["weights_in"], 16 * N_LOADS)
                for k in range(5):
                    last = v.tensor_copy(arep[:, k, :], avec[:, k:k + 1].to_broadcast([P, P]))
                last.then_inc(s["arep_ready"], 1)
                dve.wait_ge(s["wT_in_psum"], 1)
                v.tensor_copy(wT[:].rearrange("p a b -> p (a b)"), psM[:, 0, 0:2 * P]).then_inc(s["wT_ready"], 1)
                then(v.tensor_scalar(tmp[:], idx[:], float(EDGES), elast[:], ALU.is_ge, ALU.mult), "past")
                then(v.tensor_scalar(mask[:], mask[:], -1.0, -NEG, ALU.add, ALU.mult), "past")
                then(v.tensor_tensor(tmp[:], tmp[:], mask[:], ALU.add), "past")
                dve.wait_ge(s["erow_in_psum"], 1)
                for c in range(EC):
                    last = v.tensor_scalar(q_k[:, c], psS[:, c], kc[:, c:c + 1], ecol[:, c:c + 1], ALU.is_equal, ALU.mult)
                last.then_inc(s["q_ready"], 1)
                dve.wait_ge(s["wa_in_psum"], 1)
                for k, (rep, two) in enumerate(((ws1, st1), (wt1, st1), (ws3, st3), (wt3, st3))):
                    v.tensor_copy(rep[:], psF[:, 0, k * P:(k + 1) * P])
                    v.tensor_copy(two[:, k % 2:k % 2 + 1], psF[:, 0, k * P:k * P + 1])
                v.tensor_copy(bst[:, 0, :], psM[:, 0, 256:258]).then_inc(s["setup_done"], 1)
                v.tensor_scalar(no1_i[:], adj_i[:], 0.0, -BIG, ALU.is_le, ALU.mult)
                dve.wait_ge(s["adjT_copied"], NT)
                v.tensor_scalar(no1_j[:], adj_j[:], 0.0, -BIG, ALU.is_le, ALU.mult)
                then(v.tensor_scalar(eps1[:], eps_c[:], 1.0, None, ALU.add), "eps_ready")
                dve.wait_ge(s["eye_set"], 1)
                v.scalar_tensor_tensor(gin_j[:], eye[:], eps1[:], adj_j[:], ALU.mult, ALU.add)
                for i in range(NT):
                    dve.wait_ge(s["vals_in_psum"], i + 1)
                    then(v.tensor_tensor(vals[:, i], psG[:, i % 2], tmp[:, i], ALU.add), "vals_taken")
                    v.tensor_reduce(rowm[:, i:i + 1], vals[:, i], axis=AX_X, op=ALU.max,
                                    negate=True).then_inc(s["rowm_ready"], 1)
                for i in range(NT):
                    dve.wait_ge(s["exp2_ready"], i + 1)
                    then(v.reciprocal(rowr[:, i:i + 1], rowz[:, i:i + 1]), "rowr_ready")
                    then(v.scalar_tensor_tensor(dia[:, i], vals[:, i], rowr[:, i:i + 1], eye[:, i], ALU.mult,
                                                ALU.mult), "dia_set")
                    v.scalar_tensor_tensor(vals[:, i], vals[:, i], rowr[:, i:i + 1], dia[:, i], ALU.mult,
                                           ALU.subtract).then_inc(s["dia_ready"], 1)

            @block.scalar
            def _(act):

                for j in range(NT):
                    act.wait_ge(s["adjT_in_psum"], j + 1)
                    a.copy(adj_j[:, j], psS[:, j % 2]).then_inc(s["adjT_copied"], 1)
                for c in range(EC):
                    act.wait_ge(s["sel_k_in_psum"], c + 1)
                    a.copy(sel_k[:, c], psG[:, c]).then_inc(s["sel_k_ready"], 1)
                for i in range(NT):
                    act.wait_ge(s["rowm_ready"], i + 1)
                    a.activation(vals[:, i], vals[:, i], ACT.Exp, bias=rowm[:, i:i + 1],
                                 accum_out=rowz[:, i:i + 1]).then_inc(s["exp2_ready"], 1)
                act.wait_ge(s["diag_in_psum"], 1)
                a.copy(diag2[:], psR[:, 0])
                for j in range(NT):
                    act.wait_ge(s["att2T_in_psum"], j + 1)
                    a.copy(att2_j[:, j], psS[:, j % 2]).then_inc(s["att2T_copied"], 1)
                act.wait_ge(s["att2T_copied"], NT)

        nc.clear_and_free_semaphores(list(s.values()))
        nc.all_engine_barrier()
        s = Signals()
        block = ctx.enter_context(nc.Block())

        def turns(eng, body):
            for it in range(LAST_DELAY + 1):
                body(Turn(it, GRAPHS))
            with eng.Fori(LAST_DELAY + 1, GRAPHS) as it:
                body(Turn(it, GRAPHS))
            for it in range(GRAPHS, GRAPHS + LAST_DELAY):
                body(Turn(it, GRAPHS))

        SMALL = 7


        @block.sync
        def _(sp):
            def load_xA(g):
                sp.wait_ge(s["xA_transposed"], g.last)
                sp.wait_ge(s["xA_scaled"], g.last)
                sp.wait_ge(s["xhA_ready"], g.last)
                sp.dma_start(xA[:], x_v[g.g]).then_inc(s["xA_in"], 16)

            def store(g):
                sp.wait_ge(s["xout_ready"], g.now)
                sp.dma_start(out_v[g.g], xout[:]).then_inc(s["xout_stored"], 16)

            def turn(t):
                t.run(load_xA, 0)
                t.run(store, 4)

            turns(sp, turn)
            sp.wait_ge(s["xout_stored"], 16 * GRAPHS)

        @block.gpsimd
        def _(pool):
            def rstd(k, var=None):
                def step(g):
                    L = ln[k]
                    pool.wait_ge(s["stats_" + k], g.now)
                    pool.tensor_tensor(L["ve"][:], var if var is not None else L["mv"][:, :, 1],
                                       consts[:, 2:3].to_broadcast([P, NT]), ALU.add).then_inc(s["ve_" + k], 1)
                    pool.wait_ge(s["ve_" + k], g.now)
                    pool.wait_ge(s["nb_" + k], g.last)
                    if k != "B":
                        pool.wait_ge(s["applied_" + k], g.last)
                    pool.tensor_tensor(L["r"][:], L["ve"][:], consts[:, 0:1].to_broadcast([P, NT]),
                                       ALU.pow).then_inc(s["rstd_" + k], 1)
                return step

            rstd_A, rstd_Z, rstd_C, rstd_D, rstd_E = (rstd(k) for k in "AZCDE")
            rstd_B = rstd("B", var=tvB[:])

            def hb_C(g):
                pool.wait_ge(s["applied_B"], g.now)
                pool.wait_ge(s["qC_ready"], g.last)
                pool.tensor_tensor(hbC[:], hgat[:], b2_row[:].to_broadcast([P, NT, P]),
                                   ALU.add).then_inc(s["hbC_ready"], 1)

            def half_xA(g):
                pool.wait_ge(s["xTA_ready"], g.now)
                pool.wait_ge(s["y_A"], g.last)
                pool.tensor_tensor(xhA[:], xA[:], consts[:, 1:2].unsqueeze(2).to_broadcast([P, NT, P]),
                                   ALU.add).then_inc(s["xhA_ready"], 1)

            def bias_D(g):
                pool.wait_ge(s["applied_C"], g.now)
                pool.wait_ge(s["y_D"], g.last)
                pool.tensor_tensor(xbD[:], xD[:], l2b_row[:].to_broadcast([P, NT, P]),
                                   ALU.add).then_inc(s["xbD_ready"], 1)

            def diag_D(g):
                pool.wait_ge(s["xTD_ready"], g.now)
                pool.wait_ge(s["aggD_ready"], g.last)
                pool.tensor_tensor(xTdD[:], xTD[:], diag2[:], ALU.mult).then_inc(s["xTdD_ready"], 1)

            def minus1_E(g):
                pool.wait_ge(s["applied_D"], g.now)
                pool.wait_ge(s["y_E"], g.last)
                pool.tensor_tensor(xmE[:], xE[:], consts[:, 3:4].unsqueeze(2).to_broadcast([P, NT, P]),
                                   ALU.add).then_inc(s["xmE_ready"], 1)

            def y_E(g):
                pool.wait_ge(s["y1E"], g.now)
                pool.wait_ge(s["xmE_ready"], g.now)
                pool.wait_ge(s["applied_E"], g.last)
                pool.tensor_tensor(ln["E"]["y"][:], y1E[:], xmE[:], ALU.add).then_inc(s["y_E"], 1)

            def power_A(g):
                pool.wait_ge(s["veA_ready"], g.now)
                pool.wait_ge(s["expA"], NT * g.last)
                pool.wait_ge(s["nmA_ready"], g.last)
                pool.tensor_tensor(irA[:], veA[:], consts[:, 1:2], ALU.pow).then_inc(s["irA_ready"], 1)
                pool.tensor_tensor(rA[:], veA[:], consts[:, 0:1], ALU.pow).then_inc(s["rA_ready"], 1)

            def mult_B(j):
                def step(g):
                    pool.wait_ge(s["expB"], g.tile(j))
                    pool.wait_ge(s["aggB_ready"], g.last)
                    pool.tensor_tensor(paB[:, j], att[B]["p"][:, j], adj_j[:, j], ALU.mult).then_inc(s["paB"], 1)
                return step

            def add_B(j):
                def step(g):
                    p = att[B]["p"]
                    before = p[:, 0] if j == 1 else psumB[:, j - 2]
                    pool.wait_ge(s["expB"], g.tile(j))
                    if j > 1:
                        pool.wait_ge(s["psB"], g.tile(j - 2, NT - 1))
                    pool.wait_ge(s["zsumB_ready"], g.last)
                    pool.tensor_tensor(psumB[:, j - 1], before, p[:, j], ALU.add).then_inc(s["psB"], 1)
                return step

            mult_B0, mult_B1, mult_B2, mult_B3 = (mult_B(j) for j in range(NT))
            add_B1, add_B2, add_B3 = (add_B(j) for j in range(1, NT))

            def gain_B(g):
                pool.wait_ge(s["applied0_B"], g.now)
                pool.wait_ge(s["applied_B"], g.last)
                pool.tensor_tensor(ngB[:], nB[:], gg_row[:].to_broadcast([P, NT, P]),
                                   ALU.mult).then_inc(s["ngB_ready"], 1)
                pool.wait_ge(s["ngB_ready"], g.now)
                pool.tensor_tensor(nB[:], ngB[:], gb_row[:].to_broadcast([P, NT, P]),
                                   ALU.add).then_inc(s["nbB_ready"], 1)

            def turn(t):
                t.run(rstd_Z, 3)
                t.run(add_B1, 2)
                t.run(mult_B1, 2)
                t.run(add_B2, 2)
                t.run(rstd_A, 1)
                t.run(mult_B2, 2)
                t.run(add_B3, 2)
                t.run(rstd_C, 3)
                t.run(mult_B3, 2)
                t.run(power_A, 0)
                t.run(bias_D, 3)
                t.run(diag_D, 3)
                t.run(y_E, 4)
                t.run(rstd_E, 4)
                t.run(rstd_D, 3)
                t.run(rstd_B, 2)
                t.run(gain_B, 2)
                t.run(mult_B0, 1)
                t.run(minus1_E, 3)
                t.run(hb_C, 2)
                t.run(half_xA, 0)

            turns(pool, turn)

        @block.tensor
        def _(pe):
            IN_T = [
                ("zT_ready", 3, 0, 1), ("xTA_ready", 0, 0, 1), ("xTB_ready", 1, 0, 1), ("xTD_ready", 3, 0, 1),
                ("rowsA_ready", 0, 0, 1), ("crowB", 1, 0, 1), ("sB_ready", 1, 0, 1), ("xTE_ready", 3, 0, 1),
                ("sE_ready", 3, 0, 1), ("crowE", 3, 0, 1),
            ]
            IN_F = [
                ("hE_ready", 4, 0, 1), ("qC_ready", 3, 0, 1), ("h1D_ready", 3, 0, 1), ("hB_ready", 1, 0, 1),
                ("ginT_ready", 2, 0, 1), ("y_Z", 2, 0, 1),
            ]
            IN_M = [
                ("stA_ready", 0, 0, 1), ("meanA", 0, 0, 1), ("varA", 0, 0, 1), ("stB_taken", 1, 0, 1),
                ("rzB_ready", 2, 0, 1), ("stE_taken", 3, 0, 1),
            ]
            IN_R = [
                ("maxB_ready", 1, 0, 1), ("maxE_ready", 3, 0, 1),
            ]
            IN_S0 = [
                ("wE", 4, 0, 4), ("wE", 4, 2, 4), ("vA", 0, 0, 4), ("vA", 0, 2, 4), ("wB", 1, 0, 4),
                ("wB", 1, 2, 4),
            ]
            IN_S1 = [
                ("wE", 4, 1, 4), ("wE", 4, 3, 4), ("vA", 0, 1, 4), ("vA", 0, 3, 4), ("wB", 1, 1, 4),
                ("wB", 1, 3, 4),
            ]
            IN_G0 = [
                ("euE_ready", 4, 0, 1), ("y_D", 3, 0, 1), ("thA_ready", 0, 0, 1),
            ]
            IN_G1 = [
                ("euE_ready", 4, 0, 1), ("applied0_B", 2, 0, 1),
            ]

            def bank_free(g, readers, mine, tile=0):
                at = next(i for i, r in enumerate(readers) if r[0] == mine and r[2] == tile)
                for back in range(1, len(readers) + 1):
                    name, delay, k, per = readers[at - back]
                    reader = g.turn.graph(delay + (back > at))
                    if reader.real:
                        pe.wait_ge(s[name], reader.tile(k, per))
                        return

            def transpose(src):
                for i in range(NT):
                    last = nc.tensor.transpose(psT[:, 0, i * P:(i + 1) * P], src[:, i], ident[:])
                return last

            def features(src, w):
                for i in range(NT):
                    last = mm(psF[:, 0, i * P:(i + 1) * P], src[:, i * P:(i + 1) * P], w, start=True, stop=True)
                return last

            def columns(dst, src, w):
                for i in range(NT):
                    last = mm(dst[:, 2 * i:2 * i + 2], src[:, i * P:(i + 1) * P], w, start=True, stop=True)
                return last

            def transpose_xA(g):
                pe.wait_ge(s["xA_in"], 16 * g.now)
                bank_free(g, IN_T, "xTA_ready")
                transpose(xA).then_inc(s["xA_transposed"], 1)

            def columns_A(g):
                pe.wait_ge(s["xTA_ready"], g.now)
                bank_free(g, IN_M, "stA_ready")
                columns(mA0, xTA, a01[:]).then_inc(s["stA_in_psum"], 1)

            def sum_A(g):
                pe.wait_ge(s["stA_ready"], g.now)
                bank_free(g, IN_M, "meanA")
                mm(mA1, ones[:], stA[:].rearrange("p t c -> p (t c)"), start=True, stop=True).then_inc(
                    s["sumA_in_psum"], 1)

            def squares_A(g):
                pe.wait_ge(s["sqA_ready"], g.now)
                bank_free(g, IN_M, "varA")
                mm(mA2, ones[:], sqA[:].rearrange("p t c -> p (t c)"), start=True, stop=True).then_inc(
                    s["sqA_in_psum"], 1)

            def rows_A(g):
                pe.wait_ge(s["spA"], g.now)
                bank_free(g, IN_T, "rowsA_ready")
                for i in range(2 * NT):
                    last = nc.tensor.transpose(psTb[:, i * P:(i + 1) * P], spA[:, i // NT, i % NT], identb[:])
                last.then_inc(s["rows_in_psum_A"], 1)

            def pair_A(j):
                def step(g):
                    pe.wait_ge(s["rowsA_ready"], g.now)
                    bank_free(g, (IN_S0, IN_S1)[j % 2], "vA", j)
                    mm(psS[:, j % 2], rowsA[:, N + j * P:N + (j + 1) * P], rowsA[:, 0:N], start=True,
                       stop=True).then_inc(s[f"eA{j}"], 1)
                return step

            pair_A0, pair_A1, pair_A2, pair_A3 = (pair_A(j) for j in range(NT))

            def agg_A(half):
                def step(g):
                    if half == 0:
                        pe.wait_ge(s["xA_scaled"], g.now)
                        bank_free(g, IN_G0, "thA_ready")
                    for i in range(half * NT // 2, (half + 1) * NT // 2):
                        for j in range(NT):
                            last = mm(psG[:, 0, i * P:(i + 1) * P], pA[:, j, i * P:(i + 1) * P], xsA[:, j],
                                      start=(j == 0), stop=(j == NT - 1))
                    if half == 1:
                        last.then_inc(s["aggA_ready"], 1)
                return step

            agg_A0, agg_A1 = agg_A(0), agg_A(1)

            def transpose_xB(g):
                pe.wait_ge(s["applied_A"], g.now)
                bank_free(g, IN_T, "xTB_ready")
                transpose(xB).then_inc(s["xB_transposed"], 1)

            def transpose_xE(g):
                pe.wait_ge(s["applied_D"], g.now)
                bank_free(g, IN_T, "xTE_ready")
                transpose(xE).then_inc(s["xE_transposed"], 1)

            def project(n, xT, ws, wt, st, w, mcols):
                def s_row(g):
                    pe.wait_ge(s[f"xT{n}_ready"], g.now)
                    bank_free(g, IN_T, f"s{n}_ready")
                    mm(psT[:, 0], ws[:], xT[:], start=True, stop=True).then_inc(s[f"s{n}_in_psum"], 1)

                def cols(g):
                    pe.wait_ge(s[f"xT{n}_ready"], g.now)
                    bank_free(g, IN_M, f"st{n}_taken")
                    columns(mcols, xT, st[:]).then_inc(s[f"st{n}_in_psum"], 1)

                def t_row(g):
                    pe.wait_ge(s[f"xT{n}_ready"], g.now)
                    bank_free(g, IN_R, f"max{n}_ready")
                    mm(psR[:, 0], wt[:], xT[:], start=True, stop=True).then_inc(s[f"t{n}_in_psum"], 1)

                def feats(g):
                    pe.wait_ge(s[f"xT{n}_ready"], g.now)
                    bank_free(g, IN_F, f"h{n}_ready")
                    features(xT, w[:]).then_inc(s[f"h{n}_in_psum"], 1)

                def c_row(g):
                    pe.wait_ge(s["sp" + n], g.now)
                    bank_free(g, IN_T, "crow" + n)
                    for i in range(NT):
                        last = nc.tensor.transpose(psTb[:, i * P:(i + 1) * P], att[B if n == "B" else E]["sp"][:, i],
                                                   identb[:])
                    last.then_inc(s["rows_in_psum_" + n], 1)
                return s_row, cols, t_row, feats, c_row

            s_B, columns_B, t_B, h_B, rows_B = project("B", xTB, ws1, wt1, st1, wp_sb, mB)
            s_E, columns_E, t_E, h_E, rows_E = project("E", xTE, ws3, wt3, st3, w3_sb, mE)

            def scores(n, b, no_edge, j):
                def step(g):
                    pe.wait_ge(s["crow" + n], g.now)
                    bank_free(g, (IN_S0, IN_S1)[j % 2], "w" + n, j)
                    mm(psS[:, j % 2], identb[:], no_edge[:, j], start=True, stop=False)
                    mm(psS[:, j % 2], onesb[:], b["crow"][:], start=False, stop=True).then_inc(s["cmask" + n], 1)
                return step

            scores_B0, scores_B1, scores_B2, scores_B3 = (scores("B", att[B], no1_j, j) for j in range(NT))
            scores_E0, scores_E1, scores_E2, scores_E3 = (scores("E", att[E], no3_j, j) for j in range(NT))

            def agg_B(j):
                def step(g):
                    if j == 0:
                        pe.wait_ge(s["hB_ready"], g.now)
                        bank_free(g, IN_G1, "applied0_B")
                    pe.wait_ge(s["paB"], g.tile(j))
                    for i in range(NT):
                        last = mm(psG[:, 1, i * P:(i + 1) * P], paB[:, j, i * P:(i + 1) * P],
                                  att[B]["h"][:, j, 0:P], start=(j == 0 and i == 0), stop=(j == NT - 1),
                                  skip_group_check=True)
                    if j == NT - 1:
                        last.then_inc(s["aggB_ready"], 1)
                return step

            agg_B0, agg_B1, agg_B2, agg_B3 = (agg_B(j) for j in range(NT))

            def zsum_B(g):
                pe.wait_ge(s["psB"], (NT - 1) * g.now)
                bank_free(g, IN_M, "rzB_ready")
                for i in range(NT):
                    last = mm(mZ[:, i:i + 1], psumB[:, 2, i * P:(i + 1) * P], ones[:, 0:1], start=True, stop=True)
                last.then_inc(s["zsumB_ready"], 1)

            def agg_E(j):
                def step(g):
                    if j == 0:
                        pe.wait_ge(s["hE_ready"], g.now)
                        bank_free(g, IN_G0, "euE_ready")
                        bank_free(g, IN_G1, "euE_ready")
                    pe.wait_ge(s["expE"], g.tile(j))
                    for i in range(NT):
                        k = (i % 2) * (P + 2)
                        last = mm(psG[:, i // 2, k:k + P + 2], att[E]["p"][:, j, i * P:(i + 1) * P],
                                  att[E]["h"][:, j], start=(j == 0 and i % 2 == 0), stop=(j == NT - 1),
                                  skip_group_check=True)
                    if j == NT - 1:
                        last.then_inc(s["aggE_ready"], 1)
                return step

            agg_E0, agg_E1, agg_E2, agg_E3 = (agg_E(j) for j in range(NT))

            def gin(half):
                def step(g):
                    if half == 0:
                        pe.wait_ge(s["applied_B"], g.now)
                        bank_free(g, IN_F, "ginT_ready")
                    for j in range(half * NT // 2, (half + 1) * NT // 2):
                        last = mm(psF[:, 0], hgat[:, j], gin_j[:, j], start=(j == 0), stop=(j == NT - 1))
                    if half == 1:
                        last.then_inc(s["ginT_in_psum"], 1)
                return step

            gin0, gin1 = gin(0), gin(1)

            def z_C(g):
                pe.wait_ge(s["ginT_ready"], g.now)
                bank_free(g, IN_F, "y_Z")
                features(ginT, w1_sb[:]).then_inc(s["z_in_psum"], 1)

            def zT_C(g):
                pe.wait_ge(s["applied_Z"], g.now)
                bank_free(g, IN_T, "zT_ready")
                transpose(znC).then_inc(s["zT_in_psum"], 1)

            def x2_C(g):
                pe.wait_ge(s["zT_ready"], g.now)
                bank_free(g, IN_F, "qC_ready")
                features(zT, w2_sb[:]).then_inc(s["x2C_in_psum"], 1)

            def transpose_xD(g):
                pe.wait_ge(s["applied_C"], g.now)
                bank_free(g, IN_T, "xTD_ready")
                transpose(xD).then_inc(s["xD_transposed"], 1)

            def h_D(g):
                pe.wait_ge(s["xTD_ready"], g.now)
                bank_free(g, IN_F, "h1D_ready")
                features(xTD, l2w1[:]).then_inc(s["h1D_in_psum"], 1)

            def agg_D(half):
                def step(g):
                    if half == 0:
                        pe.wait_ge(s["h1D_ready"], g.now)
                        pe.wait_ge(s["xTdD_ready"], g.now)
                        bank_free(g, IN_G0, "y_D")
                    for i in range(half * NT // 2, (half + 1) * NT // 2):
                        dst = psG[:, 0, i * P:(i + 1) * P]
                        for j in range(NT):
                            mm(dst, att2_j[:, j, i * P:(i + 1) * P], h1D[:, j], start=(j == 0), stop=False)
                        last = mm(dst, xTdD[:, i * P:(i + 1) * P], l2w0[:], start=False, stop=True)
                    if half == 1:
                        last.then_inc(s["aggD_ready"], 1)
                return step

            agg_D0, agg_D1 = agg_D(0), agg_D(1)

            def turn(t):
                t.run(scores_E0, 4)
                t.run(scores_E1, 4)
                t.run(h_E, 4)
                t.run(scores_E2, 4)
                t.run(zT_C, 3)
                t.run(scores_E3, 4)
                t.run(x2_C, 3)
                t.run(transpose_xA, 0)
                t.run(agg_E0, 4)
                t.run(agg_E1, 4)
                t.run(columns_A, 0)
                t.run(agg_E2, 4)
                t.run(transpose_xB, 1)
                t.run(sum_A, 0)
                t.run(agg_E3, 4)
                t.run(squares_A, 0)
                t.run(columns_B, 1)
                t.run(transpose_xD, 3)
                t.run(t_B, 1)
                t.run(h_D, 3)
                t.run(rows_A, 0)
                t.run(agg_B0, 2)
                t.run(agg_D0, 3)
                t.run(agg_D1, 3)
                t.run(agg_B1, 2)
                t.run(agg_B2, 2)
                t.run(agg_B3, 2)
                t.run(rows_B, 1)
                t.run(zsum_B, 2)
                t.run(s_B, 1)
                t.run(pair_A0, 0)
                t.run(pair_A1, 0)
                t.run(h_B, 1)
                t.run(pair_A2, 0)
                t.run(pair_A3, 0)
                t.run(scores_B0, 1)
                t.run(transpose_xE, 3)
                t.run(scores_B1, 1)
                t.run(columns_E, 3)
                t.run(t_E, 3)
                t.run(s_E, 3)
                t.run(gin0, 2)
                t.run(gin1, 2)
                t.run(scores_B2, 1)
                t.run(scores_B3, 1)
                t.run(z_C, 2)
                t.run(rows_E, 3)
                t.run(agg_A0, 0)
                t.run(agg_A1, 0)

            turns(pe, turn)

        @block.vector
        def _(dve):
            def stats_of(k):
                def step(g):
                    L = ln[k]
                    dve.wait_ge(s["y_" + k], g.now)
                    dve.wait_ge(s["ve_" + k], g.last)
                    for i in range(NT):
                        last = v.bn_stats(L["st"][:, i], L["y"][:, i])
                    last.then_inc(s["bn_" + k], 1)
                    dve.wait_ge(s["bn_" + k], 1)
                    dve.wait_ge(s["bn_" + k], g.now)
                    for i in range(NT):
                        last = v.bn_aggr(L["mv"][:, i], L["st"][:, i])
                    last.then_inc(s["stats_" + k], 1)
                return step

            bn_A, bn_Z, bn_C, bn_D, bn_E = (stats_of(k) for k in "AZCDE")

            def neg_mean(g, k, rstd):
                L = ln[k]
                dve.wait_ge(s["applied0_B" if k == "B" else "applied_" + k], g.last)
                v.scalar_tensor_tensor(L["nb"][:], L["mv"][:, :, 0], -1.0, rstd, ALU.mult,
                                       ALU.mult).then_inc(s["nb_" + k], 1)

            def neg_mean_of(k):
                def step(g):
                    dve.wait_ge(s["rstd_" + k], g.now)
                    neg_mean(g, k, ln[k]["r"][:])
                return step

            nb_A, nb_Z, nb_C, nb_D, nb_E = (neg_mean_of(k) for k in "AZCDE")

            def row_max(n, b, no_edge, src):
                small = s["small_" + n]

                def cols(g):
                    dve.wait_ge(s[f"st{n}_in_psum"], g.now)
                    dve.wait_ge(s["exp" + n], NT * g.last)
                    if n == "B":
                        v.tensor_tensor(b["st"][:], src, bst[:].to_broadcast([P, NT, 2]), ALU.add).then_inc(
                            s["stB_taken"], 1)
                    else:
                        v.tensor_copy(b["st"][:], src).then_inc(s["stE_taken"], 1)

                def maxima(g):
                    dve.wait_ge(s[f"st{n}_taken"], g.now)
                    dve.wait_ge(s[f"t{n}_in_psum"], g.now)
                    if n == "B":
                        dve.wait_ge(s["paB"], NT * g.last)
                        dve.wait_ge(s["psB"], (NT - 1) * g.last)
                    else:
                        dve.wait_ge(s["aggE_ready"], g.last)
                    v.tensor_scalar(b["nt"][:], b["st"][:, :, 1], -1.0, None, ALU.mult).then_inc(small, 1)
                    v.tensor_scalar(b["q"][:], b["st"][:, :, 0], 0.25, None, ALU.mult).then_inc(small, 1)
                    for i in range(NT):
                        last = v.tensor_tensor_reduce(out=b["w"][:, i], in0=psR[:, 0], in1=no_edge[:, i], scale=1.0,
                                                      scalar=-3e38, op0=ALU.add, op1=ALU.max,
                                                      accum_out=b["mx"][:, i:i + 1])
                    last.then_inc(s[f"max{n}_ready"], 1)

                def split(g):
                    dve.wait_ge(s[f"max{n}_ready"], g.now)
                    if n == "B":
                        v.scalar_tensor_tensor(b["u"][:], b["mx"][:], bst[:, 0, 1:2], b["st"][:, :, 0], ALU.add,
                                               ALU.add).then_inc(small, 1)
                    else:
                        v.tensor_tensor(b["u"][:], b["mx"][:], b["st"][:, :, 0], ALU.add).then_inc(small, 1)
                    dve.wait_ge(small, g.tile(2, SMALL))
                    v.scalar_tensor_tensor(b["m"][:], b["u"][:], SLOPE, b["u"][:], ALU.mult, ALU.max).then_inc(small, 1)
                    dve.wait_ge(small, g.tile(3, SMALL))
                    v.scalar_tensor_tensor(b["c"][:, :, 0], b["m"][:], -1.25, b["q"][:], ALU.mult,
                                           ALU.add).then_inc(small, 1)
                    dve.wait_ge(s["rows_in_psum_" + n], g.last)
                    parts = [b["sp"][:, :, k:k + 1] for k in range(2)]
                    dve.wait_ge(small, g.tile(4, SMALL))
                    v.tensor_copy(parts[0], b["c"][:]).then_inc(small, 1)
                    dve.wait_ge(small, g.tile(5, SMALL))
                    v.tensor_tensor(b["r1"][:], b["c"][:], parts[0], ALU.subtract).then_inc(small, 1)
                    dve.wait_ge(small, g.tile(6, SMALL))
                    v.tensor_copy(parts[1], b["r1"][:]).then_inc(s["sp" + n], 1)
                return cols, maxima, split

            cols_B, max_B, split_B = row_max("B", att[B], no1_i, pair(mB))
            cols_E, max_E, split_E = row_max("E", att[E], no3_i, pair(mE))

            def w(n, b, j):
                def step(g):
                    if j == 0:
                        dve.wait_ge(s[f"s{n}_ready"], g.now)
                    dve.wait_ge(s["cmask" + n], g.tile(j))
                    v.scalar_tensor_tensor(b["w"][:, j], b["srow"][:], b["nt"][:, j:j + 1], psS[:, j % 2],
                                           ALU.max, ALU.add).then_inc(s["w" + n], 1)
                return step

            w_B0, w_B1, w_B2, w_B3 = (w("B", att[B], j) for j in range(NT))
            w_E0, w_E1, w_E2, w_E3 = (w("E", att[E], j) for j in range(NT))

            def centre_A0(g):
                dve.wait_ge(s["stA_in_psum"], g.now)
                dve.wait_ge(s["cenA_ready"], g.last)
                v.tensor_copy(stA[:], pair(mA0)).then_inc(s["stA_ready"], 1)

            def centre_A1(g):
                dve.wait_ge(s["sumA_in_psum"], g.now)
                v.tensor_reduce(meanA[:, 0, :], pair(mA1).rearrange("p t c -> p c t"), axis=AX_X,
                                op=ALU.add).then_inc(s["meanA"], 1)
                dve.wait_ge(s["meanA"], g.now)
                dve.wait_ge(s["spA"], g.last)
                v.scalar_tensor_tensor(cenA[:], meanA[:].to_broadcast([P, NT, 2]), -1.0 / N, stA[:], ALU.mult,
                                       ALU.add).then_inc(s["cenA_ready"], 1)
                dve.wait_ge(s["cenA_ready"], g.now)
                v.tensor_tensor(sqA[:], cenA[:], cenA[:], ALU.mult).then_inc(s["sqA_ready"], 1)

            def variance_A(g):
                dve.wait_ge(s["sqA_in_psum"], g.now)
                v.tensor_reduce(varA[:, 0:1], mA2, axis=AX_X, op=ALU.add).then_inc(s["varA"], 1)
                dve.wait_ge(s["varA"], g.now)
                dve.wait_ge(s["rA_ready"], g.last)
                v.tensor_scalar(veA[:], varA[:, 0:1], 1.0 / N, PAIR_EPS, ALU.mult, ALU.add).then_inc(
                    s["veA_ready"], 1)

            def split_A(g):
                dve.wait_ge(s["irA_ready"], g.now)
                v.tensor_scalar(cenA[:, :, 1], cenA[:, :, 1], irA[:], None, ALU.add).then_inc(s["tirA"], 1)
                dve.wait_ge(s["tirA"], g.now)
                dve.wait_ge(s["rows_in_psum_A"], g.last)
                split_to = lambda k: [spA[:, 0, :, k:k + 1], spA[:, 1, :, 3 + k:4 + k]]
                for k, (val, rest) in enumerate(((cenA, r1A), (r1A, r2A), (r2A, None))):
                    for h in range(2):
                        last = v.tensor_copy(split_to(k)[h], val[:, :, h:h + 1])
                    last.then_inc(s[("hiA", "midA", "spA")[k]], 1)
                    if rest is not None:
                        dve.wait_ge(s[("hiA", "midA")[k]], g.now)
                        for h in range(2):
                            last = v.tensor_tensor(rest[:, :, h:h + 1], val[:, :, h:h + 1], split_to(k)[h],
                                                   ALU.subtract)
                        last.then_inc(s[("rest1A", "rest2A")[k]], 1)
                        dve.wait_ge(s[("rest1A", "rest2A")[k]], g.now)

            def v_A(j):
                def step(g):
                    dve.wait_ge(s[f"eA{j}"], 1)
                    dve.wait_ge(s[f"eA{j}"], g.now)
                    v.tensor_tensor_reduce(out=vA[:, j], in0=psS[:, j % 2], in1=adj_j[:, j], scale=1.0,
                                           scalar=-3e38, op0=ALU.mult, op1=ALU.max,
                                           accum_out=vmaxA[:, j:j + 1]).then_inc(s["vA"], 1)
                return step

            v_A0, v_A1, v_A2, v_A3 = (v_A(j) for j in range(NT))

            def max_A(g):
                dve.wait_ge(s["vA"], NT * g.now)
                v.scalar_tensor_tensor(lmA[:], vmaxA[:], SLOPE, vmaxA[:], ALU.mult, ALU.max).then_inc(s["lmA"], 1)
                dve.wait_ge(s["lmA"], g.now)
                dve.wait_ge(s["rA_ready"], g.now)
                dve.wait_ge(s["expA"], NT * g.last)
                v.tensor_scalar(nmA[:], lmA[:], rA[:], -1.0, ALU.mult, ALU.mult).then_inc(s["nmA_ready"], 1)

            def lrelu_A(j):
                def step(g):
                    if j == 0:
                        dve.wait_ge(s["aggA_ready"], g.last)
                        dve.wait_ge(s["vA"], NT * g.now)
                    v.scalar_tensor_tensor(pA[:, j], vA[:, j], SLOPE, vA[:, j], ALU.mult, ALU.max).then_inc(
                        s["lA"], 1)
                return step

            lrelu_A0, lrelu_A1, lrelu_A2, lrelu_A3 = (lrelu_A(j) for j in range(NT))

            def recip_A(g):
                dve.wait_ge(s["expA"], NT * g.now)
                dve.wait_ge(s["xA_scaled"], g.last)
                v.reciprocal(rzA[:], zsA[:]).then_inc(s["rzA"], 1)

            def y_A(g):
                dve.wait_ge(s["thA_ready"], g.now)
                dve.wait_ge(s["xhA_ready"], g.now)
                dve.wait_ge(s["applied_A"], g.last)
                v.scalar_tensor_tensor(ln["A"]["y"][:], thA[:], 0.5, xhA[:], ALU.mult, ALU.add).then_inc(s["y_A"], 1)

            def copy_hB(g):
                dve.wait_ge(s["hB_in_psum"], g.now)
                dve.wait_ge(s["aggB_ready"], g.last)
                v.tensor_tensor(att[B]["h"][:, :, 0:P], tiles(psF[:, 0]), bp_row[:].to_broadcast([P, NT, P]),
                                ALU.add).then_inc(s["hB_ready"], 1)

            def bn_B(g):
                dve.wait_ge(s["aggB_ready"], g.now)
                for i in range(NT):
                    last = v.bn_stats(ln["B"]["st"][:, i], psG[:, 1, i * P:(i + 1) * P])
                last.then_inc(s["bn_B"], 1)

            def stats_B(g):
                dve.wait_ge(s["zsumB_ready"], g.now)
                dve.wait_ge(s["scB_ready"], g.last)
                v.reciprocal(att[B]["rz"][:], mZ[:, 0:NT]).then_inc(s["rzB_ready"], 1)
                dve.wait_ge(s["rzB_ready"], 1)
                dve.wait_ge(s["bn_B"], g.now)
                dve.wait_ge(s["nb_B"], g.last)
                for i in range(NT):
                    last = v.bn_aggr(ln["B"]["mv"][:, i], ln["B"]["st"][:, i])
                last.then_inc(s["aggr_B"], 1)
                dve.wait_ge(s["rzB_ready"], g.now)
                v.tensor_tensor(rrB[:], att[B]["rz"][:], att[B]["rz"][:], ALU.mult).then_inc(s["rrB"], 1)
                dve.wait_ge(s["aggr_B"], g.now)
                dve.wait_ge(s["rrB"], g.now)
                dve.wait_ge(s["ve_B"], g.last)
                v.tensor_tensor(tvB[:], ln["B"]["mv"][:, :, 1], rrB[:], ALU.mult).then_inc(s["stats_B"], 1)

            def nb_B(g):
                dve.wait_ge(s["rstd_B"], g.now)
                dve.wait_ge(s["applied0_B"], g.last)
                v.tensor_tensor(scB[:], ln["B"]["r"][:], att[B]["rz"][:], ALU.mult).then_inc(s["scB_ready"], 1)
                dve.wait_ge(s["scB_ready"], g.now)
                neg_mean(g, "B", scB[:])

            def y_Z(g):
                dve.wait_ge(s["z_in_psum"], g.now)
                dve.wait_ge(s["applied_Z"], g.last)
                v.tensor_tensor(zC[:], tiles(psF[:, 0]), b1_row[:].to_broadcast([P, NT, P]), ALU.add).then_inc(
                    s["y_Z"], 1)

            def y_C(g):
                dve.wait_ge(s["x2C_in_psum"], g.now)
                dve.wait_ge(s["hbC_ready"], g.now)
                v.tensor_tensor(qC[:], tiles(psF[:, 0]), hbC[:], ALU.add).then_inc(s["qC_ready"], 1)
                dve.wait_ge(s["qC_ready"], g.now)
                dve.wait_ge(s["xBC_ready"], g.now)
                dve.wait_ge(s["applied_C"], g.last)
                v.scalar_tensor_tensor(ln["C"]["y"][:], qC[:], 0.0, xBC[:], ALU.max, ALU.add).then_inc(s["y_C"], 1)

            def y_D(g):
                dve.wait_ge(s["aggD_ready"], g.now)
                dve.wait_ge(s["xbD_ready"], g.now)
                dve.wait_ge(s["applied_D"], g.last)
                v.tensor_tensor(ln["D"]["y"][:], tiles(psG[:, 0]), xbD[:], ALU.add).then_inc(s["y_D"], 1)

            def recip_E(g):
                dve.wait_ge(s["aggE_ready"], g.now)
                dve.wait_ge(s["euE_ready"], g.last)
                for i in range(NT):
                    k = (i % 2) * (P + 2) + P
                    last = v.reciprocal(att[E]["rz"][:, i:i + 1], psG[:, i // 2, k:k + 1])
                last.then_inc(s["rzE_ready"], 1)

            def y1_E(g):
                dve.wait_ge(s["ruE_ready"], g.now)
                dve.wait_ge(s["euE_ready"], g.now)
                dve.wait_ge(s["y_E"], g.last)
                v.scalar_tensor_tensor(y1E[:], euE[:], 1.0, ruE[:], ALU.min, ALU.add).then_inc(s["y1E"], 1)

            def turn(t):
                t.run(nb_Z, 3)
                t.run(w_E0, 4)
                t.run(y_A, 1)
                t.run(w_E1, 4)
                t.run(bn_A, 1)
                t.run(w_E2, 4)
                t.run(y_C, 3)
                t.run(nb_A, 1)
                t.run(bn_C, 3)
                t.run(w_E3, 4)
                t.run(centre_A0, 0)
                t.run(nb_C, 3)
                t.run(centre_A1, 0)
                t.run(variance_A, 0)
                t.run(recip_E, 4)
                t.run(split_A, 0)
                t.run(cols_B, 1)
                t.run(y1_E, 4)
                t.run(max_B, 1)
                t.run(bn_E, 4)
                t.run(split_B, 1)
                t.run(nb_E, 4)
                t.run(y_D, 3)
                t.run(bn_D, 3)
                t.run(bn_B, 2)
                t.run(stats_B, 2)
                t.run(nb_D, 3)
                t.run(v_A0, 0)
                t.run(v_A1, 0)
                t.run(nb_B, 2)
                t.run(v_A2, 0)
                t.run(v_A3, 0)
                t.run(w_B0, 1)
                t.run(max_A, 0)
                t.run(lrelu_A0, 0)
                t.run(w_B1, 1)
                t.run(copy_hB, 1)
                t.run(cols_E, 3)
                t.run(lrelu_A1, 0)
                t.run(lrelu_A2, 0)
                t.run(lrelu_A3, 0)
                t.run(max_E, 3)
                t.run(recip_A, 0)
                t.run(split_E, 3)
                t.run(w_B2, 1)
                t.run(y_Z, 2)
                t.run(bn_Z, 2)
                t.run(w_B3, 1)

            turns(dve, turn)

        @block.scalar
        def _(act):
            def normalise(g, k, src, dst, scale=None, name=None):
                L = ln[k]
                act.wait_ge(s["nb_" + k], g.now)
                act.wait_ge(s["rstd_" + k], g.now)
                for i in range(NT):
                    last = a.activation(dst[:, i], src(i), ACT.Identity, scale=(L["r"] if scale is None else scale)[:, i:i + 1],
                                        bias=L["nb"][:, i:i + 1])
                last.then_inc(s[name or "applied_" + k], 1)

            def exp(n, b, j):
                def step(g):
                    act.wait_ge(s["w" + n], g.tile(j))
                    a.activation(b["p"][:, j], b["w"][:, j], ACT.Exp, scale=1.0 - SLOPE,
                                 bias=b["st"][:, j, 1:2]).then_inc(s["exp" + n], 1)
                return step

            exp_B0, exp_B1, exp_B2, exp_B3 = (exp("B", att[B], j) for j in range(NT))
            exp_E0, exp_E1, exp_E2, exp_E3 = (exp("E", att[E], j) for j in range(NT))

            def copy_xTA(g):
                act.wait_ge(s["xA_transposed"], g.now)
                act.wait_ge(s["stA_in_psum"], g.last)
                a.copy(xTA[:], psT[:, 0]).then_inc(s["xTA_ready"], 1)

            def copy_rowsA(g):
                act.wait_ge(s["rows_in_psum_A"], g.now)
                act.wait_ge(s["eA3"], g.last)
                a.copy(rowsA[:], psTb).then_inc(s["rowsA_ready"], 1)

            def exp_A(j):
                def step(g):
                    act.wait_ge(s["lA"], g.tile(j))
                    act.wait_ge(s["nmA_ready"], g.now)
                    act.wait_ge(s["rzA"], g.last)
                    a.activation(pA[:, j], pA[:, j], ACT.Exp, scale=rA[:], bias=nmA[:, j:j + 1],
                                 accum_out=zsA[:, j:j + 1]).then_inc(s["expA"], 1)
                return step

            exp_A0, exp_A1, exp_A2, exp_A3 = (exp_A(j) for j in range(NT))

            def scale_xA(g):
                act.wait_ge(s["rzA"], g.now)
                act.wait_ge(s["aggA_ready"], g.last)
                for j in range(NT):
                    last = a.activation(xsA[:, j], xA[:, j], ACT.Copy, scale=rzA[:, j:j + 1])
                last.then_inc(s["xA_scaled"], 1)

            def tanh_A(g):
                act.wait_ge(s["aggA_ready"], g.now)
                act.wait_ge(s["y_A"], g.last)
                a.activation(thA[:], tiles(psG[:, 0]), ACT.Tanh, scale=0.5).then_inc(s["thA_ready"], 1)

            def norm_A(g):
                act.wait_ge(s["xB_transposed"], g.last)
                act.wait_ge(s["xBC_ready"], g.last)
                normalise(g, "A", lambda i: ln["A"]["y"][:, i], xB)

            def copy_xBC(g):
                act.wait_ge(s["applied_A"], g.now)
                act.wait_ge(s["y_C"], g.last)
                a.copy(xBC[:], xB[:]).then_inc(s["xBC_ready"], 1)

            def copy_xTB(g):
                act.wait_ge(s["xB_transposed"], g.now)
                for used in ("hB_in_psum", "sB_in_psum", "stB_in_psum", "tB_in_psum"):
                    act.wait_ge(s[used], g.last)
                a.copy(xTB[:], psT[:, 0]).then_inc(s["xTB_ready"], 1)

            def copy_sB(g):
                act.wait_ge(s["sB_in_psum"], g.now)
                act.wait_ge(s["wB"], NT * g.last)
                a.activation(att[B]["srow"][:], psT[:, 0], ACT.Identity, bias=bst[:, 0, 0:1]).then_inc(
                    s["sB_ready"], 1)

            def copy_cB(g):
                act.wait_ge(s["rows_in_psum_B"], g.now)
                act.wait_ge(s["cmaskB"], NT * g.last)
                a.copy(att[B]["crow"][:], psTb[:, 0:N]).then_inc(s["crowB"], 1)

            def norm_B(g):
                act.wait_ge(s["nbB_ready"], g.last)
                act.wait_ge(s["applied_B"], g.last)
                act.wait_ge(s["scB_ready"], g.now)
                normalise(g, "B", lambda i: psG[:, 1, i * P:(i + 1) * P], nB, scale=scB, name="applied0_B")

            def relu_B(g):
                act.wait_ge(s["nbB_ready"], g.now)
                act.wait_ge(s["hbC_ready"], g.last)
                act.wait_ge(s["ginT_in_psum"], g.last)
                a.activation(hgat[:], nB[:], ACT.Relu).then_inc(s["applied_B"], 1)

            def copy_ginT(g):
                act.wait_ge(s["ginT_in_psum"], g.now)
                act.wait_ge(s["z_in_psum"], g.last)
                a.copy(ginT[:], psF[:, 0]).then_inc(s["ginT_ready"], 1)

            def norm_Z(g):
                act.wait_ge(s["zT_in_psum"], g.last)
                normalise(g, "Z", lambda i: zC[:, i], znC)

            def copy_zT(g):
                act.wait_ge(s["zT_in_psum"], g.now)
                act.wait_ge(s["x2C_in_psum"], g.last)
                a.activation(zT[:], psT[:, 0], ACT.Relu, scale=mlp_gb[:, 0:1], bias=mlp_gb[:, 1:2]).then_inc(s["zT_ready"], 1)

            def norm_C(g):
                act.wait_ge(s["xbD_ready"], g.last)
                act.wait_ge(s["xD_transposed"], g.last)
                normalise(g, "C", lambda i: ln["C"]["y"][:, i], xD)

            def copy_xTD(g):
                act.wait_ge(s["xD_transposed"], g.now)
                act.wait_ge(s["h1D_in_psum"], g.last)
                act.wait_ge(s["xTdD_ready"], g.last)
                a.copy(xTD[:], psT[:, 0]).then_inc(s["xTD_ready"], 1)

            def copy_hD(g):
                act.wait_ge(s["h1D_in_psum"], g.now)
                act.wait_ge(s["aggD_ready"], g.last)
                a.copy(h1D[:].rearrange("p t d -> p (t d)"), psF[:, 0]).then_inc(s["h1D_ready"], 1)

            def norm_D(g):
                act.wait_ge(s["xmE_ready"], g.last)
                act.wait_ge(s["xE_transposed"], g.last)
                normalise(g, "D", lambda i: ln["D"]["y"][:, i], xE)

            def copy_xTE(g):
                act.wait_ge(s["xE_transposed"], g.now)
                for used in ("hE_in_psum", "sE_in_psum", "stE_in_psum", "tE_in_psum"):
                    act.wait_ge(s[used], g.last)
                a.copy(xTE[:], psT[:, 0]).then_inc(s["xTE_ready"], 1)

            def copy_sE(g):
                act.wait_ge(s["sE_in_psum"], g.now)
                act.wait_ge(s["wE"], NT * g.last)
                a.copy(att[E]["srow"][:], psT[:, 0]).then_inc(s["sE_ready"], 1)

            def copy_hE(g):
                act.wait_ge(s["hE_in_psum"], g.now)
                act.wait_ge(s["aggE_ready"], g.last)
                a.copy(att[E]["h"][:, :, 0:P], tiles(psF[:, 0])).then_inc(s["hE_ready"], 1)

            def copy_cE(g):
                act.wait_ge(s["rows_in_psum_E"], g.now)
                act.wait_ge(s["cmaskE"], NT * g.last)
                a.copy(att[E]["crow"][:], psTb[:, 0:N]).then_inc(s["crowE"], 1)

            def result_E(f, dst, name):
                def step(g):
                    act.wait_ge(s["rzE_ready"], g.now)
                    act.wait_ge(s["y1E"], g.last)
                    for i in range(NT):
                        k = (i % 2) * (P + 2)
                        last = a.activation(dst[:, i], psG[:, i // 2, k:k + P], f, scale=att[E]["rz"][:, i:i + 1])
                    last.then_inc(s[name], 1)
                return step

            relu_E = result_E(ACT.Relu, ruE, "ruE_ready")
            expm_E = result_E(ACT.Exp, euE, "euE_ready")

            def norm_E(g):
                act.wait_ge(s["xout_stored"], 16 * g.last)
                normalise(g, "E", lambda i: ln["E"]["y"][:, i], xout, name="xout_ready")
                act.sem_inc(s["applied_E"], 1)

            def turn(t):
                t.run(exp_B3, 2)
                t.run(tanh_A, 1)
                t.run(norm_Z, 3)
                t.run(copy_hE, 4)
                t.run(copy_zT, 3)
                t.run(exp_E0, 4)
                t.run(exp_E1, 4)
                t.run(copy_xTA, 0)
                t.run(exp_E2, 4)
                t.run(copy_xBC, 2)
                t.run(norm_A, 1)
                t.run(exp_E3, 4)
                t.run(copy_xTB, 1)
                t.run(norm_C, 3)
                t.run(relu_E, 4)
                t.run(copy_xTD, 3)
                t.run(expm_E, 4)
                t.run(copy_hD, 3)
                t.run(copy_rowsA, 0)
                t.run(norm_E, 4)
                t.run(copy_cB, 1)
                t.run(copy_sB, 1)
                t.run(norm_D, 3)
                t.run(norm_B, 2)
                t.run(copy_xTE, 3)
                t.run(exp_A0, 0)
                t.run(relu_B, 2)
                t.run(exp_A1, 0)
                t.run(exp_A2, 0)
                t.run(exp_A3, 0)
                t.run(exp_B0, 1)
                t.run(copy_sE, 3)
                t.run(copy_ginT, 2)
                t.run(scale_xA, 0)
                t.run(exp_B1, 1)
                t.run(exp_B2, 1)
                t.run(copy_cE, 3)

            turns(act, turn)


_INS = ["x", "adj", "L0_gnn_a", "L1_gnn_Wp", "L1_gnn_bp", "L1_gnn_a_src", "L1_gnn_a_dst", "L1_gnn_gat_g",
        "L1_gnn_gat_b", "L1_gnn_eps", "L1_gnn_W1", "L1_gnn_b1", "L1_gnn_mlp_g", "L1_gnn_mlp_b", "L1_gnn_W2",
        "L1_gnn_b2", "L2_gnn_W", "L2_gnn_e", "L2_gnn_bias", "L3_gnn_W", "L3_gnn_a_src", "L3_gnn_a_dst"]


def kernel(**inputs):
    import numpy as _np
    import concourse.bacc as _bacc
    from concourse import mybir as _mybir
    from concourse.bass_utils import run_bass_kernel_spmd as _run

    nc = _bacc.Bacc("TRN2", target_bir_lowering=False, num_devices=1)
    arrays, args = {}, []
    for name in _INS:
        a = _np.ascontiguousarray(inputs[name])
        arrays[f"in_{name}_dram"] = a
        args.append(nc.dram_tensor(f"in_{name}_dram", a.shape, _mybir.dt.from_np(a.dtype), kind="ExternalInput").ap())
    out = nc.dram_tensor("out_0_dram", inputs["x"].shape, _mybir.dt.float32, kind="ExternalOutput").ap()
    resnorm_gnn(nc, *args, out)
    r = _run(nc, [arrays], core_ids=[0])
    return r.results[0]["out_0_dram"]
```
